# Optimizing a Trainium2 kernel written in Bass

```python
import numpy as np
import jax
import jax.numpy as jnp

def _softmax(x, axis=-1):
    return jax.nn.softmax(x, axis=axis)

def _gelu(x):
    return jax.nn.gelu(x, approximate=True)

def _silu(x):
    return jax.nn.silu(x)

def _sigmoid(x):
    return jax.nn.sigmoid(x)

def _layernorm(x, axis=-1, eps=1e-05):
    m = jnp.mean(x, axis=axis, keepdims=True)
    v = jnp.var(x, axis=axis, keepdims=True)
    return (x - m) / jnp.sqrt(v + eps)

def _scatter_add(tgt, idx, src, axis=0):
    return tgt.at[idx].add(src)

def _segment_sum(src, seg, n):
    return jax.ops.segment_sum(src, seg, n)
kernel_name = 'mk_hybrid_d1_jaxref_r4_c8ff23'

def setup_inputs(seed: int=0):
    np.random.seed(seed)
    _w = jnp.asarray

    def _L0_attn_a_setup():
        import jax, jax.numpy as jnp
        import numpy as np
        from jax import lax
        BLOCKS = 16
        NUM_HEADS = 8
        KEY_DIM = 64
        WIDTH = 128
        D_MODEL = 512

        def _forward(x, conv_w, conv_b, wq, bq, wk, bk, wv, bv, wo, bo, proj_w, proj_b):
            N, T, D = x.shape
            xp = jnp.pad(x, ((0, 0), (2, 0), (0, 0)))
            qkv = lax.conv_general_dilated(xp, conv_w, window_strides=(1,), padding='VALID', dimension_numbers=('NWC', 'WIO', 'NWC')) + conv_b
            q, k, v = jnp.split(qkv, 3, axis=-1)
            block_len = T // BLOCKS
            qb = q.reshape(N * BLOCKS, block_len, WIDTH)
            kb = k.reshape(N * BLOCKS, block_len, WIDTH)
            vb = v.reshape(N * BLOCKS, block_len, WIDTH)
            qh = jnp.einsum('bsd,dhk->bshk', qb, wq) + bq
            kh = jnp.einsum('bsd,dhk->bshk', kb, wk) + bk
            vh = jnp.einsum('bsd,dhk->bshk', vb, wv) + bv
            scale = 1.0 / jnp.sqrt(jnp.asarray(KEY_DIM, qh.dtype))
            scores = jnp.einsum('bqhk,bshk->bhqs', qh * scale, kh)
            causal = jnp.tril(jnp.ones((block_len, block_len), bool))
            scores = jnp.where(causal[None, None], scores, jnp.asarray(-1000000000.0, scores.dtype))
            attn = jax.nn.softmax(scores, axis=-1)
            ctx = jnp.einsum('bhqs,bshk->bqhk', attn, vh)
            mha_out = jnp.einsum('bqhk,hko->bqo', ctx, wo) + bo
            mha_out = mha_out.reshape(N, T, WIDTH)
            out = mha_out @ proj_w + proj_b
            return out
        key = jax.random.key(seed)
        ks = jax.random.split(key, 8)
        N, T = (4, 1024)
        s = lambda *sh: 0.02
        x = jax.random.normal(ks[0], (N, T, D_MODEL), jnp.float32)
        conv_w = jax.random.normal(ks[1], (3, D_MODEL, 3 * WIDTH), jnp.float32) * 0.02
        conv_b = jnp.zeros((3 * WIDTH,), jnp.float32)
        wq = jax.random.normal(ks[2], (WIDTH, NUM_HEADS, KEY_DIM), jnp.float32) * 0.05
        wk = jax.random.normal(ks[3], (WIDTH, NUM_HEADS, KEY_DIM), jnp.float32) * 0.05
        wv = jax.random.normal(ks[4], (WIDTH, NUM_HEADS, KEY_DIM), jnp.float32) * 0.05
        bq = jnp.zeros((NUM_HEADS, KEY_DIM), jnp.float32)
        bk = jnp.zeros((NUM_HEADS, KEY_DIM), jnp.float32)
        bv = jnp.zeros((NUM_HEADS, KEY_DIM), jnp.float32)
        wo = jax.random.normal(ks[5], (NUM_HEADS, KEY_DIM, WIDTH), jnp.float32) * 0.05
        bo = jnp.zeros((WIDTH,), jnp.float32)
        proj_w = jax.random.normal(ks[6], (WIDTH, D_MODEL), jnp.float32) * 0.05
        proj_b = jnp.zeros((D_MODEL,), jnp.float32)
        return dict(x=x, conv_w=conv_w, conv_b=conv_b, wq=wq, bq=bq, wk=wk, bk=bk, wv=wv, bv=bv, wo=wo, bo=bo, proj_w=proj_w, proj_b=proj_b)
    _L0_attn_a_in = _L0_attn_a_setup()

    def _L0_attn_b_setup():
        import jax, jax.numpy as jnp
        import numpy as np
        HEADS = 16
        key = jax.random.key(seed)
        ks = jax.random.split(key, 5)
        B, T, D = (2, 512, 512)
        s = 0.02
        return {'x': jax.random.normal(ks[0], (B, T, D), dtype=jnp.float32), 'Wq': jax.random.normal(ks[1], (D, D), dtype=jnp.float32) * s, 'Wk': jax.random.normal(ks[2], (D, D), dtype=jnp.float32) * s, 'Wv': jax.random.normal(ks[3], (D, D), dtype=jnp.float32) * s, 'Wo': jax.random.normal(ks[4], (D, D), dtype=jnp.float32) * s}
    _L0_attn_b_in = _L0_attn_b_setup()

    def _L0_ffn_setup():
        import jax, jax.numpy as jnp
        import numpy as np
        RANK = 64
        SCALING = 1.0 / RANK
        TEMPERATURE = 1.0
        key = jax.random.key(seed)
        k_x, k_a, k_b, k_w = jax.random.split(key, 4)
        B_, S, D = (4, 512, 512)
        E, R, O = (8, RANK, 512)
        x = jax.random.normal(k_x, (B_, S, D), dtype=jnp.float32)
        A = jax.random.normal(k_a, (E, R, D), dtype=jnp.float32) * (1.0 / np.sqrt(D))
        Bw = jax.random.normal(k_b, (E, O, R), dtype=jnp.float32) * 0.02
        Wr = jax.random.normal(k_w, (E, D), dtype=jnp.float32) * (1.0 / np.sqrt(D))
        br = jnp.zeros((E,), dtype=jnp.float32)
        return {'x': x, 'A': A, 'B': Bw, 'Wr': Wr, 'br': br}
    _L0_ffn_in = _L0_ffn_setup()
    _d = {'L0_attn_a_x': _L0_attn_a_in['x'], 'L0_attn_a_conv_w': _L0_attn_a_in['conv_w'], 'L0_attn_a_conv_b': _L0_attn_a_in['conv_b'], 'L0_attn_a_wq': _L0_attn_a_in['wq'], 'L0_attn_a_bq': _L0_attn_a_in['bq'], 'L0_attn_a_wk': _L0_attn_a_in['wk'], 'L0_attn_a_bk': _L0_attn_a_in['bk'], 'L0_attn_a_wv': _L0_attn_a_in['wv'], 'L0_attn_a_bv': _L0_attn_a_in['bv'], 'L0_attn_a_wo': _L0_attn_a_in['wo'], 'L0_attn_a_bo': _L0_attn_a_in['bo'], 'L0_attn_a_proj_w': _L0_attn_a_in['proj_w'], 'L0_attn_a_proj_b': _L0_attn_a_in['proj_b'], 'L0_attn_b_Wq': _L0_attn_b_in['Wq'], 'L0_attn_b_Wk': _L0_attn_b_in['Wk'], 'L0_attn_b_Wv': _L0_attn_b_in['Wv'], 'L0_attn_b_Wo': _L0_attn_b_in['Wo'], 'L0_ffn_A': _L0_ffn_in['A'], 'L0_ffn_B': _L0_ffn_in['B'], 'L0_ffn_Wr': _L0_ffn_in['Wr'], 'L0_ffn_br': _L0_ffn_in['br']}
    _x0 = _d['L0_attn_a_x']
    _d['L0_attn_a_x'] = jax.random.normal(jax.random.fold_in(jax.random.key(seed), 1), (2, 2048, 512), dtype=_x0.dtype)
    del _x0
    return _d

def reference(L0_attn_a_x, L0_attn_a_conv_w, L0_attn_a_conv_b, L0_attn_a_wq, L0_attn_a_bq, L0_attn_a_wk, L0_attn_a_bk, L0_attn_a_wv, L0_attn_a_bv, L0_attn_a_wo, L0_attn_a_bo, L0_attn_a_proj_w, L0_attn_a_proj_b, L0_attn_b_Wq, L0_attn_b_Wk, L0_attn_b_Wv, L0_attn_b_Wo, L0_ffn_A, L0_ffn_B, L0_ffn_Wr, L0_ffn_br):

    def _L0_attn_a_ref(x, conv_w, conv_b, wq, bq, wk, bk, wv, bv, wo, bo, proj_w, proj_b):
        import jax, jax.numpy as jnp
        import numpy as np
        from jax import lax
        BLOCKS = 16
        NUM_HEADS = 8
        KEY_DIM = 64
        WIDTH = 128
        D_MODEL = 512

        def _forward(x, conv_w, conv_b, wq, bq, wk, bk, wv, bv, wo, bo, proj_w, proj_b):
            N, T, D = x.shape
            xp = jnp.pad(x, ((0, 0), (2, 0), (0, 0)))
            qkv = lax.conv_general_dilated(xp, conv_w, window_strides=(1,), padding='VALID', dimension_numbers=('NWC', 'WIO', 'NWC')) + conv_b
            q, k, v = jnp.split(qkv, 3, axis=-1)
            block_len = T // BLOCKS
            qb = q.reshape(N * BLOCKS, block_len, WIDTH)
            kb = k.reshape(N * BLOCKS, block_len, WIDTH)
            vb = v.reshape(N * BLOCKS, block_len, WIDTH)
            qh = jnp.einsum('bsd,dhk->bshk', qb, wq) + bq
            kh = jnp.einsum('bsd,dhk->bshk', kb, wk) + bk
            vh = jnp.einsum('bsd,dhk->bshk', vb, wv) + bv
            scale = 1.0 / jnp.sqrt(jnp.asarray(KEY_DIM, qh.dtype))
            scores = jnp.einsum('bqhk,bshk->bhqs', qh * scale, kh)
            causal = jnp.tril(jnp.ones((block_len, block_len), bool))
            scores = jnp.where(causal[None, None], scores, jnp.asarray(-1000000000.0, scores.dtype))
            attn = jax.nn.softmax(scores, axis=-1)
            ctx = jnp.einsum('bhqs,bshk->bqhk', attn, vh)
            mha_out = jnp.einsum('bqhk,hko->bqo', ctx, wo) + bo
            mha_out = mha_out.reshape(N, T, WIDTH)
            out = mha_out @ proj_w + proj_b
            return out
        return _forward(x, conv_w, conv_b, wq, bq, wk, bk, wv, bv, wo, bo, proj_w, proj_b)

    def _L0_attn_b_ref(x, Wq, Wk, Wv, Wo):
        import jax, jax.numpy as jnp
        import numpy as np
        HEADS = 16
        B, T, _ = x.shape
        H = HEADS
        Dh = Wq.shape[1] // H
        q = (x @ Wq).reshape(B, T, H, Dh)
        k = (x @ Wk).reshape(B, T, H, Dh)
        v = (x @ Wv).reshape(B, T, H, Dh)
        scores = jnp.einsum('bthd,bshd->bhts', q, k)
        mask = jnp.tril(jnp.ones((T, T), dtype=scores.dtype))
        scores = scores * mask
        attn = jax.nn.softmax(scores / T ** 0.5, axis=-1)
        out = jnp.einsum('bhts,bshd->bthd', attn, v).reshape(B, T, H * Dh)
        return out @ Wo

    def _L0_ffn_ref(x, A, B, Wr, br):
        import jax, jax.numpy as jnp
        import numpy as np
        RANK = 64
        SCALING = 1.0 / RANK
        TEMPERATURE = 1.0
        batch, seq, d = x.shape
        E, out_dim = (B.shape[0], B.shape[1])
        x_flat = x.reshape(-1, d)
        logits = (x_flat @ Wr.T + br) / TEMPERATURE
        probs = jax.nn.softmax(logits, axis=-1)
        expert_idx = jnp.argmax(probs, axis=-1)
        expert_weight = jnp.max(probs, axis=-1)
        h = jnp.einsum('nd,erd->ner', x_flat, A)
        y = jnp.einsum('ner,eor->neo', h, B) * SCALING
        sel = jnp.take_along_axis(y, expert_idx[:, None, None], axis=1)[:, 0, :]
        out_flat = sel * expert_weight[:, None]
        return out_flat.reshape(batch, seq, out_dim)
    x = L0_attn_a_x
    x = x + _L0_attn_a_ref(_layernorm(x, axis=-1), L0_attn_a_conv_w, L0_attn_a_conv_b, L0_attn_a_wq, L0_attn_a_bq, L0_attn_a_wk, L0_attn_a_bk, L0_attn_a_wv, L0_attn_a_bv, L0_attn_a_wo, L0_attn_a_bo, L0_attn_a_proj_w, L0_attn_a_proj_b)
    x = x + _L0_ffn_ref(_layernorm(x, axis=-1), L0_ffn_A, L0_ffn_B, L0_ffn_Wr, L0_ffn_br)
    x = x + _L0_attn_b_ref(_layernorm(x, axis=-1), L0_attn_b_Wq, L0_attn_b_Wk, L0_attn_b_Wv, L0_attn_b_Wo)
    x = x + _L0_ffn_ref(_layernorm(x, axis=-1), L0_ffn_A, L0_ffn_B, L0_ffn_Wr, L0_ffn_br)
    return x

_drawn_inputs = setup_inputs


def setup_inputs(seed=0):
    import zlib

    import numpy as np

    out = dict(_drawn_inputs(seed))
    spreads = {'L0_attn_a_conv_b': (0.0, 0.1),
     'L0_attn_a_bq': (0.0, 0.8),
     'L0_attn_a_bk': (0.0, 0.8),
     'L0_attn_a_bv': (0.0, 0.1),
     'L0_attn_a_bo': (0.0, 0.1),
     'L0_attn_a_proj_b': (0.0, 0.1),
     'L0_ffn_br': (0.0, 0.8)}
    factors = {'L0_attn_a_wq': 5.86,
     'L0_attn_a_wk': 5.723,
     'L0_attn_b_Wq': 8.0,
     'L0_attn_b_Wk': 8.0,
     'L0_ffn_A': 8.0,
     'L0_ffn_B': 8.0,
     'L0_ffn_Wr': 8.0}
    for name, (base, spread) in spreads.items():
        noise = np.random.default_rng([zlib.crc32(name.encode()), seed]).standard_normal(out[name].shape)
        drawn = base * np.exp(spread * noise) if base else spread * noise
        out[name] = jnp.asarray(drawn.astype(out[name].dtype))
    for name, factor in factors.items():
        out[name] = (out[name] * factor).astype(out[name].dtype)
    return out
```

```python
import concourse.bass as bass
from concourse import mybir
from contextlib import ExitStack

fp32 = mybir.dt.float32
f32r = mybir.dt.float32r
ALU = mybir.AluOpType
ACT = mybir.ActivationFunctionType
AX = mybir.AxisListType

P = 128
D = 512
KT = D // P
TOKENS = 4096
BATCH = 2
T = TOKENS // BATCH
CHUNK = 512
TT = CHUNK // P
CHUNKS = TOKENS // CHUNK
EPS = 1e-5
TAPS = 3
HALO = TAPS - 1
A_HEADS, A_DIM, A_WIDTH = 8, 64, 128
PAIRS = A_HEADS // 2
A_SCALE = A_DIM ** -0.5
EXPERTS, RANK = 8, 64
B_HEADS, B_DIM = 16, 32
TQ = T // P
B_SCALE = T ** -0.5
BANKS = 8
BIG = 3.0e38


class Split:

    def __init__(self, new, name, shape):
        self.high = new(name + "_high", shape, f32r)
        self.low = new(name + "_low", shape, f32r)


def product(pe, out, stationary, moving, at, mv, first, last):
    pe.matmul(out, stationary.high[at], moving.high[mv], start=first, stop=False)
    pe.matmul(out, stationary.low[at], moving.high[mv], start=False, stop=False)
    return pe.matmul(out, stationary.high[at], moving.low[mv], start=False, stop=last)


def load_weights(nc, weights, others=()):
    with ExitStack() as ctx:
        raw = [ctx.enter_context(nc.sbuf_tensor(f"{n}_raw", list(s.high.shape), fp32)) for n, _, s in weights]
        arrived = [ctx.enter_context(nc.semaphore(f"{n}_arrived")) for n, _, _ in weights]
        others_in = ctx.enter_context(nc.semaphore("others_in"))
        weight_high = ctx.enter_context(nc.semaphore("weight_high"))
        block = ctx.enter_context(nc.Block())

        @block.sync
        def _(sp):
            for (_, view, _), tile, sem in zip(weights, raw, arrived):
                sp.dma_start(tile[:], view).then_inc(sem, 16)
            for tile, view in others:
                sp.dma_start(tile, view).then_inc(others_in, 16)
            if others:
                sp.wait_ge(others_in, 16 * len(others))

        @block.scalar
        def _(act):
            for (_, _, split), tile, sem in zip(weights, raw, arrived):
                act.wait_ge(sem, 16)
                act.activation(split.high[:], tile[:], ACT.Copy).then_inc(weight_high, 1)

        @block.vector
        def _(dve):
            for n, ((_, _, split), tile) in enumerate(zip(weights, raw)):
                dve.wait_ge(weight_high, n + 1)
                dve.tensor_tensor(split.low[:], tile[:], split.high[:].bitcast(fp32), ALU.subtract)



def wait_for(engine, semaphore, value):
    if not isinstance(value, int) or value > 0:
        engine.wait_ge(semaphore, value)


class Norm:

    def __init__(self, nc, ctx, tag):
        def sbuf(name, shape):
            return ctx.enter_context(nc.sbuf_tensor(f"{name}_{tag}", shape, fp32))

        def sem(name):
            return ctx.enter_context(nc.semaphore(f"{name}_{tag}"))

        self.x = sbuf("x", [P, TT, D])
        self.xn = sbuf("xn", [P, TT, D])
        self.stats = sbuf("stats", [P, TT, 6])
        self.moments = sbuf("moments", [P, TT, 2])
        self.var_eps = sbuf("var_eps", [P, TT])
        self.rstd = sbuf("rstd", [P, TT])
        self.eps = sbuf("eps", [P, TT])
        self.minus_half = sbuf("minus_half", [P, TT])
        self.x_loaded = sem("x_loaded")
        self.stats_taken = sem("stats_taken")
        self.moments_ready = sem("moments_ready")
        self.norm_steps = sem("norm_steps")
        self.xn_ready = sem("xn_ready")
        self.constants_set = sem("constants_set")

    def load(self, sp, view, i):
        sp.wait_ge(self.xn_ready, i)
        sp.dma_start(self.x[:], view[bass.ds(i * CHUNK, CHUNK), :].rearrange("(t p) d -> p t d", p=P)).then_inc(
            self.x_loaded, 16
        )

    def take_moments(self, dve, i):
        dve.wait_ge(self.x_loaded, 16 * (i + 1))
        dve.wait_ge(self.xn_ready, i)
        for t in range(TT):
            last = dve.bn_stats(self.stats[:, t, :], self.x[:, t, :])
        last.then_inc(self.stats_taken, 1)
        dve.wait_ge(self.constants_set, 2)
        dve.wait_ge(self.stats_taken, i + 1)
        for t in range(TT):
            last = dve.bn_aggr(self.moments[:, t, :], self.stats[:, t, :])
        last.then_inc(self.moments_ready, 1)

    def set_constants(self, pool):
        pool.memset(self.minus_half[:], -0.5).then_inc(self.constants_set, 1)
        pool.memset(self.eps[:], EPS).then_inc(self.constants_set, 1)
        pool.wait_ge(self.constants_set, 2)

    def apply(self, pool, i):
        pool.wait_ge(self.moments_ready, i + 1)
        pool.tensor_tensor(self.var_eps[:], self.moments[:, :, 1], self.eps[:], ALU.add).then_inc(self.norm_steps, 1)
        pool.tensor_tensor(
            self.xn[:], self.x[:], self.moments[:, :, 0:1].broadcast_to([P, TT, D]), ALU.subtract
        ).then_inc(self.norm_steps, 1)
        pool.wait_ge(self.norm_steps, 3 * i + 1)
        pool.tensor_tensor(self.rstd[:], self.var_eps[:], self.minus_half[:], ALU.pow).then_inc(self.norm_steps, 1)
        pool.wait_ge(self.norm_steps, 3 * i + 3)
        pool.tensor_tensor(
            self.xn[:], self.xn[:], self.rstd[:].rearrange("p (t a) -> p t a", a=1).broadcast_to([P, TT, D]), ALU.mult
        ).then_inc(self.xn_ready, 1)


def all_but_last(engine, body):
    with engine.Fori(0, CHUNKS - 1) as i:
        body(i, False)
    body(CHUNKS - 1, True)


def turn(pe, bank, source, columns, identity):
    for t in range(TT):
        last = pe.transpose(bank[:, t * P : (t + 1) * P], source[:, t, columns], identity[:])
    return last


def tile(n):
    return slice(n * P, (n + 1) * P)


def conv_attention(nc, x_in, x_out, w):
    with ExitStack() as ctx:
        def sbuf(name, shape, dt=fp32):
            return ctx.enter_context(nc.sbuf_tensor(f"{name}_a", shape, dt))

        def sem(name):
            return ctx.enter_context(nc.semaphore(f"{name}_a"))

        conv = Split(sbuf, "conv", [P, TAPS * KT, 3 * A_WIDTH])
        wq, wk, wv = (Split(sbuf, n, [P, D]) for n in ("wq", "wk", "wv"))
        wo = Split(sbuf, "wo", [P, PAIRS, A_WIDTH])
        proj = Split(sbuf, "proj", [P, D])
        identity = sbuf("identity", [P, P])
        causal = sbuf("causal", [P, P])
        conv_b = sbuf("conv_b", [P, 3])
        bq, bk, bv = (sbuf(n, [P, PAIRS]) for n in ("bq", "bk", "bv"))
        bo = sbuf("bo", [P, 1])
        proj_b = sbuf("proj_b", [P, D])
        keep = sbuf("keep", [P, CHUNKS])
        load_weights(nc, [
            ("conv", w["conv_w"].rearrange("s (k p) n -> p (s k) n", p=P), conv),
            ("wq", w["wq"], wq), ("wk", w["wk"], wk), ("wv", w["wv"], wv),
            ("wo", w["wo"].rearrange("(j p) n -> p j n", p=P), wo),
            ("proj", w["proj_w"], proj),
        ], [
            (identity[:], w["identity"]), (causal[:], w["causal"]), (keep[:], w["keep"]),
            (conv_b[:], w["conv_b"]), (bq[:], w["bq"]), (bk[:], w["bk"]), (bv[:], w["bv"]),
            (bo[:], w["bo"]), (proj_b[:], w["proj_b"].broadcast_to([P, D])),
        ])

        norm = Norm(nc, ctx, "a")
        xT = Split(sbuf, "xT", [P, KT, HALO + CHUNK])
        qkv = [Split(sbuf, n, [P, CHUNK]) for n in ("q", "k", "v")]
        qh = [Split(sbuf, f"qh{e}", [P, CHUNK]) for e in range(2)]
        kh = [Split(sbuf, f"kh{e}", [P, CHUNK]) for e in range(2)]
        vh = Split(sbuf, "vh", [P, TT, D])
        masked = [sbuf(f"masked{h}", [P, TT, P]) for h in range(2)]
        peak = [sbuf(f"peak{h}", [P, TT]) for h in range(2)]
        minus_peak = [[sbuf(f"minus_peak{e}{h}", [P, TT]) for h in range(2)] for e in range(2)]
        probs = [[sbuf(f"probs{e}{h}", [P, TT, P]) for h in range(2)] for e in range(2)]
        sums = [[sbuf(f"sums{e}{h}", [P, TT]) for h in range(2)] for e in range(2)]
        over_sums = [[sbuf(f"over_sums{e}{h}", [P, TT]) for h in range(2)] for e in range(2)]
        probsT = [Split(sbuf, f"probsT{h}", [P, CHUNK]) for h in range(2)]
        ctxT = Split(sbuf, "ctxT", [P, PAIRS, CHUNK])
        mixT = Split(sbuf, "mixT", [P, CHUNK])
        result = sbuf("result", [P, TT, D])
        banks = ctx.enter_context(nc.psum_tensor("banks_a", [P, BANKS, CHUNK], fp32))

        bank_filled, high_ready, bank_drained = sem("bank_filled"), sem("high_ready"), sem("bank_drained")
        halo_cleared, halo_high, halo_low = sem("halo_cleared"), sem("halo_high"), sem("halo_low")
        masked_ready, peak_taken, peak_ready = sem("masked_ready"), sem("peak_taken"), sem("peak_ready")
        exp_done, sums_inverted, probs_ready = sem("exp_done"), sem("sums_inverted"), sem("probs_ready")
        residual_loaded, residual_ready, stored = sem("residual_loaded"), sem("residual_ready"), sem("stored")

        X0, CONV0, V0, MIX, OUT0, TILES = 0, 4, 11, 43, 44, 48
        Q = [7] + [15 + 8 * (j - 1) for j in range(1, PAIRS)]
        K = [n + 1 for n in Q]
        S = [n + 2 for n in Q]
        PT = [19 + 8 * j for j in range(PAIRS)]
        C = [n + 2 for n in PT]
        PT[3], C[3] = 39, 41
        order = [("q", 0), ("k", 0), ("s", 0), ("v", 0)]
        for j in range(1, PAIRS):
            order += [("q", j), ("k", j), ("s", j), ("t", j - 1), ("c", j - 1)]
        order += [("t", 3), ("c", 3)]
        split_tiles = [n for n in range(OUT0) if n not in S and n - 1 not in S]
        SPLITS = len(split_tiles)

        def highs(n):
            return sum(m < n for m in split_tiles)

        block = ctx.enter_context(nc.Block())

        @block.sync
        def _(sp):
            def chunk(i, last):
                sp.wait_ge(stored, 16 * i)
                sp.dma_start(
                    result[:], x_in[bass.ds(i * CHUNK, CHUNK), :].rearrange("(t p) d -> p t d", p=P)
                ).then_inc(residual_loaded, 16)
                if not last:
                    norm.load(sp, x_in, i + 1)
                sp.wait_ge(bank_drained, TILES * (i + 1))
                sp.dma_start(
                    x_out[bass.ds(i * CHUNK, CHUNK), :].rearrange("(t p) d -> p t d", p=P), result[:]
                ).then_inc(stored, 16)

            norm.load(sp, x_in, 0)
            all_but_last(sp, chunk)
            sp.wait_ge(stored, 16 * CHUNKS)

        @block.gpsimd
        def _(pool):
            for part in (xT.high, xT.low):
                pool.memset(part[:, :, CHUNK:].bitcast(fp32), 0.0).then_inc(halo_cleared, 1)
            norm.set_constants(pool)
            norm.apply(pool, 0)

            def chunk(i, last):
                pool.wait_ge(residual_loaded, 16 * (i + 1))
                pool.tensor_tensor(
                    result[:], result[:], proj_b[:].rearrange("p (a d) -> p a d", a=1).broadcast_to([P, TT, D]), ALU.add
                ).then_inc(residual_ready, 1)
                if not last:
                    pool.wait_ge(bank_filled, TILES * i + X0 + KT)
                    norm.apply(pool, i + 1)
                for j in range(PAIRS):
                    for h in range(2):
                        n = 2 * j + h + 1
                        pool.wait_ge(sums_inverted, 2 * PAIRS * i + n)
                        e = j % 2
                        pool.tensor_tensor(
                            probs[e][h][:], probs[e][h][:],
                            over_sums[e][h][:].rearrange("p (t a) -> p t a", a=1).broadcast_to([P, TT, P]), ALU.mult,
                        ).then_inc(probs_ready, 1)

            all_but_last(pool, chunk)

        @block.tensor
        def _(pe):
            with pe.Fori(0, CHUNKS) as i:
                def fill(n, needs=None):
                    if needs is None or needs < n - BANKS:
                        needs = n - BANKS
                    if needs >= 0:
                        pe.wait_ge(bank_drained, TILES * i + needs + 1)
                    elif n == 0:
                        pe.wait_ge(bank_drained, TILES * i)
                    return banks[:, n % BANKS, :]

                pe.wait_ge(norm.xn_ready, i + 1)
                for k in range(KT):
                    turn(pe, fill(X0 + k), norm.xn, tile(k), identity).then_inc(bank_filled, 1)
                for c in range(3):
                    out = fill(CONV0 + c, X0 + KT - 1)
                    for s in range(TAPS):
                        for k in range(KT):
                            last = product(
                                pe, out, conv, xT, (slice(None), s * KT + k, tile(c)),
                                (slice(None), k, slice(s, s + CHUNK)),
                                s == 0 and k == 0, s == TAPS - 1 and k == KT - 1,
                            )
                    last.then_inc(bank_filled, 1)
                for what, j in order:
                    e = j % 2
                    if what == "q":
                        out = fill(Q[j], CONV0)
                        product(pe, out, wq, qkv[0], (slice(None), tile(j)), slice(None), True, True).then_inc(bank_filled, 1)
                    elif what == "k":
                        out = fill(K[j], CONV0 + 1)
                        product(pe, out, wk, qkv[1], (slice(None), tile(j)), slice(None), True, True).then_inc(bank_filled, 1)
                    elif what == "v":
                        for t in range(TT):
                            out = fill(V0 + t, CONV0 + 2)
                            product(pe, out, qkv[2], wv, (slice(None), tile(t)), slice(None), True, True).then_inc(bank_filled, 1)
                    elif what == "s":
                        for h in range(2):
                            out = fill(S[j] + h, K[j])
                            rows = slice(64 * h, 64 * h + 64)
                            for t in range(TT):
                                last = product(pe, out[:, tile(t)], qh[e], kh[e], (rows, tile(t)), (rows, tile(t)), True, True)
                            last.then_inc(bank_filled, 1)
                    elif what == "t":
                        for h in range(2):
                            out = fill(PT[j] + h)
                            pe.wait_ge(probs_ready, 2 * PAIRS * i + 2 * j + h + 1)
                            turn(pe, out, probs[e][h], slice(0, P), identity).then_inc(bank_filled, 1)
                    else:
                        for h in range(2):
                            out = fill(C[j] + h, max(PT[j] + h, V0 + TT - 1))
                            for t in range(TT):
                                last = product(
                                    pe, out[:, tile(t)], vh, probsT[h], (slice(None), t, tile(j)),
                                    (slice(None), tile(t)), True, True,
                                )
                            last.then_inc(bank_filled, 1)
                out = fill(MIX, C[3] + 1)
                for j in range(PAIRS):
                    last = product(pe, out, wo, ctxT, (slice(None), j), (slice(None), j), j == 0, j == PAIRS - 1)
                last.then_inc(bank_filled, 1)
                for t in range(TT):
                    out = fill(OUT0 + t, MIX)
                    product(pe, out, mixT, proj, (slice(None), tile(t)), slice(None), True, True).then_inc(bank_filled, 1)

        @block.scalar
        def _(act):
            act.wait_ge(halo_cleared, 2)
            with act.Fori(0, CHUNKS) as i:
                def high(n, out, rows=slice(0, P), bias=None):
                    act.wait_ge(bank_filled, TILES * i + n + 1)
                    source = banks[rows, n % BANKS, :]
                    if bias is None:
                        act.activation(out, source, ACT.Copy).then_inc(high_ready, 1)
                    else:
                        act.activation(out, source, ACT.Identity, bias=bias).then_inc(high_ready, 1)

                act.wait_ge(bank_filled, TILES * i)
                act.activation(
                    xT.high[:, :, 0:HALO], xT.high[:, :, CHUNK:].bitcast(fp32), ACT.Copy, scale=keep[:, bass.ds(i, 1)]
                ).then_inc(halo_high, 1)
                act.wait_ge(halo_high, i + 1)
                for k in range(KT):
                    high(X0 + k, xT.high[:, k, HALO:])
                for c in range(3):
                    high(CONV0 + c, qkv[c].high[:], bias=conv_b[:, c : c + 1])
                for what, j in order:
                    e = j % 2
                    if what == "q":
                        high(Q[j], qh[e].high[:], bias=bq[:, j : j + 1])
                    elif what == "k":
                        high(K[j], kh[e].high[:], bias=bk[:, j : j + 1])
                    elif what == "v":
                        for t in range(TT):
                            high(V0 + t, vh.high[:, t, :])
                    elif what == "s":
                        for h in range(2):
                            act.wait_ge(peak_ready, 2 * PAIRS * i + 2 * j + h + 1)
                            for t in range(TT):
                                last = act.activation(
                                    probs[e][h][:, t, :], masked[h][:, t, :], ACT.Exp, bias=minus_peak[e][h][:, t : t + 1],
                                    scale=A_SCALE, accum_out=sums[e][h][:, t : t + 1],
                                )
                            last.then_inc(exp_done, 1)
                    elif what == "t":
                        for h in range(2):
                            high(PT[j] + h, probsT[h].high[:])
                    else:
                        for h in range(2):
                            rows = slice(64 * h, 64 * h + 64)
                            high(C[j] + h, ctxT.high[rows, j, :], rows, bv[rows, j : j + 1])
                high(MIX, mixT.high[:], bias=bo[:, 0:1])

        @block.vector
        def _(dve):
            dve.wait_ge(halo_cleared, 2)
            norm.take_moments(dve, 0)

            def chunk(i, last_chunk):
                def low(n, split, at, rows=slice(0, P), bias=None):
                    dve.wait_ge(high_ready, SPLITS * i + highs(n) + 1)
                    source, of = banks[rows, n % BANKS, :], split.high[at].bitcast(fp32)
                    if bias is None:
                        dve.tensor_tensor(split.low[at], source, of, ALU.subtract).then_inc(bank_drained, 1)
                    else:
                        dve.scalar_tensor_tensor(
                            out=split.low[at], in0=source, scalar=bias, in1=of, op0=ALU.add, op1=ALU.subtract
                        ).then_inc(bank_drained, 1)

                def invert(j):
                    for h in range(2):
                        dve.wait_ge(exp_done, 2 * PAIRS * i + 2 * j + h + 1)
                        dve.reciprocal(over_sums[j % 2][h][:], sums[j % 2][h][:]).then_inc(sums_inverted, 1)

                dve.wait_ge(bank_filled, TILES * i)
                dve.tensor_scalar(
                    xT.low[:, :, 0:HALO], xT.low[:, :, CHUNK:].bitcast(fp32), keep[:, bass.ds(i, 1)], None, ALU.mult
                ).then_inc(halo_low, 1)
                dve.wait_ge(halo_low, i + 1)
                for k in range(KT):
                    low(X0 + k, xT, (slice(None), k, slice(HALO, HALO + CHUNK)))
                for c in range(3):
                    low(CONV0 + c, qkv[c], slice(None), bias=conv_b[:, c : c + 1])
                    if c == 0 and not last_chunk:
                        norm.take_moments(dve, i + 1)
                for what, j in order:
                    e = j % 2
                    if what == "q":
                        low(Q[j], qh[e], slice(None), bias=bq[:, j : j + 1])
                    elif what == "k":
                        low(K[j], kh[e], slice(None), bias=bk[:, j : j + 1])
                        if j >= 1:
                            invert(j - 1)
                    elif what == "v":
                        for t in range(TT):
                            low(V0 + t, vh, (slice(None), t))
                    elif what == "s":
                        for h in range(2):
                            n = 2 * PAIRS * i + 2 * j + h + 1
                            dve.wait_ge(bank_filled, TILES * i + S[j] + h + 1)
                            dve.tensor_tensor(
                                masked[h][:], banks[:, (S[j] + h) % BANKS, :].rearrange("p (t s) -> p t s", s=P),
                                causal[:].rearrange("p (a s) -> p a s", a=1).broadcast_to([P, TT, P]), ALU.add,
                            ).then_inc(bank_drained, 1)
                            dve.wait_ge(bank_drained, TILES * i + S[j] + h + 1)
                            dve.tensor_reduce(peak[h][:], masked[h][:], AX.X, ALU.max).then_inc(peak_taken, 1)
                            dve.wait_ge(peak_taken, n)
                            dve.tensor_scalar(minus_peak[e][h][:], peak[h][:], -A_SCALE, None, ALU.mult).then_inc(peak_ready, 1)
                        if j == PAIRS - 1:
                            invert(j)
                    elif what == "t":
                        for h in range(2):
                            low(PT[j] + h, probsT[h], slice(None))
                    else:
                        for h in range(2):
                            rows = slice(64 * h, 64 * h + 64)
                            low(C[j] + h, ctxT, (rows, j), rows, bv[rows, j : j + 1])
                low(MIX, mixT, slice(None), bias=bo[:, 0:1])
                dve.wait_ge(residual_ready, i + 1)
                for t in range(TT):
                    dve.wait_ge(bank_filled, TILES * i + OUT0 + t + 1)
                    dve.tensor_tensor(
                        result[:, t, :], banks[:, (OUT0 + t) % BANKS, :], result[:, t, :], ALU.add
                    ).then_inc(bank_drained, 1)

            all_but_last(dve, chunk)


def routed_experts(nc, x_in, x_out, w, tag):
    with ExitStack() as ctx:
        def sbuf(name, shape, dt=fp32):
            return ctx.enter_context(nc.sbuf_tensor(f"{name}_{tag}", shape, dt))

        def sem(name):
            return ctx.enter_context(nc.semaphore(f"{name}_{tag}"))

        down = Split(sbuf, "down", [P, KT, EXPERTS * RANK])
        up = Split(sbuf, "up", [P, EXPERTS * RANK // P, D])
        router = Split(sbuf, "router", [P, KT, EXPERTS])
        identity = sbuf("identity", [P, P])
        router_b = sbuf("router_b", [P, EXPERTS])
        rank = sbuf("rank", [P, EXPERTS])
        load_weights(nc, [
            (f"down_{tag}", w["down"].rearrange("(k p) n -> p k n", p=P), down),
            (f"up_{tag}", w["up"].rearrange("(k p) n -> p k n", p=P), up),
            (f"router_{tag}", w["router"].rearrange("(k p) n -> p k n", p=P), router),
        ], [
            (identity[:], w["identity"]), (router_b[:], w["router_b"].broadcast_to([P, EXPERTS])),
            (rank[:], w["expert_rank"].broadcast_to([P, EXPERTS])),
        ])
        norm = Norm(nc, ctx, tag)
        xT = Split(sbuf, "xT", [P, KT, CHUNK])
        logits = sbuf("logits", [P, TT, EXPERTS])
        peak = sbuf("peak", [P, TT])
        shifted = sbuf("shifted", [P, TT, EXPERTS])
        exps = sbuf("exps", [P, TT, EXPERTS])
        total = sbuf("total", [P, TT])
        weight = sbuf("weight", [P, TT])
        ranked = sbuf("ranked", [P, TT, EXPERTS])
        first = sbuf("first", [P, TT])
        chosen = sbuf("chosen", [P, TT, EXPERTS])
        gate = sbuf("gate", [P, TT, EXPERTS])
        hidden = sbuf("hidden", [P, TT, EXPERTS * RANK])
        hiddenT = Split(sbuf, "hiddenT", [P, KT, CHUNK])
        result = sbuf("result", [P, TT, D])
        banks = ctx.enter_context(nc.psum_tensor(f"banks_{tag}", [P, BANKS, CHUNK], fp32))
        bank_filled, high_ready, bank_drained = sem("bank_filled"), sem("high_ready"), sem("bank_drained")
        router_filled, gate_steps, exp_done = sem("router_filled"), sem("gate_steps"), sem("exp_done")
        residual_loaded, stored = sem("residual_loaded"), sem("stored")
        RING, X0, H0, HT0, OUT0, TILES = 4, 0, 4, 8, 12, 16
        LOGITS = RING
        GATE_STEPS = 9

        def over_experts(a):
            return a.rearrange("p (t a) -> p t a", a=1).broadcast_to([P, TT, EXPERTS])

        def over_tiles(a):
            return a.rearrange("p (a e) -> p a e", a=1).broadcast_to([P, TT, EXPERTS])

        block = ctx.enter_context(nc.Block())

        @block.sync
        def _(sp):
            def chunk(i, last):
                sp.wait_ge(stored, 16 * i)
                sp.dma_start(
                    result[:], x_in[bass.ds(i * CHUNK, CHUNK), :].rearrange("(t p) d -> p t d", p=P)
                ).then_inc(residual_loaded, 16)
                if not last:
                    norm.load(sp, x_in, i + 1)
                sp.wait_ge(bank_drained, TILES * (i + 1))
                sp.dma_start(
                    x_out[bass.ds(i * CHUNK, CHUNK), :].rearrange("(t p) d -> p t d", p=P), result[:]
                ).then_inc(stored, 16)

            norm.load(sp, x_in, 0)
            all_but_last(sp, chunk)
            sp.wait_ge(stored, 16 * CHUNKS)

        @block.gpsimd
        def _(pool):
            norm.set_constants(pool)
            norm.apply(pool, 0)
            with pool.Fori(0, CHUNKS - 1) as i:
                pool.wait_ge(bank_filled, TILES * i + X0 + KT)
                norm.apply(pool, i + 1)

        @block.tensor
        def _(pe):
            with pe.Fori(0, CHUNKS) as i:
                def fill(n, needs=-1):
                    pe.wait_ge(bank_drained, TILES * i + max(needs, n - RING) + 1 if n >= RING else TILES * i)
                    return banks[:, n % RING, :]

                pe.wait_ge(norm.xn_ready, i + 1)
                for k in range(KT):
                    turn(pe, fill(X0 + k), norm.xn, tile(k), identity).then_inc(bank_filled, 1)
                pe.wait_ge(bank_drained, TILES * i + X0 + KT)
                for t in range(TT):
                    for k in range(KT):
                        last = product(
                            pe, banks[:, LOGITS, t * EXPERTS : (t + 1) * EXPERTS], xT, router,
                            (slice(None), k, tile(t)), (slice(None), k), k == 0, k == KT - 1,
                        )
                last.then_inc(router_filled, 1)
                for t in range(TT):
                    out = fill(H0 + t)
                    for k in range(KT):
                        last = product(pe, out, xT, down, (slice(None), k, tile(t)), (slice(None), k), k == 0, k == KT - 1)
                    last.then_inc(bank_filled, 1)
                for k in range(KT):
                    turn(pe, fill(HT0 + k, H0 + TT - 1), hidden, tile(k), identity).then_inc(bank_filled, 1)
                for t in range(TT):
                    out = fill(OUT0 + t, HT0 + KT - 1)
                    for k in range(KT):
                        last = product(pe, out, hiddenT, up, (slice(None), k, tile(t)), (slice(None), k), k == 0, k == KT - 1)
                    last.then_inc(bank_filled, 1)

        @block.scalar
        def _(act):
            with act.Fori(0, CHUNKS) as i:
                def high(n, out):
                    act.wait_ge(bank_filled, TILES * i + n + 1)
                    act.activation(out, banks[:, n % RING, :], ACT.Copy).then_inc(high_ready, 1)

                for k in range(KT):
                    high(X0 + k, xT.high[:, k, :])
                act.wait_ge(gate_steps, GATE_STEPS * i + 3)
                act.activation(exps[:], shifted[:], ACT.Exp).then_inc(exp_done, 1)
                for k in range(KT):
                    high(HT0 + k, hiddenT.high[:, k, :])

        @block.vector
        def _(dve):
            norm.take_moments(dve, 0)

            def chunk(i, last_chunk):
                def low(n, m, split, at):
                    dve.wait_ge(high_ready, 2 * KT * i + m + 1)
                    dve.tensor_tensor(
                        split.low[at], banks[:, n % RING, :], split.high[at].bitcast(fp32), ALU.subtract
                    ).then_inc(bank_drained, 1)

                for k in range(KT):
                    low(X0 + k, k, xT, (slice(None), k))
                at = GATE_STEPS * i
                dve.wait_ge(router_filled, i + 1)
                dve.tensor_tensor(
                    logits[:], banks[:, LOGITS, 0 : TT * EXPERTS].rearrange("p (t e) -> p t e", e=EXPERTS),
                    over_tiles(router_b[:]), ALU.add,
                ).then_inc(gate_steps, 1)
                dve.wait_ge(gate_steps, at + 1)
                dve.tensor_reduce(peak[:], logits[:], AX.X, ALU.max).then_inc(gate_steps, 1)
                dve.wait_ge(gate_steps, at + 2)
                dve.tensor_tensor(shifted[:], logits[:], over_experts(peak[:]), ALU.subtract).then_inc(gate_steps, 1)
                dve.wait_ge(gate_steps, at + 3)
                dve.scalar_tensor_tensor(
                    out=ranked[:], in0=shifted[:], scalar=0.0, in1=over_tiles(rank[:]), op0=ALU.is_ge, op1=ALU.mult
                ).then_inc(gate_steps, 1)
                dve.wait_ge(gate_steps, at + 4)
                dve.tensor_reduce(first[:], ranked[:], AX.X, ALU.max).then_inc(gate_steps, 1)
                dve.wait_ge(gate_steps, at + 5)
                dve.tensor_tensor(chosen[:], ranked[:], over_experts(first[:]), ALU.is_equal).then_inc(gate_steps, 1)
                dve.wait_ge(exp_done, i + 1)
                dve.tensor_reduce(total[:], exps[:], AX.X, ALU.add).then_inc(gate_steps, 1)
                dve.wait_ge(gate_steps, at + 7)
                dve.reciprocal(weight[:], total[:]).then_inc(gate_steps, 1)
                dve.wait_ge(gate_steps, at + 8)
                dve.scalar_tensor_tensor(
                    out=gate[:], in0=chosen[:], scalar=1.0 / RANK, in1=over_experts(weight[:]), op0=ALU.mult, op1=ALU.mult
                ).then_inc(gate_steps, 1)
                dve.wait_ge(gate_steps, at + 9)
                for t in range(TT):
                    dve.wait_ge(bank_filled, TILES * i + H0 + t + 1)
                    dve.tensor_tensor(
                        hidden[:, t, :].rearrange("p (e r) -> p e r", r=RANK),
                        banks[:, (H0 + t) % RING, :].rearrange("p (e r) -> p e r", r=RANK),
                        gate[:, t, :].rearrange("p (e a) -> p e a", a=1).broadcast_to([P, EXPERTS, RANK]), ALU.mult,
                    ).then_inc(bank_drained, 1)
                for k in range(KT):
                    low(HT0 + k, KT + k, hiddenT, (slice(None), k))
                if not last_chunk:
                    norm.take_moments(dve, i + 1)
                dve.wait_ge(residual_loaded, 16 * (i + 1))
                for t in range(TT):
                    dve.wait_ge(bank_filled, TILES * i + OUT0 + t + 1)
                    dve.tensor_tensor(
                        result[:, t, :], banks[:, (OUT0 + t) % RING, :], result[:, t, :], ALU.add
                    ).then_inc(bank_drained, 1)

            all_but_last(dve, chunk)


def project_qkv(nc, x_in, qT, kT, v, w):
    with ExitStack() as ctx:
        def sbuf(name, shape, dt=fp32):
            return ctx.enter_context(nc.sbuf_tensor(f"{name}_p", shape, dt))

        def sem(name):
            return ctx.enter_context(nc.semaphore(f"{name}_p"))

        weights = [Split(sbuf, n, [P, KT, D]) for n in ("Wq", "Wk", "Wv")]
        identity = sbuf("identity", [P, P])
        load_weights(nc, [
            (n, w[n].rearrange("(k p) n -> p k n", p=P), s) for n, s in zip(("Wq", "Wk", "Wv"), weights)
        ], [(identity[:], w["identity"])])
        norm = Norm(nc, ctx, "p")
        xT = Split(sbuf, "xT", [P, KT, CHUNK])
        outT = [Split(sbuf, n, [P, KT, CHUNK]) for n in ("queries", "keys")]
        values = sbuf("values", [P, TT, D])
        banks = ctx.enter_context(nc.psum_tensor("banks_p", [P, BANKS, CHUNK], fp32))
        bank_filled, high_ready, bank_drained = sem("bank_filled"), sem("high_ready"), sem("bank_drained")
        queries_stored, keys_stored, values_stored = sem("queries_stored"), sem("keys_stored"), sem("values_stored")
        X0, Q0, K0, V0, TILES = 0, 4, 8, 12, 16
        SPLITS = 12
        HEAD_PAIRS = B_HEADS // 2
        CHUNKS_PER_SEQUENCE = T // CHUNK
        block = ctx.enter_context(nc.Block())

        @block.sync
        def _(sp):
            with sp.Fori(0, BATCH) as b:
                with sp.Fori(0, CHUNKS_PER_SEQUENCE) as c:
                    i = b * CHUNKS_PER_SEQUENCE + c
                    for at, dst, src, done in ((Q0, qT, outT[0], queries_stored), (K0, kT, outT[1], keys_stored)):
                        sp.wait_ge(bank_drained, TILES * i + at + KT)
                        for half, part in ((0, src.high), (1, src.low)):
                            for k in range(KT):
                                sp.dma_start(
                                    dst[half, bass.ds(b * D + k * P, P), bass.ds(c * CHUNK, CHUNK)],
                                    part[:, k, :].bitcast(fp32),
                                ).then_inc(done, 16)
                    sp.wait_ge(bank_drained, TILES * i + V0 + TT)
                    for t in range(TT):
                        sp.dma_start(
                            v[bass.ds(b * HEAD_PAIRS, HEAD_PAIRS), bass.ds(c * CHUNK + t * P, P), :].rearrange("g p c -> p g c"),
                            values[:, t, :].rearrange("p (g c) -> p g c", c=2 * B_DIM),
                        ).then_inc(values_stored, 16)
            sp.wait_ge(queries_stored, 2 * KT * 16 * CHUNKS)
            sp.wait_ge(keys_stored, 2 * KT * 16 * CHUNKS)
            sp.wait_ge(values_stored, TT * 16 * CHUNKS)

        @block.gpsimd
        def _(pool):
            norm.set_constants(pool)
            norm.load(pool, x_in, 0)
            norm.apply(pool, 0)
            norm.load(pool, x_in, 1)
            with pool.Fori(0, CHUNKS - 2) as i:
                pool.wait_ge(bank_filled, TILES * i + X0 + KT)
                norm.apply(pool, i + 1)
                norm.load(pool, x_in, i + 2)
            pool.wait_ge(bank_filled, TILES * (CHUNKS - 2) + X0 + KT)
            norm.apply(pool, CHUNKS - 1)

        @block.tensor
        def _(pe):
            with pe.Fori(0, CHUNKS) as i:
                def fill(n, needs=-1):
                    needs = max(needs, n - BANKS)
                    pe.wait_ge(bank_drained, TILES * i + needs + 1 if needs >= 0 else TILES * i)
                    return banks[:, n % BANKS, :]

                pe.wait_ge(norm.xn_ready, i + 1)
                for k in range(KT):
                    turn(pe, fill(X0 + k), norm.xn, tile(k), identity).then_inc(bank_filled, 1)
                for at, weight in ((Q0, weights[0]), (K0, weights[1])):
                    for m in range(KT):
                        out = fill(at + m, X0 + KT - 1)
                        for k in range(KT):
                            last = product(pe, out, weight, xT, (slice(None), k, tile(m)), (slice(None), k), k == 0, k == KT - 1)
                        last.then_inc(bank_filled, 1)
                for t in range(TT):
                    out = fill(V0 + t)
                    for k in range(KT):
                        last = product(pe, out, xT, weights[2], (slice(None), k, tile(t)), (slice(None), k), k == 0, k == KT - 1)
                    last.then_inc(bank_filled, 1)

        @block.scalar
        def _(act):
            with act.Fori(0, CHUNKS) as i:
                for at, split, done in ((X0, xT, None), (Q0, outT[0], queries_stored), (K0, outT[1], keys_stored)):
                    if done is not None:
                        act.wait_ge(done, 2 * KT * 16 * i)
                    for k in range(KT):
                        act.wait_ge(bank_filled, TILES * i + at + k + 1)
                        act.activation(split.high[:, k, :], banks[:, (at + k) % BANKS, :], ACT.Copy).then_inc(high_ready, 1)

        @block.vector
        def _(dve):
            norm.take_moments(dve, 0)

            def chunk(i, last_chunk):
                for at, split, done in ((X0, xT, None), (Q0, outT[0], queries_stored), (K0, outT[1], keys_stored)):
                    if done is not None:
                        dve.wait_ge(done, 2 * KT * 16 * i)
                    for k in range(KT):
                        dve.wait_ge(high_ready, SPLITS * i + at + k + 1)
                        dve.tensor_tensor(
                            split.low[:, k, :], banks[:, (at + k) % BANKS, :], split.high[:, k, :].bitcast(fp32), ALU.subtract
                        ).then_inc(bank_drained, 1)
                    if at == Q0 and not last_chunk:
                        norm.take_moments(dve, i + 1)
                dve.wait_ge(values_stored, TT * 16 * i)
                for t in range(TT):
                    dve.wait_ge(bank_filled, TILES * i + V0 + t + 1)
                    dve.tensor_copy(values[:, t, :], banks[:, (V0 + t) % BANKS, :]).then_inc(bank_drained, 1)

            all_but_last(dve, chunk)


HEAD_PAIRS = B_HEADS // 2
PAIR_DIM = 2 * B_DIM
WITH_SUM = B_DIM + 1


def sum_later_values(nc, v, later, w):
    with ExitStack() as ctx:
        def sbuf(name, shape, dt=fp32):
            return ctx.enter_context(nc.sbuf_tensor(f"{name}_s", shape, dt))

        def sem(name):
            return ctx.enter_context(nc.semaphore(f"{name}_s"))

        values = sbuf("values", [P, TQ, D])
        rest = sbuf("rest", [P, TQ, D])
        sums = sbuf("sums", [P, TQ, D])
        after = sbuf("after", [P, P])
        ones = sbuf("ones", [P, P])
        banks = ctx.enter_context(nc.psum_tensor("banks_s", [P, BANKS, D], fp32))
        values_loaded, constants_loaded, ones_set = sem("values_loaded"), sem("constants_loaded"), sem("ones_set")
        rest_ready, bank_filled, bank_drained, stored = sem("rest_ready"), sem("bank_filled"), sem("bank_drained"), sem("stored")
        block = ctx.enter_context(nc.Block())

        def by_pair(a, b, t):
            return a[bass.ds(b * HEAD_PAIRS, HEAD_PAIRS), tile(t), :].rearrange("g p c -> p g c")

        @block.sync
        def _(sp):
            sp.dma_start(after[:], w["after"]).then_inc(constants_loaded, 16)
            with sp.Fori(0, BATCH) as b:
                sp.wait_ge(bank_filled, TQ * b)
                for t in reversed(range(TQ)):
                    sp.dma_start(
                        values[:, t, :].rearrange("p (g c) -> p g c", c=PAIR_DIM), by_pair(v, b, t)
                    ).then_inc(values_loaded, 16)
                sp.wait_ge(bank_drained, TQ * (b + 1))
                for t in range(TQ):
                    sp.dma_start(
                        by_pair(later, b, t), sums[:, t, :].rearrange("p (g c) -> p g c", c=PAIR_DIM)
                    ).then_inc(stored, 16)
            sp.wait_ge(stored, 16 * TQ * BATCH)

        @block.gpsimd
        def _(pool):
            pool.memset(ones[:], 1.0).then_inc(ones_set, 1)
            pool.memset(rest[:, TQ - 1, :], 0.0).then_inc(ones_set, 1)
            pool.wait_ge(ones_set, 2)
            with pool.Fori(0, BATCH) as b:
                pool.wait_ge(bank_filled, TQ * b)
                pool.wait_ge(values_loaded, 16 * TQ * (b + 1))
                for t in reversed(range(TQ - 1)):
                    pool.wait_ge(rest_ready, (TQ - 1) * b + TQ - 2 - t)
                    pool.tensor_tensor(rest[:, t, :], rest[:, t + 1, :], values[:, t + 1, :], ALU.add).then_inc(rest_ready, 1)

        @block.tensor
        def _(pe):
            pe.wait_ge(constants_loaded, 16)
            pe.wait_ge(ones_set, 2)
            with pe.Fori(0, BATCH) as b:
                pe.wait_ge(values_loaded, 16 * TQ * (b + 1))
                for n, t in enumerate(reversed(range(TQ))):
                    if n > 0:
                        pe.wait_ge(rest_ready, (TQ - 1) * b + n)
                    pe.wait_ge(bank_drained, TQ * b + n + 1 - BANKS if n >= BANKS else TQ * b)
                    pe.matmul(banks[:, n % BANKS, :], after[:], values[:, t, :], start=True, stop=False)
                    pe.matmul(banks[:, n % BANKS, :], ones[:], rest[:, t, :], start=False, stop=True).then_inc(bank_filled, 1)

        @block.scalar
        def _(act):
            with act.Fori(0, BATCH) as b:
                act.wait_ge(stored, 16 * TQ * b)
                for n, t in enumerate(reversed(range(TQ))):
                    act.wait_ge(bank_filled, TQ * b + n + 1)
                    act.activation(sums[:, t, :], banks[:, n % BANKS, :], ACT.Copy).then_inc(bank_drained, 1)


def causal_product_attention(nc, qT, kT, v, later, context, w):
    with ExitStack() as ctx:
        def sbuf(name, shape, dt=fp32):
            return ctx.enter_context(nc.sbuf_tensor(f"{name}_b", shape, dt))

        def sem(name):
            return ctx.enter_context(nc.semaphore(f"{name}_b"))

        ROWS = 3 * B_DIM
        PEAK_ROW = ROWS
        QC = T // CHUNK
        GPAIRS = BATCH * HEAD_PAIRS
        units = [(c, j) for c in range(QC) for j in range(TT * c + TT)]
        UNITS = len(units)
        pieces = [(h, i, k) for h in range(2) for i in range(TQ) for k in range(i // TT + 1)]
        PIECES = len(pieces)
        LAG = 2
        PIECE_TO = 36
        PEAKS_AT = PIECE_TO + 1
        TURN_LAG = 3
        KEPT = 4
        DIAGONALS = TQ
        ends = [sum(TT * d + TT for d in range(c + 1)) - 1 for c in range(QC)]
        NORM_STEPS = 2

        def pieces_at(u):
            def before(u):
                return PIECES * min(u, PIECE_TO) // PIECE_TO
            return range(before(u), before(u + 1))

        queries = [sbuf(f"queries{e}", [P, 2, T], f32r) for e in range(2)]
        keys = [sbuf(f"keys{e}", [P, 2, T], f32r) for e in range(2)]
        values = [sbuf(f"values{e}", [P, TQ, 2, WITH_SUM]) for e in range(2)]
        later_values = sbuf("later_values", [P, TQ, 2, WITH_SUM])
        counts = sbuf("counts", [P, TQ])
        later_part = [sbuf(f"later_part{e}", [P, TQ, 2, WITH_SUM]) for e in range(2)]
        exps = [sbuf(f"exps{n}", [P, 2, CHUNK]) for n in range(KEPT)]
        identity = sbuf("identity", [P, P])
        upto = sbuf("upto", [P, P])
        since = sbuf("since", [P, P])
        scratch = [sbuf(f"scratch{n}", [P, P]) for n in range(2)]
        piece_peaks = sbuf("piece_peaks", [P, 2, TQ, 6])
        peaks = sbuf("peaks", [P, 2, TQ])
        minus_peaks = sbuf("minus_peaks", [P, 2 * TQ], f32r)
        minus_peaks_T = sbuf("minus_peaks_T", [2 * TQ, P], f32r)
        later_weight = sbuf("later_weight", [P, 2, TQ])
        sumsT = sbuf("sumsT", [P, CHUNK])
        numerator = sbuf("numerator", [P, TT, 2, WITH_SUM])
        over_sum = sbuf("over_sum", [P, TT, 2])
        out = sbuf("out", [P, TQ, 2, B_DIM])
        banks = ctx.enter_context(nc.psum_tensor("banks_b", [P, BANKS, CHUNK], fp32))
        SCORES, PRODUCTS = 2, 6

        constants_loaded, constants_set, counts_loaded = sem("constants_loaded"), sem("constants_set"), sem("counts_loaded")
        counts_set = sem("counts_set")
        queries_loaded = [[sem(f"queries_loaded{e}{c}") for c in range(QC)] for e in range(2)]
        keys_loaded = [[sem(f"keys_loaded{e}{c}") for c in range(QC)] for e in range(2)]
        values_loaded, later_loaded = sem("values_loaded"), sem("later_loaded")
        piece_filled, piece_taken, peaks_taken, peaks_negated = sem("piece_filled"), sem("piece_taken"), sem("peaks_taken"), sem("peaks_negated")
        peaks_turned, peaks_copied, peak_rows_loaded = sem("peaks_turned"), sem("peaks_copied"), sem("peak_rows_loaded")
        later_weight_ready, later_part_ready = sem("later_weight_ready"), sem("later_part_ready")
        scores_filled, exp_done, diagonal_masked = sem("scores_filled"), sem("exp_done"), sem("diagonal_masked")
        products_done, sums_copied, chunk_turned, norm_steps, chunk_out = (
            sem("products_done"), sem("sums_copied"), sem("chunk_turned"), sem("norm_steps"), sem("chunk_out"))
        stored, blocks_masked = sem("stored"), sem("blocks_masked")
        block = ctx.enter_context(nc.Block())

        PARTS = 3
        VALUE_LOADS = 2
        TAIL = LAG + TURN_LAG + 1

        def for_pairs(engine, at, rounds=(GPAIRS - 2) // 2):

            def step(e, g, first=False):
                for u in range(UNITS):
                    if u < TAIL and not first:
                        at(1 - e, g - 1, UNITS + u)
                    at(e, g, u)

            step(0, 0, first=True)
            with engine.Fori(0, rounds) as r:
                step(1, r * 2 + 1)
                step(0, r * 2 + 2)
            for g in range(2 * rounds + 1, GPAIRS):
                step(g % 2, g)
            for u in range(TAIL):
                at(1, GPAIRS - 1, UNITS + u)

        def is_last(g):
            return isinstance(g, int) and g == GPAIRS - 1

        def loads(e, g):
            return 8 * PARTS * (g + 2 - e)

        def query_start(c, j):
            return max(CHUNK * c, P * j)

        def is_diagonal(u):
            c, j = units[u]
            return j >= TT * c

        def diagonals(u):
            return sum(is_diagonal(n) for n in range(u + 1))

        @block.sync
        def _(sp):
            for dst, name in ((identity, "identity"), (upto, "upto"), (since, "since")):
                sp.dma_start(dst[:], w[name]).then_inc(constants_loaded, 16)
            sp.dma_start(counts[:], w["later_counts"]).then_inc(counts_loaded, 16)

            def load_chunk(e, g, c, tiles, view, done, halves):
                for n, half in enumerate(halves):
                    sp.dma_start(
                        tiles[e][n * B_DIM : (n + 1) * B_DIM, :, c * CHUNK : (c + 1) * CHUNK].bitcast(fp32),
                        view[half, bass.ds(g * PAIR_DIM, PAIR_DIM), c * CHUNK : (c + 1) * CHUNK].rearrange(
                            "(h r) t -> r h t", h=2
                        ),
                    ).then_inc(done[e][c], 16)

            def load_queries(e, g, c):
                load_chunk(e, g, c, queries, qT, queries_loaded, (0, 1, 0))

            def load_keys(e, g, c):
                load_chunk(e, g, c, keys, kT, keys_loaded, (0, 0, 1))

            def load_values(e, g):
                for dst, src, done in ((values[e], v, values_loaded), (later_values, later, later_loaded)):
                    for h in range(2):
                        sp.dma_start(
                            dst[:, :, h, 0:B_DIM],
                            src[g, :, h * B_DIM : (h + 1) * B_DIM].rearrange("(t p) c -> p t c", p=P),
                        ).then_inc(done, 16)

            def load_peak_rows(e, g):
                sp.wait_ge(peaks_copied, g + 1)
                for h in range(2):
                    sp.dma_start(
                        queries[e][PEAK_ROW : PEAK_ROW + 1, h, :].bitcast(fp32).rearrange("a (t p) -> a t p", p=P),
                        minus_peaks_T[h * TQ : (h + 1) * TQ, :].bitcast(fp32),
                    ).then_inc(peak_rows_loaded, 16)

            for e in range(2):
                for c in range(QC):
                    load_queries(e, e, c)
                    load_keys(e, e, c)
                if e == 0:
                    load_values(0, 0)
            load_peak_rows(0, 0)

            def at(e, g, u):
                if u == LAG and not is_last(g):
                    wait_for(sp, products_done, UNITS * g)
                    sp.wait_ge(later_part_ready, g + 1)
                    load_values(1 - e, g + 1)
                if u == PEAKS_AT and not is_last(g):
                    load_peak_rows(1 - e, g + 1)
                if not isinstance(g, int) or g < GPAIRS - 2:
                    for c in range(QC):
                        if u == ends[c] + 1:
                            sp.wait_ge(scores_filled, UNITS * g + ends[c] + 1)
                            load_queries(e, g + 2, c)
                        if u == ends[QC - 2] + 1 + TT * (c + 1):
                            sp.wait_ge(scores_filled, UNITS * g + ends[QC - 2] + 1 + TT * (c + 1))
                            load_keys(e, g + 2, c)
                if u == UNITS + LAG + TURN_LAG:
                    sp.wait_ge(chunk_out, QC * (g + 1))
                    sp.dma_start(
                        context[g, :, :].rearrange("(t p) c -> p t c", p=P), out[:].rearrange("p t h c -> p t (h c)")
                    ).then_inc(stored, 16)

            for_pairs(sp, at, (GPAIRS - 2) // 2 - 1)
            sp.wait_ge(stored, 16 * GPAIRS)

        @block.gpsimd
        def _(pool):
            for e in range(2):
                pool.memset(values[e][:, :, :, B_DIM:], 1.0).then_inc(constants_set, 1)
            pool.memset(sumsT[:], 0.0).then_inc(constants_set, 1)
            pool.memset(piece_peaks[:], 0.0).then_inc(constants_set, 1)
            for e in range(2):
                pool.wait_ge(constants_set, 4 + e)
                pool.memset(keys[e][PEAK_ROW : PEAK_ROW + 1, :, :].bitcast(fp32), 1.0).then_inc(constants_set, 1)
            pool.wait_ge(constants_set, 6)
            pool.memset(piece_peaks[:, :, TQ - 1, 5:6], -BIG).then_inc(constants_set, 1)
            pool.wait_ge(constants_loaded, 16 * 3)
            pool.wait_ge(counts_loaded, 16)
            for h in range(2):
                pool.tensor_copy(later_values[:, :, h, B_DIM], counts[:]).then_inc(counts_set, 1)
            pool.wait_ge(counts_set, 2)

            def weigh_later(e, g):
                pool.wait_ge(later_loaded, 16 * VALUE_LOADS * (g + 1))
                pool.wait_ge(later_weight_ready, g + 1)
                pool.tensor_tensor(
                    later_part[e][:], later_values[:],
                    later_weight[:].rearrange("p h (t a) -> p t h a", a=1).broadcast_to([P, TQ, 2, WITH_SUM]), ALU.mult,
                ).then_inc(later_part_ready, 1)

            weigh_later(0, 0)

            def at(e, g, u):
                if u < UNITS and is_diagonal(u):
                    pool.wait_ge(exp_done, UNITS * g + u + 1)
                    corner = exps[u % KEPT][:, :, 0:P]
                    pool.tensor_tensor(
                        corner, corner, since[:].rearrange("p (a q) -> p a q", a=1).broadcast_to([P, 2, P]), ALU.mult
                    ).then_inc(diagonal_masked, 1)
                if u == PEAKS_AT and not is_last(g):
                    wait_for(pool, chunk_out, QC * g)
                    weigh_later(1 - e, g + 1)

            for_pairs(pool, at)

        @block.tensor
        def _(pe):
            pe.wait_ge(constants_loaded, 16 * 3)
            pe.wait_ge(constants_set, 7)

            def piece(e, g, n):
                h, i, k = pieces[n]
                if h == 0 and i % TT == 0 and k == 0:
                    pe.wait_ge(queries_loaded[e][i // TT], loads(e, g))
                    pe.wait_ge(keys_loaded[e][i // TT], loads(e, g))
                if n == 0:
                    wait_for(pe, peaks_copied, g)
                wait_for(pe, piece_taken, PIECES * g + n - 1)
                width = min(CHUNK, P * (i + 1) - CHUNK * k)
                pe.matmul(
                    banks[:, n % 2, 0:width], queries[e][0:ROWS, h, tile(i)],
                    keys[e][0:ROWS, h, CHUNK * k : CHUNK * k + width], start=True, stop=True,
                ).then_inc(piece_filled, 1)

            def turn_peaks(g):
                pe.wait_ge(peaks_negated, g + 1)
                pe.transpose(banks[0 : 2 * TQ, 0, 0:P], minus_peaks[:].bitcast(fp32), identity[:]).then_inc(peaks_turned, 1)

            for n in range(PIECES):
                piece(0, 0, n)
            turn_peaks(0)

            def turn_sums(g, c):
                pe.wait_ge(sums_copied, QC * g + c + 1)
                for t in range(TT):
                    last = pe.transpose(banks[:, PRODUCTS + c % 2, tile(t)], sumsT[:, tile(t)], identity[:])
                last.then_inc(chunk_turned, 1)

            def scores(e, g, u):
                c, j = units[u]
                if u == 0:
                    pe.wait_ge(peak_rows_loaded, 32 * (g + 1))
                wait_for(pe, exp_done, UNITS * g + u - 1)
                q0 = query_start(c, j)
                width = CHUNK * (c + 1) - q0
                for h in range(2):
                    last = pe.matmul(
                        banks[:, SCORES + 2 * (u % 2) + h, 0:width], keys[e][0 : ROWS + 1, h, tile(j)],
                        queries[e][0 : ROWS + 1, h, q0 : q0 + width], start=True, stop=True,
                    )
                last.then_inc(scores_filled, 1)

            def products(e, g, u):
                c, j = units[u]
                pe.wait_ge(exp_done, UNITS * g + u + 1)
                if u == 0:
                    pe.wait_ge(values_loaded, 16 * VALUE_LOADS * (g + 1))
                if is_diagonal(u):
                    pe.wait_ge(diagonal_masked, DIAGONALS * g + diagonals(u))
                if j == 0:
                    wait_for(pe, chunk_out, QC * g + c - 1)
                width = CHUNK * (c + 1) - query_start(c, j)
                for h in range(2):
                    last = pe.matmul(
                        banks[64 * h : 64 * h + WITH_SUM, PRODUCTS + c % 2, CHUNK - width :], values[e][:, j, h, :],
                        exps[u % KEPT][:, h, 0:width], start=j == 0, stop=j == TT * c + TT - 1,
                    )
                last.then_inc(products_done, 1)

            def at(e, g, u):
                for c, end in enumerate(ends):
                    if u == end + LAG + TURN_LAG:
                        turn_sums(g, c)
                next_pieces = [] if u >= UNITS or is_last(g) else list(pieces_at(u))
                for n in next_pieces[:1]:
                    piece(1 - e, g + 1, n)
                if u == PEAKS_AT and not is_last(g):
                    turn_peaks(g + 1)
                if u < UNITS:
                    scores(e, g, u)
                for n in next_pieces[1:2]:
                    piece(1 - e, g + 1, n)
                if LAG <= u < UNITS + LAG:
                    products(e, g, u - LAG)
                for n in next_pieces[2:]:
                    piece(1 - e, g + 1, n)

            for_pairs(pe, at)

        @block.scalar
        def _(act):
            def copy_peaks(g):
                act.wait_ge(peaks_turned, g + 1)
                wait_for(act, peak_rows_loaded, 32 * g)
                act.activation(minus_peaks_T[:], banks[0 : 2 * TQ, 0, 0:P], ACT.Copy).then_inc(peaks_copied, 1)
                wait_for(act, later_part_ready, g)
                act.activation(
                    later_weight[:].rearrange("p h t -> p (h t)"), minus_peaks[:].bitcast(fp32), ACT.Exp, scale=B_SCALE
                ).then_inc(later_weight_ready, 1)

            copy_peaks(0)

            def at(e, g, u):
                if u >= UNITS:
                    return
                c, j = units[u]
                act.wait_ge(scores_filled, UNITS * g + u + 1)
                wait_for(act, products_done, UNITS * g + u + 1 - KEPT)
                width = CHUNK * (c + 1) - query_start(c, j)
                bank = SCORES + 2 * (u % 2)
                act.activation(
                    exps[u % KEPT][:, :, 0:width], banks[:, bank : bank + 2, 0:width], ACT.Exp, scale=B_SCALE
                ).then_inc(exp_done, 1)
                if u == PEAKS_AT and not is_last(g):
                    copy_peaks(g + 1)

            for_pairs(act, at)

        @block.vector
        def _(dve):
            dve.wait_ge(constants_set, 7)
            dve.wait_ge(constants_loaded, 16 * 3)

            def take_piece(g, n):
                h, i, k = pieces[n]
                before = min(CHUNK, P * i - CHUNK * k)
                dve.wait_ge(piece_filled, PIECES * g + n + 1)
                if before:
                    last = dve.tensor_reduce(piece_peaks[:, h, i, k : k + 1], banks[:, n % 2, 0:before], AX.X, ALU.max)
                if k == i // TT and before:
                    last = dve.tensor_tensor_reduce(
                        scratch[n % 2][:], banks[:, n % 2, before : before + P], upto[:], 1.0, -BIG, ALU.mult, ALU.max,
                        piece_peaks[:, h, i, 4:5],
                    )
                elif k == i // TT:
                    dve.tensor_tensor(scratch[n % 2][:], banks[:, n % 2, 0:P], upto[:], ALU.mult).then_inc(blocks_masked, 1)
                    dve.wait_ge(blocks_masked, 2 * QC * g + h * QC + k + 1)
                    last = dve.tensor_reduce(piece_peaks[:, h, i, 4:5], scratch[n % 2][:], AX.X, ALU.max)
                last.then_inc(piece_taken, 1)

            def finish_peaks(g):
                dve.wait_ge(piece_taken, PIECES * (g + 1))
                dve.tensor_reduce(peaks[:], piece_peaks[:], AX.X, ALU.max).then_inc(peaks_taken, 1)
                dve.wait_ge(peaks_taken, g + 1)
                wait_for(dve, later_weight_ready, g)
                dve.tensor_scalar(
                    minus_peaks[:], peaks[:].rearrange("p h t -> p (h t)"), -1.0, None, ALU.mult
                ).then_inc(peaks_negated, 1)

            for n in range(PIECES):
                take_piece(0, n)
            finish_peaks(0)

            def copy_sums(g, c):
                dve.wait_ge(products_done, UNITS * g + ends[c] + 1)
                wait_for(dve, chunk_turned, QC * g + c)
                for h in range(2):
                    rows = slice(64 * h, 64 * h + WITH_SUM)
                    last = dve.tensor_copy(sumsT[rows, :], banks[rows, PRODUCTS + c % 2, :])
                last.then_inc(sums_copied, 1)

            def normalise(e, g, c):
                done = QC * g + c
                if c == 0:
                    dve.wait_ge(later_part_ready, g + 1)
                    wait_for(dve, stored, 16 * g)
                dve.wait_ge(chunk_turned, done + 1)
                dve.tensor_tensor(
                    numerator[:],
                    banks[:, PRODUCTS + c % 2, :].rearrange("p (t h c) -> p t h c", h=2, c=64)[:, :, :, 0:WITH_SUM],
                    later_part[e][:, TT * c : TT * c + TT, :, :], ALU.add,
                ).then_inc(norm_steps, 1)
                dve.wait_ge(norm_steps, NORM_STEPS * done + 1)
                dve.reciprocal(over_sum[:], numerator[:, :, :, B_DIM]).then_inc(norm_steps, 1)
                dve.wait_ge(norm_steps, NORM_STEPS * done + 2)
                dve.tensor_tensor(
                    out[:, TT * c : TT * c + TT, :, :], numerator[:, :, :, 0:B_DIM],
                    over_sum[:].rearrange("p t (h a) -> p t h a", a=1).broadcast_to([P, TT, 2, B_DIM]), ALU.mult,
                ).then_inc(chunk_out, 1)

            def at(e, g, u):
                if u < UNITS and not is_last(g):
                    for n in pieces_at(u):
                        take_piece(g + 1, n)
                    if u == PIECE_TO - 1:
                        finish_peaks(g + 1)
                for c, end in enumerate(ends):
                    if u == end + LAG:
                        copy_sums(g, c)
                    if u == end + LAG + TURN_LAG:
                        normalise(e, g, c)

            for_pairs(dve, at)


def project_context(nc, context, x_in, x_out, w):
    with ExitStack() as ctx:
        def sbuf(name, shape, dt=fp32):
            return ctx.enter_context(nc.sbuf_tensor(f"{name}_o", shape, dt))

        def sem(name):
            return ctx.enter_context(nc.semaphore(f"{name}_o"))

        wo = Split(sbuf, "Wo", [P, KT, D])
        identity = sbuf("identity", [P, P])
        load_weights(nc, [("Wo", w["Wo"].rearrange("(k p) n -> p k n", p=P), wo)], [(identity[:], w["identity"])])
        mixed = [sbuf(f"mixed{e}", [P, TT, D]) for e in range(2)]
        result = [sbuf(f"result{e}", [P, TT, D]) for e in range(2)]
        mixedT = Split(sbuf, "mixedT", [P, KT, CHUNK])
        banks = ctx.enter_context(nc.psum_tensor("banks_o", [P, BANKS, CHUNK], fp32))
        bank_filled, high_ready, bank_drained = sem("bank_filled"), sem("high_ready"), sem("bank_drained")
        context_loaded = [sem(f"context_loaded{e}") for e in range(2)]
        residual_loaded = [sem(f"residual_loaded{e}") for e in range(2)]
        stored = [sem(f"stored{e}") for e in range(2)]
        X0, OUT0, TILES = 0, 4, 8
        block = ctx.enter_context(nc.Block())
        ROUNDS = CHUNKS // 2
        ROUNDS_PER_SEQUENCE = ROUNDS // BATCH

        @block.sync
        def _(sp):
            with sp.Fori(0, BATCH) as b:
                with sp.Fori(0, ROUNDS_PER_SEQUENCE) as c:
                    r = b * ROUNDS_PER_SEQUENCE + c
                    for e in range(2):
                        sp.wait_ge(bank_filled, TILES * 2 * r)
                        for t in range(TT):
                            sp.dma_start(
                                mixed[e][:, t, :].rearrange("p (g c) -> p g c", c=PAIR_DIM),
                                context[
                                    bass.ds(b * HEAD_PAIRS, HEAD_PAIRS), bass.ds(c * 2 * CHUNK + e * CHUNK + t * P, P), :
                                ].rearrange("g p c -> p g c"),
                            ).then_inc(context_loaded[e], 16)
                        sp.wait_ge(stored[e], 16 * r)
                        sp.dma_start(
                            result[e][:], x_in[bass.ds(r * 2 * CHUNK + e * CHUNK, CHUNK), :].rearrange("(t p) d -> p t d", p=P)
                        ).then_inc(residual_loaded[e], 16)

        @block.gpsimd
        def _(pool):
            with pool.Fori(0, ROUNDS) as r:
                for e in range(2):
                    pool.wait_ge(bank_drained, TILES * 2 * r + TILES * (e + 1))
                    pool.dma_start(
                        x_out[bass.ds(r * 2 * CHUNK + e * CHUNK, CHUNK), :].rearrange("(t p) d -> p t d", p=P), result[e][:]
                    ).then_inc(stored[e], 16)
            for e in range(2):
                pool.wait_ge(stored[e], 16 * ROUNDS)

        @block.tensor
        def _(pe):
            with pe.Fori(0, ROUNDS) as r:
                for e in range(2):
                    at = r * (2 * TILES) + e * TILES
                    pe.wait_ge(context_loaded[e], 16 * TT * (r + 1))
                    for k in range(KT):
                        pe.wait_ge(bank_drained, at)
                        turn(pe, banks[:, X0 + k, :], mixed[e], tile(k), identity).then_inc(bank_filled, 1)
                    for t in range(TT):
                        pe.wait_ge(bank_drained, at + KT)
                        for k in range(KT):
                            last = product(
                                pe, banks[:, OUT0 + t, :], mixedT, wo, (slice(None), k, tile(t)), (slice(None), k),
                                k == 0, k == KT - 1,
                            )
                        last.then_inc(bank_filled, 1)

        @block.scalar
        def _(act):
            with act.Fori(0, ROUNDS) as r:
                for e in range(2):
                    for k in range(KT):
                        act.wait_ge(bank_filled, r * (2 * TILES) + e * TILES + k + 1)
                        act.activation(mixedT.high[:, k, :], banks[:, X0 + k, :], ACT.Copy).then_inc(high_ready, 1)

        @block.vector
        def _(dve):
            with dve.Fori(0, ROUNDS) as r:
                for e in range(2):
                    for k in range(KT):
                        dve.wait_ge(high_ready, r * (2 * KT) + e * KT + k + 1)
                        dve.tensor_tensor(
                            mixedT.low[:, k, :], banks[:, X0 + k, :], mixedT.high[:, k, :].bitcast(fp32), ALU.subtract
                        ).then_inc(bank_drained, 1)
                    dve.wait_ge(residual_loaded[e], 16 * (r + 1))
                    for t in range(TT):
                        dve.wait_ge(bank_filled, r * (2 * TILES) + e * TILES + OUT0 + t + 1)
                        dve.tensor_tensor(
                            result[e][:, t, :], banks[:, OUT0 + t, :], result[e][:, t, :], ALU.add
                        ).then_inc(bank_drained, 1)


def hybrid_block(nc, w, x, out):
    def scratch(name, shape):
        return nc.dram_tensor(name, shape, fp32, kind="Internal").ap()

    x1, x2, x3 = (scratch(n, [TOKENS, D]) for n in ("x1", "x2", "x3"))
    qT, kT = (scratch(n, [2, BATCH * D, T]) for n in ("qT", "kT"))
    v, later, context = (scratch(n, [BATCH * HEAD_PAIRS, T, PAIR_DIM]) for n in ("v", "later", "context"))
    conv_attention(nc, x, x1, w)
    routed_experts(nc, x1, x2, w, "e1")
    project_qkv(nc, x2, qT, kT, v, w)
    sum_later_values(nc, v, later, w)
    causal_product_attention(nc, qT, kT, v, later, context, w)
    project_context(nc, context, x2, x3, w)
    routed_experts(nc, x3, out, w, "e2")


def kernel(**inputs):
    import numpy as np
    import concourse.bacc as bacc
    from concourse.bass_utils import run_bass_kernel_spmd

    a = {n: np.asarray(x) for n, x in inputs.items()}
    one = np.float32(1)
    arrays = {
        "x": a["L0_attn_a_x"].reshape(TOKENS, D),
        "conv_w": a["L0_attn_a_conv_w"],
        "conv_b": a["L0_attn_a_conv_b"].reshape(3, A_WIDTH).T,
        "wq": a["L0_attn_a_wq"].reshape(A_WIDTH, D),
        "wk": a["L0_attn_a_wk"].reshape(A_WIDTH, D),
        "wv": a["L0_attn_a_wv"].reshape(A_WIDTH, D),
        "bq": a["L0_attn_a_bq"].reshape(PAIRS, P).T,
        "bk": a["L0_attn_a_bk"].reshape(PAIRS, P).T,
        "bv": a["L0_attn_a_bv"].reshape(PAIRS, P).T,
        "wo": a["L0_attn_a_wo"].reshape(D, A_WIDTH),
        "bo": a["L0_attn_a_bo"].reshape(A_WIDTH, 1),
        "proj_w": a["L0_attn_a_proj_w"],
        "proj_b": a["L0_attn_a_proj_b"].reshape(1, D),
        "Wq": a["L0_attn_b_Wq"], "Wk": a["L0_attn_b_Wk"], "Wv": a["L0_attn_b_Wv"], "Wo": a["L0_attn_b_Wo"],
        "down": a["L0_ffn_A"].reshape(EXPERTS * RANK, D).T,
        "up": a["L0_ffn_B"].transpose(0, 2, 1).reshape(EXPERTS * RANK, D),
        "router": a["L0_ffn_Wr"].T,
        "router_b": a["L0_ffn_br"].reshape(1, EXPERTS),
        "identity": np.eye(P, dtype=np.float32),
        "causal": np.triu(np.full((P, P), -1e9 / A_SCALE, np.float32), 1),
        "keep": np.tile((np.arange(CHUNKS) % (T // CHUNK) > 0).astype(np.float32), (P, 1)),
        "expert_rank": np.arange(EXPERTS, 0, -1, dtype=np.float32).reshape(1, EXPERTS),
        "upto": np.tril(np.full((P, P), one)),
        "since": np.triu(np.full((P, P), one)),
        "after": np.tril(np.full((P, P), one), -1),
        "later_counts": (T - 1 - np.arange(T, dtype=np.float32)).reshape(TQ, P).T,
    }
    arrays = {n: np.ascontiguousarray(x) for n, x in arrays.items()}
    nc = bacc.Bacc("TRN2", target_bir_lowering=False, num_devices=1)
    dram = {n: nc.dram_tensor(n, x.shape, mybir.dt.from_np(x.dtype), kind="ExternalInput").ap() for n, x in arrays.items()}
    out = nc.dram_tensor("out", [TOKENS, D], fp32, kind="ExternalOutput").ap()
    hybrid_block(nc, dram, dram["x"], out)
    got = run_bass_kernel_spmd(nc, [arrays], core_ids=[0])
    return got.results[0]["out"].reshape(BATCH, T, D)
```

```python
import concourse.bass as bass
from concourse import mybir
from contextlib import ExitStack

fp32 = mybir.dt.float32
f32r = mybir.dt.float32r
ALU = mybir.AluOpType
ACT = mybir.ActivationFunctionType
AX = mybir.AxisListType

P = 128
D = 512
KT = D // P
TOKENS = 4096
BATCH = 2
T = TOKENS // BATCH
CHUNK = 512
TT = CHUNK // P
CHUNKS = TOKENS // CHUNK
EPS = 1e-5
TAPS = 3
HALO = TAPS - 1
A_HEADS, A_DIM, A_WIDTH = 8, 64, 128
PAIRS = A_HEADS // 2
A_SCALE = A_DIM ** -0.5
EXPERTS, RANK = 8, 64
B_HEADS, B_DIM = 16, 32
TQ = T // P
B_SCALE = T ** -0.5
BANKS = 8
BIG = 3.0e38


class Split:

    def __init__(self, new, name, shape):
        self.high = new(name + "_high", shape, f32r)
        self.low = new(name + "_low", shape, f32r)


def product(pe, out, stationary, moving, at, mv, first, last):
    pe.matmul(out, stationary.high[at], moving.high[mv], start=first, stop=False)
    pe.matmul(out, stationary.low[at], moving.high[mv], start=False, stop=False)
    return pe.matmul(out, stationary.high[at], moving.low[mv], start=False, stop=last)


class Weights:

    def __init__(self, sem, parts, tag):
        self.parts = parts
        self.arrived = [sem(f"weight{n}_arrived_{tag}") for n in range(len(parts))]
        self.high_ready = sem(f"weight_high_ready_{tag}")
        self.ready = sem(f"weight_ready_{tag}")

    def load(self, engine, n):
        _, view, staged = self.parts[n]
        engine.dma_start(staged, view).then_inc(self.arrived[n], 16)

    def write_high(self, act, n):
        split, _, staged = self.parts[n]
        act.wait_ge(self.arrived[n], 16)
        act.activation(split.high[:], staged, ACT.Copy).then_inc(self.high_ready, 1)

    def write_low(self, dve, n):
        split, _, staged = self.parts[n]
        dve.wait_ge(self.high_ready, n + 1)
        dve.tensor_tensor(split.low[:], staged, split.high[:].bitcast(fp32), ALU.subtract).then_inc(self.ready, 1)

    def wait(self, engine, n):
        engine.wait_ge(self.ready, n + 1)


def load_weights(nc, weights, others=()):
    with ExitStack() as ctx:
        raw = [ctx.enter_context(nc.sbuf_tensor(f"{n}_raw", list(s.high.shape), fp32)) for n, _, s in weights]
        arrived = [ctx.enter_context(nc.semaphore(f"{n}_arrived")) for n, _, _ in weights]
        others_in = ctx.enter_context(nc.semaphore("others_in"))
        weight_high = ctx.enter_context(nc.semaphore("weight_high"))
        block = ctx.enter_context(nc.Block())

        @block.sync
        def _(sp):
            for (_, view, _), tile, sem in zip(weights, raw, arrived):
                sp.dma_start(tile[:], view).then_inc(sem, 16)
            for tile, view in others:
                sp.dma_start(tile, view).then_inc(others_in, 16)
            if others:
                sp.wait_ge(others_in, 16 * len(others))

        @block.scalar
        def _(act):
            for (_, _, split), tile, sem in zip(weights, raw, arrived):
                act.wait_ge(sem, 16)
                act.activation(split.high[:], tile[:], ACT.Copy).then_inc(weight_high, 1)

        @block.vector
        def _(dve):
            for n, ((_, _, split), tile) in enumerate(zip(weights, raw)):
                dve.wait_ge(weight_high, n + 1)
                dve.tensor_tensor(split.low[:], tile[:], split.high[:].bitcast(fp32), ALU.subtract)



def wait_for(engine, semaphore, value):
    if not isinstance(value, int) or value > 0:
        engine.wait_ge(semaphore, value)


class Norm:

    def __init__(self, nc, ctx, tag):
        def sbuf(name, shape):
            return ctx.enter_context(nc.sbuf_tensor(f"{name}_{tag}", shape, fp32))

        def sem(name):
            return ctx.enter_context(nc.semaphore(f"{name}_{tag}"))

        self.x = sbuf("x", [P, TT, D])
        self.xn = sbuf("xn", [P, TT, D])
        self.stats = sbuf("stats", [P, TT, 6])
        self.moments = sbuf("moments", [P, TT, 2])
        self.var_eps = sbuf("var_eps", [P, TT])
        self.rstd = sbuf("rstd", [P, TT])
        self.eps = sbuf("eps", [P, TT])
        self.minus_half = sbuf("minus_half", [P, TT])
        self.x_loaded = sem("x_loaded")
        self.stats_taken = sem("stats_taken")
        self.moments_ready = sem("moments_ready")
        self.norm_steps = sem("norm_steps")
        self.xn_ready = sem("xn_ready")
        self.constants_set = sem("constants_set")

    def load(self, sp, view, i):
        wait_for(sp, self.xn_ready, i)
        sp.dma_start(self.x[:], view[bass.ds(i * CHUNK, CHUNK), :].rearrange("(t p) d -> p t d", p=P)).then_inc(
            self.x_loaded, 16
        )

    def take_moments(self, dve, i):
        dve.wait_ge(self.x_loaded, 16 * (i + 1))
        wait_for(dve, self.xn_ready, i)
        for t in range(TT):
            last = dve.bn_stats(self.stats[:, t, :], self.x[:, t, :])
        last.then_inc(self.stats_taken, 1)
        dve.wait_ge(self.constants_set, 2)
        dve.wait_ge(self.stats_taken, i + 1)
        for t in range(TT):
            last = dve.bn_aggr(self.moments[:, t, :], self.stats[:, t, :])
        last.then_inc(self.moments_ready, 1)

    def set_constants(self, pool):
        pool.memset(self.minus_half[:], -0.5).then_inc(self.constants_set, 1)
        pool.memset(self.eps[:], EPS).then_inc(self.constants_set, 1)
        pool.wait_ge(self.constants_set, 2)

    def apply(self, pool, i):
        pool.wait_ge(self.moments_ready, i + 1)
        pool.tensor_tensor(self.var_eps[:], self.moments[:, :, 1], self.eps[:], ALU.add).then_inc(self.norm_steps, 1)
        pool.tensor_tensor(
            self.xn[:], self.x[:], self.moments[:, :, 0:1].broadcast_to([P, TT, D]), ALU.subtract
        ).then_inc(self.norm_steps, 1)
        pool.wait_ge(self.norm_steps, 3 * i + 1)
        pool.tensor_tensor(self.rstd[:], self.var_eps[:], self.minus_half[:], ALU.pow).then_inc(self.norm_steps, 1)
        pool.wait_ge(self.norm_steps, 3 * i + 3)
        pool.tensor_tensor(
            self.xn[:], self.xn[:], self.rstd[:].rearrange("p (t a) -> p t a", a=1).broadcast_to([P, TT, D]), ALU.mult
        ).then_inc(self.xn_ready, 1)


def all_but_last(engine, body):
    with engine.Fori(0, CHUNKS - 1) as i:
        body(i, False)
    body(CHUNKS - 1, True)


def all_steps(engine, step, peeled=1):
    step(0, False)
    with engine.Fori(1, CHUNKS - peeled) as i:
        step(i, False)
    for i in range(CHUNKS - peeled, CHUNKS):
        step(i, i == CHUNKS - 1)


def norms_more(i):
    return not isinstance(i, int) or i + 2 < CHUNKS


def turn(pe, bank, source, columns, identity):
    for t in range(TT):
        last = pe.transpose(bank[:, t * P : (t + 1) * P], source[:, t, columns], identity[:])
    return last


def tile(n):
    return slice(n * P, (n + 1) * P)


def conv_attention(nc, x_in, x_out, w):
    with ExitStack() as ctx:
        def sbuf(name, shape, dt=fp32):
            return ctx.enter_context(nc.sbuf_tensor(f"{name}_a", shape, dt))

        def sem(name):
            return ctx.enter_context(nc.semaphore(f"{name}_a"))

        conv = [Split(sbuf, f"conv_{n}", [P, TAPS * KT, A_WIDTH]) for n in "qkv"]
        wq, wk, wv = (Split(sbuf, n, [P, D]) for n in ("wq", "wk", "wv"))
        wo = Split(sbuf, "wo", [P, PAIRS, A_WIDTH])
        proj = Split(sbuf, "proj", [P, D])
        identity = sbuf("identity", [P, P])
        causal = sbuf("causal", [P, P])
        conv_b = sbuf("conv_b", [P, 3])
        bq, bk, bv = (sbuf(n, [P, PAIRS]) for n in ("bq", "bk", "bv"))
        bo = sbuf("bo", [P, 1])
        proj_b = sbuf("proj_b", [P, D])
        keep = sbuf("keep", [P, CHUNKS])

        CONVS = ("v", "q", "k")
        of_conv = {"q": 0, "k": 1, "v": 2}
        W_Q, W_K, W_V, W_LAST = 3, 4, 5, 7
        CONSTANTS = [
            (keep[:], w["keep"]), (conv_b[:], w["conv_b"]), (bq[:], w["bq"]), (bk[:], w["bk"]),
            (causal[:], w["causal"]), (bv[:], w["bv"]), (bo[:], w["bo"]), (proj_b[:], w["proj_b"].broadcast_to([P, D])),
        ]

        norm = Norm(nc, ctx, "a")
        xT = Split(sbuf, "xT", [P, KT, HALO + CHUNK])
        qkv = [Split(sbuf, n, [P, CHUNK]) for n in ("q", "k", "v")]
        qh = [sbuf(f"qh{e}", [P, CHUNK]) for e in range(2)]
        kh = [sbuf(f"kh{e}", [P, CHUNK]) for e in range(2)]
        vh = sbuf("vh", [P, TT, D])
        masked = [sbuf(f"masked{h}", [P, TT, P]) for h in range(2)]
        peak = [sbuf(f"peak{h}", [P, TT]) for h in range(2)]
        minus_peak = [[sbuf(f"minus_peak{e}{h}", [P, TT]) for h in range(2)] for e in range(2)]
        probs = [[sbuf(f"probs{e}{h}", [P, TT, P]) for h in range(2)] for e in range(2)]
        sums = [[sbuf(f"sums{e}{h}", [P, TT]) for h in range(2)] for e in range(2)]
        over_sums = [[sbuf(f"over_sums{e}{h}", [P, TT]) for h in range(2)] for e in range(2)]
        probsT = [sbuf(f"probsT{h}", [P, CHUNK]) for h in range(2)]
        ctxT = Split(sbuf, "ctxT", [P, PAIRS, CHUNK])
        mixT = Split(sbuf, "mixT", [P, CHUNK])
        result = sbuf("result", [P, TT, D])
        conv_v_staged = sbuf("conv_v_staged", [P, TAPS * KT, A_WIDTH])

        def over_taps(a):
            return a[:, 0:TAPS, :].rearrange("p s (k n) -> p (s k) n", n=A_WIDTH)

        def flat(a):
            return a[:].rearrange("p t s -> p (t s)")

        by_output = w["conv_w"].rearrange("s (k p) n -> p (s k) n", p=P)
        staged = (conv_v_staged[:], over_taps(vh), over_taps(result))
        weights = Weights(sem, [
            *((conv[of_conv[c]], by_output[:, :, tile(of_conv[c])], to) for c, to in zip(CONVS, staged)),
            (wq, w["wq"], flat(probs[0][0])), (wk, w["wk"], flat(probs[0][1])), (wv, w["wv"], flat(probs[1][0])),
            (wo, w["wo"].rearrange("(j p) n -> p j n", p=P), probs[1][1][:]), (proj, w["proj_w"], flat(masked[0])),
        ], "a")
        banks = ctx.enter_context(nc.psum_tensor("banks_a", [P, BANKS, CHUNK], fp32))
        conv_bank = {"v": 6, "q": 7, "k": 6}

        constants_loaded, identity_loaded = sem("constants_loaded"), sem("identity_loaded")
        bank_filled, high_ready = sem("bank_filled"), sem("high_ready")
        drained_by_act, drained_by_dve = sem("drained_by_act"), sem("drained_by_dve")
        conv_filled, conv_high, conv_drained = sem("conv_filled"), sem("conv_high"), sem("conv_drained")
        halo_cleared, halo_high, halo_low = sem("halo_cleared"), sem("halo_high"), sem("halo_low")
        peak_taken, peak_ready = sem("peak_taken"), sem("peak_ready")
        exp_done, sums_inverted, probs_ready = sem("exp_done"), sem("sums_inverted"), sem("probs_ready")
        residual_loaded, residual_ready, stored = sem("residual_loaded"), sem("residual_ready"), sem("stored")

        RING = 6
        before_steps = [("x", k) for k in range(KT)] + [("q", 0), ("k", 0)]

        def tiles_of(last):
            def heads(name, j):
                return [(name, j, 0), (name, j, 1)]

            return (
                heads("s", 0) + ([] if last else [("x", k) for k in range(KT)]) + [("v", t) for t in range(TT)]
                + [("q", 1), ("k", 1)] + heads("s", 1) + heads("t", 0) + [("c", 0)]
                + [("q", 2), ("k", 2)] + heads("s", 2) + heads("t", 1) + [("q", 3), ("k", 3), ("c", 1)]
                + heads("s", 3) + heads("t", 2) + [("c", 2)] + heads("t", 3) + [("c", 3), ("mix", 0), ("mix", 1)]
                + ([] if last else [("q", 0), ("k", 0)]) + [("o", t) for t in range(TT)]
            )

        every_step = tiles_of(False)

        def by_act(name):
            return name[0] in "qkv"

        def by_dve(name):
            return not by_act(name)

        def is_split(name):
            return name[0] in ("x", "c") or name == ("mix", 0)

        class Counts:

            def __init__(self, i, last):
                self.i, self.last = i, last
                self.names = tiles_of(last)
                self.earlier = before_steps if isinstance(i, int) and i == 0 else every_step

            def start(self, kind):
                return sum(map(kind, before_steps)) + sum(map(kind, every_step)) * self.i

            def up_to(self, kind, name):
                return self.start(kind) + sum(map(kind, self.names[: self.names.index(name) + 1]))

            def filled(self, name):
                return self.up_to(bool, name)

            def bank(self, name):
                return banks[:, self.names.index(name) % RING, :]

            def freed(self, kind, n):
                n -= RING
                if n >= 0:
                    return sum(map(kind, self.names[: n + 1]))
                return -sum(map(kind, self.earlier[len(self.earlier) + n + 1 :]))

        block = ctx.enter_context(nc.Block())

        @block.sync
        def _(sp):
            norm.load(sp, x_in, 0)
            sp.dma_start(identity[:], w["identity"]).then_inc(identity_loaded, 16)
            for n in range(len(CONVS)):
                weights.load(sp, n)
            for dst, src in CONSTANTS:
                sp.dma_start(dst, src).then_inc(constants_loaded, 16)
            for n in range(W_Q, W_LAST + 1):
                weights.load(sp, n)
            norm.load(sp, x_in, 1)
            weights.wait(sp, len(CONVS) - 1)

            def step(i, last):
                wait_for(sp, stored, 16 * i)
                sp.dma_start(
                    result[:], x_in[bass.ds(i * CHUNK, CHUNK), :].rearrange("(t p) d -> p t d", p=P)
                ).then_inc(residual_loaded, 16)
                if norms_more(i):
                    norm.load(sp, x_in, i + 2)
                sp.wait_ge(drained_by_dve, Counts(i, last).up_to(by_dve, ("o", TT - 1)))
                sp.dma_start(
                    x_out[bass.ds(i * CHUNK, CHUNK), :].rearrange("(t p) d -> p t d", p=P), result[:]
                ).then_inc(stored, 16)

            all_steps(sp, step, peeled=2)
            sp.wait_ge(stored, 16 * CHUNKS)

        @block.gpsimd
        def _(pool):
            for part in (xT.high, xT.low):
                pool.memset(part[:, :, CHUNK:].bitcast(fp32), 0.0).then_inc(halo_cleared, 1)
            norm.set_constants(pool)
            norm.apply(pool, 0)
            pool.wait_ge(bank_filled, KT)
            norm.apply(pool, 1)
            pool.wait_ge(constants_loaded, 16 * len(CONSTANTS))

            def step(i, last):
                for j in range(PAIRS):
                    for h in range(2):
                        e = j % 2
                        pool.wait_ge(sums_inverted, 2 * PAIRS * i + 2 * j + h + 1)
                        pool.tensor_tensor(
                            probs[e][h][:], probs[e][h][:],
                            over_sums[e][h][:].rearrange("p (t a) -> p t a", a=1).broadcast_to([P, TT, P]), ALU.mult,
                        ).then_inc(probs_ready, 1)
                    if j == 1:
                        pool.wait_ge(residual_loaded, 16 * (i + 1))
                        pool.tensor_tensor(
                            result[:], result[:], proj_b[:].rearrange("p (a d) -> p a d", a=1).broadcast_to([P, TT, D]),
                            ALU.add,
                        ).then_inc(residual_ready, 1)
                if norms_more(i):
                    pool.wait_ge(bank_filled, Counts(i, last).filled(("x", KT - 1)))
                    norm.apply(pool, i + 2)

            all_steps(pool, step, peeled=2)

        @block.tensor
        def _(pe):
            def convolve(c, taps):
                out = banks[:, conv_bank[c], :]
                for s in taps:
                    for k in range(KT):
                        last = product(
                            pe, out, conv[of_conv[c]], xT, (slice(None), s * KT + k),
                            (slice(None), k, slice(s, s + CHUNK)), s == 0 and k == 0, s == TAPS - 1 and k == KT - 1,
                        )
                if s == TAPS - 1:
                    last.then_inc(conv_filled, 1)

            def heads(out, weight, j, of):
                product(pe, out, weight, qkv[of], (slice(None), tile(j)), slice(None), True, True).then_inc(bank_filled, 1)

            pe.wait_ge(identity_loaded, 16)
            pe.wait_ge(norm.xn_ready, 1)
            for k in range(KT):
                turn(pe, banks[:, k, :], norm.xn, tile(k), identity).then_inc(bank_filled, 1)
            pe.wait_ge(drained_by_dve, KT)
            for n, c in enumerate(CONVS):
                weights.wait(pe, n)
                if n == 2:
                    pe.wait_ge(conv_drained, 1)
                convolve(c, range(TAPS))
            weights.wait(pe, W_K)
            pe.wait_ge(conv_drained, len(CONVS))
            heads(banks[:, KT, :], wq, 0, 0)
            heads(banks[:, KT + 1, :], wk, 0, 1)
            weights.wait(pe, W_LAST)

            def step(i, last):
                counts = Counts(i, last)
                awaited = {}

                def await_drained(kind, count):
                    if count > awaited.get(kind, -RING - 1):
                        awaited[kind] = count
                        pe.wait_ge(drained_by_act if kind is by_act else drained_by_dve, counts.start(kind) + count)

                def fill(*names):
                    n = counts.names.index(names[-1])
                    await_drained(by_act, counts.freed(by_act, n))
                    await_drained(by_dve, counts.freed(by_dve, n))
                    return [counts.bank(name) for name in names]

                def needs(kind, name):
                    await_drained(kind, sum(map(kind, counts.names[: counts.names.index(name) + 1])))

                def scores(j):
                    if j == 0:
                        await_drained(by_act, 0)
                    else:
                        needs(by_act, ("k", j))
                    for h, out in enumerate(fill(("s", j, 0), ("s", j, 1))):
                        rows = slice(64 * h, 64 * h + 64)
                        for t in range(TT):
                            done = pe.matmul(
                                out[:, tile(t)], qh[j % 2][rows, tile(t)], kh[j % 2][rows, tile(t)], start=True, stop=True
                            )
                        done.then_inc(bank_filled, 1)

                def queries_and_keys(j):
                    outs = fill(("q", j), ("k", j))
                    heads(outs[0], wq, j, 0)
                    heads(outs[1], wk, j, 1)

                def turn_probs(j):
                    outs = fill(("t", j, 0), ("t", j, 1))
                    for h in range(2):
                        pe.wait_ge(probs_ready, 2 * PAIRS * i + 2 * j + h + 1)
                        turn(pe, outs[h], probs[j % 2][h], slice(0, P), identity).then_inc(bank_filled, 1)

                def contexts(j):
                    (out,) = fill(("c", j))
                    needs(by_dve, ("t", j, 1))
                    if j == 0:
                        needs(by_act, ("v", TT - 1))
                    for t in range(TT):
                        for h in range(2):
                            rows = slice(64 * h, 64 * h + 64)
                            done = pe.matmul(
                                out[rows, tile(t)], vh[:, t, j * P + 64 * h : j * P + 64 * h + 64], probsT[h][:, tile(t)],
                                start=True, stop=True,
                            )
                    done.then_inc(bank_filled, 1)

                def convolve_next(c, tap):
                    if last:
                        return
                    if c == "v" and tap == 0:
                        needs(by_dve, ("x", KT - 1))
                    if c == "k" and tap == 0:
                        pe.wait_ge(conv_drained, len(CONVS) * (i + 1) + 1)
                    convolve(c, [tap])

                scores(0)
                if not last:
                    pe.wait_ge(norm.xn_ready, i + 2)
                    for k in range(KT):
                        turn(pe, fill(("x", k))[0], norm.xn, tile(k), identity).then_inc(bank_filled, 1)
                for t in range(TT):
                    (out,) = fill(("v", t))
                    product(pe, out, qkv[2], wv, (slice(None), tile(t)), slice(None), True, True).then_inc(bank_filled, 1)
                queries_and_keys(1)
                convolve_next("v", 0)
                scores(1)
                convolve_next("v", 1)
                turn_probs(0)
                convolve_next("v", 2)
                contexts(0)
                queries_and_keys(2)
                convolve_next("q", 0)
                scores(2)
                turn_probs(1)
                queries_and_keys(3)
                convolve_next("q", 1)
                contexts(1)
                scores(3)
                convolve_next("q", 2)
                turn_probs(2)
                convolve_next("k", 0)
                contexts(2)
                convolve_next("k", 1)
                turn_probs(3)
                convolve_next("k", 2)
                contexts(3)
                out, _ = fill(("mix", 0), ("mix", 1))
                for j in range(PAIRS):
                    if j == PAIRS - 1:
                        needs(by_dve, ("c", j))
                    elif j == 0:
                        needs(by_dve, ("c", PAIRS - 2))
                    done = product(pe, out, wo, ctxT, (slice(None), j), (slice(None), j), j == 0, j == PAIRS - 1)
                done.then_inc(bank_filled, 2)
                if not last:
                    pe.wait_ge(conv_drained, len(CONVS) * (i + 2))
                    queries_and_keys(0)
                needs(by_dve, ("mix", 1))
                for t in range(TT):
                    (out,) = fill(("o", t))
                    product(pe, out, mixT, proj, (slice(None), tile(t)), slice(None), True, True).then_inc(bank_filled, 1)

            all_steps(pe, step)

        @block.scalar
        def _(act):
            act.wait_ge(halo_cleared, 2)
            act.wait_ge(constants_loaded, 16 * len(CONSTANTS))

            def turned_high(chunk, filled, bank):
                act.activation(
                    xT.high[:, :, 0:HALO], xT.high[:, :, CHUNK:].bitcast(fp32), ACT.Copy, scale=keep[:, bass.ds(chunk, 1)]
                ).then_inc(halo_high, 1)
                act.wait_ge(halo_high, chunk + 1)
                for k in range(KT):
                    act.wait_ge(bank_filled, filled(k))
                    act.activation(xT.high[:, k, HALO:], bank(k), ACT.Copy).then_inc(high_ready, 1)

            def conv_to_high(c, chunk):
                of = of_conv[c]
                act.wait_ge(conv_filled, len(CONVS) * chunk + CONVS.index(c) + 1)
                act.activation(
                    qkv[of].high[:], banks[:, conv_bank[c], :], ACT.Identity, bias=conv_b[:, of : of + 1]
                ).then_inc(conv_high, 1)

            def drain(filled, out, bank, bias=None):
                act.wait_ge(bank_filled, filled)
                if bias is None:
                    act.activation(out, bank, ACT.Copy).then_inc(drained_by_act, 1)
                else:
                    act.activation(out, bank, ACT.Identity, bias=bias).then_inc(drained_by_act, 1)

            turned_high(0, lambda k: k + 1, lambda k: banks[:, k, :])
            for n, c in enumerate(CONVS):
                weights.write_high(act, n)
            conv_to_high("v", 0)
            for n in range(W_Q, W_LAST + 1):
                weights.write_high(act, n)
            conv_to_high("q", 0)
            conv_to_high("k", 0)
            drain(KT + 1, qh[0][:], banks[:, KT, :], bq[:, 0:1])
            drain(KT + 2, kh[0][:], banks[:, KT + 1, :], bk[:, 0:1])

            def step(i, last):
                counts = Counts(i, last)

                def queries_and_keys(j):
                    drain(counts.filled(("q", j)), qh[j % 2][:], counts.bank(("q", j)), bq[:, j : j + 1])
                    drain(counts.filled(("k", j)), kh[j % 2][:], counts.bank(("k", j)), bk[:, j : j + 1])

                def exponentials(j):
                    e = j % 2
                    for h in range(2):
                        act.wait_ge(peak_ready, 2 * PAIRS * i + 2 * j + h + 1)
                        for t in range(TT):
                            done = act.activation(
                                probs[e][h][:, t, :], masked[h][:, t, :], ACT.Exp, bias=minus_peak[e][h][:, t : t + 1],
                                scale=A_SCALE, accum_out=sums[e][h][:, t : t + 1],
                            )
                        done.then_inc(exp_done, 1)

                def contexts_high(j):
                    act.wait_ge(bank_filled, counts.filled(("c", j)))
                    act.activation(
                        ctxT.high[:, j, :], counts.bank(("c", j)), ACT.Identity, bias=bv[:, j : j + 1]
                    ).then_inc(high_ready, 1)

                def conv_next(c):
                    if not last:
                        conv_to_high(c, i + 1)

                if not last:
                    turned_high(i + 1, lambda k: counts.filled(("x", k)), lambda k: counts.bank(("x", k)))
                exponentials(0)
                for t in range(TT):
                    drain(counts.filled(("v", t)), vh[:, t, :], counts.bank(("v", t)))
                queries_and_keys(1)
                exponentials(1)
                conv_next("v")
                contexts_high(0)
                queries_and_keys(2)
                queries_and_keys(3)
                exponentials(2)
                contexts_high(1)
                conv_next("q")
                exponentials(3)
                contexts_high(2)
                conv_next("k")
                contexts_high(3)
                act.wait_ge(bank_filled, counts.filled(("mix", 1)))
                act.activation(mixT.high[:], counts.bank(("mix", 0)), ACT.Identity, bias=bo[:, 0:1]).then_inc(high_ready, 1)
                if not last:
                    queries_and_keys(0)

            all_steps(act, step)

        @block.vector
        def _(dve):
            dve.wait_ge(halo_cleared, 2)
            norm.take_moments(dve, 0)
            dve.wait_ge(constants_loaded, 16 * len(CONSTANTS))

            def turned_low(chunk, high, bank):
                dve.tensor_scalar(
                    xT.low[:, :, 0:HALO], xT.low[:, :, CHUNK:].bitcast(fp32), keep[:, bass.ds(chunk, 1)], None, ALU.mult
                ).then_inc(halo_low, 1)
                dve.wait_ge(halo_low, chunk + 1)
                for k in range(KT):
                    dve.wait_ge(high_ready, high(k))
                    dve.tensor_tensor(
                        xT.low[:, k, HALO:], bank(k), xT.high[:, k, HALO:].bitcast(fp32), ALU.subtract
                    ).then_inc(drained_by_dve, 1)

            def less_high(out, bank, bias, high, done, by=1):
                dve.scalar_tensor_tensor(
                    out=out, in0=bank, scalar=bias, in1=high.bitcast(fp32), op0=ALU.add, op1=ALU.subtract
                ).then_inc(done, by)

            def conv_to_low(c, chunk):
                of = of_conv[c]
                dve.wait_ge(conv_high, len(CONVS) * chunk + CONVS.index(c) + 1)
                less_high(qkv[of].low[:], banks[:, conv_bank[c], :], conv_b[:, of : of + 1], qkv[of].high[:], conv_drained)

            turned_low(0, lambda k: k + 1, lambda k: banks[:, k, :])
            for n, c in enumerate(CONVS):
                weights.write_low(dve, n)
            conv_to_low("v", 0)
            norm.take_moments(dve, 1)
            for n in range(W_Q, W_LAST + 1):
                weights.write_low(dve, n)
            conv_to_low("q", 0)
            conv_to_low("k", 0)

            def step(i, last):
                counts = Counts(i, last)

                def mask_scores(j):
                    for h in range(2):
                        n = 2 * PAIRS * i + 2 * j + h + 1
                        dve.wait_ge(bank_filled, counts.filled(("s", j, h)))
                        dve.tensor_tensor(
                            masked[h][:], counts.bank(("s", j, h)).rearrange("p (t s) -> p t s", s=P),
                            causal[:].rearrange("p (a s) -> p a s", a=1).broadcast_to([P, TT, P]), ALU.add,
                        ).then_inc(drained_by_dve, 1)
                        dve.wait_ge(drained_by_dve, counts.up_to(by_dve, ("s", j, h)))
                        dve.tensor_reduce(peak[h][:], masked[h][:], AX.X, ALU.max).then_inc(peak_taken, 1)
                        dve.wait_ge(peak_taken, n)
                        dve.tensor_scalar(minus_peak[j % 2][h][:], peak[h][:], -A_SCALE, None, ALU.mult).then_inc(peak_ready, 1)

                def invert_sums(j):
                    for h in range(2):
                        dve.wait_ge(exp_done, 2 * PAIRS * i + 2 * j + h + 1)
                        dve.reciprocal(over_sums[j % 2][h][:], sums[j % 2][h][:]).then_inc(sums_inverted, 1)

                def copy_probs(j):
                    for h in range(2):
                        dve.wait_ge(bank_filled, counts.filled(("t", j, h)))
                        dve.tensor_copy(probsT[h][:], counts.bank(("t", j, h))).then_inc(drained_by_dve, 1)

                def contexts_low(j):
                    dve.wait_ge(high_ready, counts.up_to(is_split, ("c", j)))
                    less_high(ctxT.low[:, j, :], counts.bank(("c", j)), bv[:, j : j + 1], ctxT.high[:, j, :], drained_by_dve)

                def conv_next(c):
                    if not last:
                        conv_to_low(c, i + 1)

                mask_scores(0)
                if not last:
                    turned_low(i + 1, lambda k: counts.up_to(is_split, ("x", k)), lambda k: counts.bank(("x", k)))
                invert_sums(0)
                mask_scores(1)
                copy_probs(0)
                invert_sums(1)
                conv_next("v")
                contexts_low(0)
                if norms_more(i):
                    norm.take_moments(dve, i + 2)
                mask_scores(2)
                copy_probs(1)
                invert_sums(2)
                contexts_low(1)
                mask_scores(3)
                conv_next("q")
                copy_probs(2)
                invert_sums(3)
                contexts_low(2)
                copy_probs(3)
                conv_next("k")
                contexts_low(3)
                dve.wait_ge(high_ready, counts.up_to(is_split, ("mix", 0)))
                less_high(mixT.low[:], counts.bank(("mix", 0)), bo[:, 0:1], mixT.high[:], drained_by_dve, by=2)
                dve.wait_ge(residual_ready, i + 1)
                for t in range(TT):
                    dve.wait_ge(bank_filled, counts.filled(("o", t)))
                    dve.tensor_tensor(result[:, t, :], counts.bank(("o", t)), result[:, t, :], ALU.add).then_inc(drained_by_dve, 1)

            all_steps(dve, step, peeled=2)


class Experts:

    def __init__(self, nc, ctx, w):
        def sbuf(name, shape, dt=fp32):
            return ctx.enter_context(nc.sbuf_tensor(f"{name}_e", shape, dt))

        def sem(name):
            return ctx.enter_context(nc.semaphore(f"{name}_e"))

        self.down = Split(sbuf, "down", [P, KT, EXPERTS * RANK])
        self.up = Split(sbuf, "up", [P, EXPERTS * RANK // P, D])
        self.router = sbuf("router", [P, KT, 2, EXPERTS], f32r)
        router = Split(lambda name, shape, dt: self.router[:, :, int(name.endswith("low")), :], "router", None)
        self.identity = sbuf("identity", [P, P])
        self.router_b = sbuf("router_b", [P, EXPERTS])
        self.rank = sbuf("rank", [P, EXPERTS])
        self.constants = [
            (self.identity[:], w["identity"]), (self.router_b[:], w["router_b"].broadcast_to([P, EXPERTS])),
            (self.rank[:], w["expert_rank"].broadcast_to([P, EXPERTS])),
        ]
        self.constants_loaded = sem("constants_loaded")
        self.weights = Weights(sem, [
            (router, w["router"].rearrange("(k p) n -> p k n", p=P), sbuf("router_staged", [P, KT, EXPERTS])[:]),
            (self.down, w["down"].rearrange("(k p) n -> p k n", p=P), sbuf("down_staged", [P, KT, EXPERTS * RANK])[:]),
            (self.up, w["up"].rearrange("(k p) n -> p k n", p=P), sbuf("up_staged", [P, KT, D])[:]),
        ], "e")


def routed_experts(nc, x_in, x_out, experts, tag, load_experts):
    with ExitStack() as ctx:
        def sbuf(name, shape, dt=fp32):
            return ctx.enter_context(nc.sbuf_tensor(f"{name}_{tag}", shape, dt))

        def sem(name):
            return ctx.enter_context(nc.semaphore(f"{name}_{tag}"))

        norm = Norm(nc, ctx, tag)
        xT = Split(sbuf, "xT", [P, KT, CHUNK])
        logits = [sbuf(f"logits{n}", [P, TT, EXPERTS]) for n in range(2)]
        peak = sbuf("peak", [P, TT])
        shifted = sbuf("shifted", [P, TT, EXPERTS])
        exps = sbuf("exps", [P, TT, EXPERTS])
        total = sbuf("total", [P, TT])
        weight = sbuf("weight", [P, TT])
        ranked = sbuf("ranked", [P, TT, EXPERTS])
        first = sbuf("first", [P, TT])
        chosen = sbuf("chosen", [P, TT, EXPERTS])
        gate = sbuf("gate", [P, TT, EXPERTS])
        hidden = sbuf("hidden", [P, TT, EXPERTS * RANK])
        hiddenT = Split(sbuf, "hiddenT", [P, KT, CHUNK])
        result = sbuf("result", [P, TT, D])
        banks = ctx.enter_context(nc.psum_tensor(f"banks_{tag}", [P, BANKS, CHUNK], fp32))
        bank_filled, high_ready, bank_drained = sem("bank_filled"), sem("high_ready"), sem("bank_drained")
        router_filled, gate_steps, exp_done = sem("router_filled"), sem("gate_steps"), sem("exp_done")
        residual_loaded, stored = sem("residual_loaded"), sem("stored")
        X_BANKS, HT_BANKS, OUT_BANKS, H_BANKS, LOGITS = (0, 1, 2, 3), (4, 5, 6, 0), (1, 2, 3, 1), (4, 5, 6, 4), 7
        BEFORE, TILES = 2 * KT, 4 * KT
        GATE_STEPS = 10

        def over_experts(a):
            return a.rearrange("p (t a) -> p t a", a=1).broadcast_to([P, TT, EXPERTS])

        def over_tiles(a):
            return a.rearrange("p (a e) -> p a e", a=1).broadcast_to([P, TT, EXPERTS])

        def firsts(i, last):
            start = BEFORE + TILES * i
            turned = 0 if last else KT
            return start, start + turned, start + turned + KT, start + turned + KT + TT

        def highs(i, last):
            return KT + 2 * KT * i, KT + 2 * KT * i + (0 if last else KT)

        block = ctx.enter_context(nc.Block())

        @block.sync
        def _(sp):
            norm.load(sp, x_in, 0)
            if load_experts:
                for dst, src in experts.constants:
                    sp.dma_start(dst, src).then_inc(experts.constants_loaded, 16)
                for n in range(3):
                    experts.weights.load(sp, n)
            for i in range(1, 3):
                norm.load(sp, x_in, i)

            def step(i, last):
                wait_for(sp, stored, 16 * i)
                sp.dma_start(
                    result[:], x_in[bass.ds(i * CHUNK, CHUNK), :].rearrange("(t p) d -> p t d", p=P)
                ).then_inc(residual_loaded, 16)
                if not isinstance(i, int) or i + 3 < CHUNKS:
                    norm.load(sp, x_in, i + 3)
                sp.wait_ge(bank_drained, firsts(i, last)[2] + TT)
                sp.dma_start(
                    x_out[bass.ds(i * CHUNK, CHUNK), :].rearrange("(t p) d -> p t d", p=P), result[:]
                ).then_inc(stored, 16)

            all_steps(sp, step, peeled=3)
            sp.wait_ge(stored, 16 * CHUNKS)

        @block.gpsimd
        def _(pool):
            norm.set_constants(pool)
            norm.apply(pool, 0)
            pool.wait_ge(bank_filled, KT)
            norm.apply(pool, 1)

            def step(i, last):
                if norms_more(i):
                    pool.wait_ge(bank_filled, firsts(i, last)[0] + KT)
                    norm.apply(pool, i + 2)

            all_steps(pool, step, peeled=2)

        @block.tensor
        def _(pe):
            def turn_x():
                for k in range(KT):
                    turn(pe, banks[:, X_BANKS[k], :], norm.xn, tile(k), experts.identity).then_inc(bank_filled, 1)

            def route():
                for t in range(TT):
                    out = banks[:, LOGITS, t * 2 * EXPERTS : (t + 1) * 2 * EXPERTS]
                    for k in range(KT):
                        for part in (xT.high, xT.low):
                            last = pe.matmul(
                                out, part[:, k, tile(t)], experts.router[:, k, :, :].rearrange("p s e -> p (s e)"),
                                start=k == 0 and part is xT.high, stop=k == KT - 1 and part is xT.low,
                            )
                last.then_inc(router_filled, 1)

            def four_tiles(bank_of, left, right, reused):
                for t in range(TT):
                    if t == TT - 1:
                        pe.wait_ge(bank_drained, reused)
                    for k in range(KT):
                        last = product(
                            pe, banks[:, bank_of[t], :], left, right, (slice(None), k, tile(t)), (slice(None), k),
                            k == 0, k == KT - 1,
                        )
                    last.then_inc(bank_filled, 1)

            pe.wait_ge(experts.constants_loaded, 16 * len(experts.constants))
            pe.wait_ge(norm.xn_ready, 1)
            turn_x()
            if load_experts:
                experts.weights.wait(pe, 0)
            pe.wait_ge(bank_drained, KT)
            route()
            if load_experts:
                experts.weights.wait(pe, 1)
            four_tiles(H_BANKS, xT, experts.down, KT + 1)
            if load_experts:
                experts.weights.wait(pe, 2)

            def step(i, last):
                start, back, out, ahead = firsts(i, last)
                if not last:
                    pe.wait_ge(norm.xn_ready, i + 2)
                    pe.wait_ge(bank_drained, start - KT)
                    turn_x()
                pe.wait_ge(bank_drained, start)
                for k in range(KT):
                    if k == KT - 1 and not last:
                        pe.wait_ge(bank_drained, start + 1)
                    turn(pe, banks[:, HT_BANKS[k], :], hidden, tile(k), experts.identity).then_inc(bank_filled, 1)
                if not last:
                    pe.wait_ge(bank_drained, start + KT)
                    route()
                pe.wait_ge(bank_drained, out)
                four_tiles(OUT_BANKS, hiddenT, experts.up, out + 1)
                if not last:
                    four_tiles(H_BANKS, xT, experts.down, ahead + 1)

            all_steps(pe, step)

        @block.scalar
        def _(act):
            def high(n, bank, out):
                act.wait_ge(bank_filled, n + 1)
                act.activation(out, banks[:, bank, :], ACT.Copy).then_inc(high_ready, 1)

            def exponentials(chunk):
                act.wait_ge(gate_steps, GATE_STEPS * chunk + 4)
                act.activation(exps[:], shifted[:], ACT.Exp).then_inc(exp_done, 1)

            for k in range(KT):
                high(k, X_BANKS[k], xT.high[:, k, :])
            if load_experts:
                for n in range(3):
                    experts.weights.write_high(act, n)
            exponentials(0)

            def step(i, last):
                start, back, _, _ = firsts(i, last)
                if not last:
                    for k in range(KT):
                        high(start + k, X_BANKS[k], xT.high[:, k, :])
                for k in range(KT):
                    high(back + k, HT_BANKS[k], hiddenT.high[:, k, :])
                if not last:
                    exponentials(i + 1)

            all_steps(act, step)

        @block.vector
        def _(dve):
            def low(n, bank, split, k):
                dve.wait_ge(high_ready, n + 1)
                dve.tensor_tensor(
                    split.low[:, k, :], banks[:, bank, :], split.high[:, k, :].bitcast(fp32), ALU.subtract
                ).then_inc(bank_drained, 1)

            def take_gate(chunk):
                at = GATE_STEPS * chunk
                both = banks[:, LOGITS, 0 : TT * 2 * EXPERTS].rearrange("p (t s e) -> p t s e", s=2, e=EXPERTS)
                dve.wait_ge(router_filled, chunk + 1)
                dve.tensor_tensor(logits[0][:], both[:, :, 1, :], over_tiles(experts.router_b[:]), ALU.add).then_inc(gate_steps, 1)
                dve.wait_ge(gate_steps, at + 1)
                dve.tensor_tensor(logits[1][:], both[:, :, 0, :], logits[0][:], ALU.add).then_inc(gate_steps, 1)
                dve.wait_ge(gate_steps, at + 2)
                dve.tensor_reduce(peak[:], logits[1][:], AX.X, ALU.max).then_inc(gate_steps, 1)
                dve.wait_ge(gate_steps, at + 3)
                dve.tensor_tensor(shifted[:], logits[1][:], over_experts(peak[:]), ALU.subtract).then_inc(gate_steps, 1)
                dve.wait_ge(gate_steps, at + 4)
                dve.scalar_tensor_tensor(
                    out=ranked[:], in0=shifted[:], scalar=0.0, in1=over_tiles(experts.rank[:]), op0=ALU.is_ge, op1=ALU.mult
                ).then_inc(gate_steps, 1)
                dve.wait_ge(gate_steps, at + 5)
                dve.tensor_reduce(first[:], ranked[:], AX.X, ALU.max).then_inc(gate_steps, 1)
                dve.wait_ge(gate_steps, at + 6)
                dve.tensor_tensor(chosen[:], ranked[:], over_experts(first[:]), ALU.is_equal).then_inc(gate_steps, 1)
                dve.wait_ge(exp_done, chunk + 1)
                dve.tensor_reduce(total[:], exps[:], AX.X, ALU.add).then_inc(gate_steps, 1)
                dve.wait_ge(gate_steps, at + 8)
                dve.reciprocal(weight[:], total[:]).then_inc(gate_steps, 1)
                dve.wait_ge(gate_steps, at + 9)
                dve.scalar_tensor_tensor(
                    out=gate[:], in0=chosen[:], scalar=1.0 / RANK, in1=over_experts(weight[:]), op0=ALU.mult, op1=ALU.mult
                ).then_inc(gate_steps, 1)

            def gate_hidden(chunk, ahead):
                dve.wait_ge(gate_steps, GATE_STEPS * (chunk + 1))
                for t in range(TT):
                    dve.wait_ge(bank_filled, ahead + t + 1)
                    dve.tensor_tensor(
                        hidden[:, t, :].rearrange("p (e r) -> p e r", r=RANK),
                        banks[:, H_BANKS[t], :].rearrange("p (e r) -> p e r", r=RANK),
                        gate[:, t, :].rearrange("p (e a) -> p e a", a=1).broadcast_to([P, EXPERTS, RANK]), ALU.mult,
                    ).then_inc(bank_drained, 1)

            norm.take_moments(dve, 0)
            for k in range(KT):
                low(k, X_BANKS[k], xT, k)
            if load_experts:
                for n in range(3):
                    experts.weights.write_low(dve, n)
            take_gate(0)
            norm.take_moments(dve, 1)
            gate_hidden(0, KT)

            def step(i, last):
                start, back, out, ahead = firsts(i, last)
                high_x, high_back = highs(i, last)
                if not last:
                    for k in range(KT):
                        low(high_x + k, X_BANKS[k], xT, k)
                for k in range(KT):
                    low(high_back + k, HT_BANKS[k], hiddenT, k)
                if norms_more(i):
                    norm.take_moments(dve, i + 2)
                if not last:
                    take_gate(i + 1)
                dve.wait_ge(residual_loaded, 16 * (i + 1))
                for t in range(TT):
                    dve.wait_ge(bank_filled, out + t + 1)
                    dve.tensor_tensor(result[:, t, :], banks[:, OUT_BANKS[t], :], result[:, t, :], ALU.add).then_inc(bank_drained, 1)
                if not last:
                    gate_hidden(i + 1, ahead)

            all_steps(dve, step, peeled=2)


def project_qkv(nc, x_in, qT, kT, v, w):
    with ExitStack() as ctx:
        def sbuf(name, shape, dt=fp32):
            return ctx.enter_context(nc.sbuf_tensor(f"{name}_p", shape, dt))

        def sem(name):
            return ctx.enter_context(nc.semaphore(f"{name}_p"))

        weights = [Split(sbuf, n, [P, KT, D]) for n in ("Wq", "Wk", "Wv")]
        identity = sbuf("identity", [P, P])
        load_weights(nc, [
            (n, w[n].rearrange("(k p) n -> p k n", p=P), s) for n, s in zip(("Wq", "Wk", "Wv"), weights)
        ], [(identity[:], w["identity"])])
        norm = Norm(nc, ctx, "p")
        xT = Split(sbuf, "xT", [P, KT, CHUNK])
        outT = [Split(sbuf, n, [P, KT, CHUNK]) for n in ("queries", "keys")]
        values = sbuf("values", [P, TT, D])
        banks = ctx.enter_context(nc.psum_tensor("banks_p", [P, BANKS, CHUNK], fp32))
        bank_filled, high_ready, bank_drained = sem("bank_filled"), sem("high_ready"), sem("bank_drained")
        queries_stored, keys_stored, values_stored = sem("queries_stored"), sem("keys_stored"), sem("values_stored")
        X0, Q0, K0, V0, TILES = 0, 4, 8, 12, 16
        SPLITS = 12
        HEAD_PAIRS = B_HEADS // 2
        CHUNKS_PER_SEQUENCE = T // CHUNK
        block = ctx.enter_context(nc.Block())

        @block.sync
        def _(sp):
            with sp.Fori(0, BATCH) as b:
                with sp.Fori(0, CHUNKS_PER_SEQUENCE) as c:
                    i = b * CHUNKS_PER_SEQUENCE + c
                    for at, dst, src, done in ((Q0, qT, outT[0], queries_stored), (K0, kT, outT[1], keys_stored)):
                        sp.wait_ge(bank_drained, TILES * i + at + KT)
                        for half, part in ((0, src.high), (1, src.low)):
                            for k in range(KT):
                                sp.dma_start(
                                    dst[half, bass.ds(b * D + k * P, P), bass.ds(c * CHUNK, CHUNK)],
                                    part[:, k, :].bitcast(fp32),
                                ).then_inc(done, 16)
                    sp.wait_ge(bank_drained, TILES * i + V0 + TT)
                    for t in range(TT):
                        sp.dma_start(
                            v[bass.ds(b * HEAD_PAIRS, HEAD_PAIRS), bass.ds(c * CHUNK + t * P, P), :].rearrange("g p c -> p g c"),
                            values[:, t, :].rearrange("p (g c) -> p g c", c=2 * B_DIM),
                        ).then_inc(values_stored, 16)
            sp.wait_ge(queries_stored, 2 * KT * 16 * CHUNKS)
            sp.wait_ge(keys_stored, 2 * KT * 16 * CHUNKS)
            sp.wait_ge(values_stored, TT * 16 * CHUNKS)

        @block.gpsimd
        def _(pool):
            norm.set_constants(pool)
            norm.load(pool, x_in, 0)
            norm.apply(pool, 0)
            norm.load(pool, x_in, 1)
            with pool.Fori(0, CHUNKS - 2) as i:
                pool.wait_ge(bank_filled, TILES * i + X0 + KT)
                norm.apply(pool, i + 1)
                norm.load(pool, x_in, i + 2)
            pool.wait_ge(bank_filled, TILES * (CHUNKS - 2) + X0 + KT)
            norm.apply(pool, CHUNKS - 1)

        @block.tensor
        def _(pe):
            with pe.Fori(0, CHUNKS) as i:
                def fill(n, needs=-1):
                    needs = max(needs, n - BANKS)
                    pe.wait_ge(bank_drained, TILES * i + needs + 1 if needs >= 0 else TILES * i)
                    return banks[:, n % BANKS, :]

                pe.wait_ge(norm.xn_ready, i + 1)
                for k in range(KT):
                    turn(pe, fill(X0 + k), norm.xn, tile(k), identity).then_inc(bank_filled, 1)
                for at, weight in ((Q0, weights[0]), (K0, weights[1])):
                    for m in range(KT):
                        out = fill(at + m, X0 + KT - 1)
                        for k in range(KT):
                            last = product(pe, out, weight, xT, (slice(None), k, tile(m)), (slice(None), k), k == 0, k == KT - 1)
                        last.then_inc(bank_filled, 1)
                for t in range(TT):
                    out = fill(V0 + t)
                    for k in range(KT):
                        last = product(pe, out, xT, weights[2], (slice(None), k, tile(t)), (slice(None), k), k == 0, k == KT - 1)
                    last.then_inc(bank_filled, 1)

        @block.scalar
        def _(act):
            with act.Fori(0, CHUNKS) as i:
                for at, split, done in ((X0, xT, None), (Q0, outT[0], queries_stored), (K0, outT[1], keys_stored)):
                    if done is not None:
                        act.wait_ge(done, 2 * KT * 16 * i)
                    for k in range(KT):
                        act.wait_ge(bank_filled, TILES * i + at + k + 1)
                        act.activation(split.high[:, k, :], banks[:, (at + k) % BANKS, :], ACT.Copy).then_inc(high_ready, 1)

        @block.vector
        def _(dve):
            norm.take_moments(dve, 0)

            def chunk(i, last_chunk):
                for at, split, done in ((X0, xT, None), (Q0, outT[0], queries_stored), (K0, outT[1], keys_stored)):
                    if done is not None:
                        dve.wait_ge(done, 2 * KT * 16 * i)
                    for k in range(KT):
                        dve.wait_ge(high_ready, SPLITS * i + at + k + 1)
                        dve.tensor_tensor(
                            split.low[:, k, :], banks[:, (at + k) % BANKS, :], split.high[:, k, :].bitcast(fp32), ALU.subtract
                        ).then_inc(bank_drained, 1)
                    if at == Q0 and not last_chunk:
                        norm.take_moments(dve, i + 1)
                dve.wait_ge(values_stored, TT * 16 * i)
                for t in range(TT):
                    dve.wait_ge(bank_filled, TILES * i + V0 + t + 1)
                    dve.tensor_copy(values[:, t, :], banks[:, (V0 + t) % BANKS, :]).then_inc(bank_drained, 1)

            all_but_last(dve, chunk)


HEAD_PAIRS = B_HEADS // 2
PAIR_DIM = 2 * B_DIM
WITH_SUM = B_DIM + 1


def sum_later_values(nc, v, later, w):
    with ExitStack() as ctx:
        def sbuf(name, shape, dt=fp32):
            return ctx.enter_context(nc.sbuf_tensor(f"{name}_s", shape, dt))

        def sem(name):
            return ctx.enter_context(nc.semaphore(f"{name}_s"))

        values = sbuf("values", [P, TQ, D])
        rest = sbuf("rest", [P, TQ, D])
        sums = sbuf("sums", [P, TQ, D])
        after = sbuf("after", [P, P])
        ones = sbuf("ones", [P, P])
        banks = ctx.enter_context(nc.psum_tensor("banks_s", [P, BANKS, D], fp32))
        values_loaded, constants_loaded, ones_set = sem("values_loaded"), sem("constants_loaded"), sem("ones_set")
        rest_ready, bank_filled, bank_drained, stored = sem("rest_ready"), sem("bank_filled"), sem("bank_drained"), sem("stored")
        block = ctx.enter_context(nc.Block())

        def by_pair(a, b, t):
            return a[bass.ds(b * HEAD_PAIRS, HEAD_PAIRS), tile(t), :].rearrange("g p c -> p g c")

        @block.sync
        def _(sp):
            sp.dma_start(after[:], w["after"]).then_inc(constants_loaded, 16)
            with sp.Fori(0, BATCH) as b:
                sp.wait_ge(bank_filled, TQ * b)
                for t in reversed(range(TQ)):
                    sp.dma_start(
                        values[:, t, :].rearrange("p (g c) -> p g c", c=PAIR_DIM), by_pair(v, b, t)
                    ).then_inc(values_loaded, 16)
                sp.wait_ge(bank_drained, TQ * (b + 1))
                for t in range(TQ):
                    sp.dma_start(
                        by_pair(later, b, t), sums[:, t, :].rearrange("p (g c) -> p g c", c=PAIR_DIM)
                    ).then_inc(stored, 16)
            sp.wait_ge(stored, 16 * TQ * BATCH)

        @block.gpsimd
        def _(pool):
            pool.memset(ones[:], 1.0).then_inc(ones_set, 1)
            pool.memset(rest[:, TQ - 1, :], 0.0).then_inc(ones_set, 1)
            pool.wait_ge(ones_set, 2)
            with pool.Fori(0, BATCH) as b:
                pool.wait_ge(bank_filled, TQ * b)
                pool.wait_ge(values_loaded, 16 * TQ * (b + 1))
                for t in reversed(range(TQ - 1)):
                    pool.wait_ge(rest_ready, (TQ - 1) * b + TQ - 2 - t)
                    pool.tensor_tensor(rest[:, t, :], rest[:, t + 1, :], values[:, t + 1, :], ALU.add).then_inc(rest_ready, 1)

        @block.tensor
        def _(pe):
            pe.wait_ge(constants_loaded, 16)
            pe.wait_ge(ones_set, 2)
            with pe.Fori(0, BATCH) as b:
                pe.wait_ge(values_loaded, 16 * TQ * (b + 1))
                for n, t in enumerate(reversed(range(TQ))):
                    if n > 0:
                        pe.wait_ge(rest_ready, (TQ - 1) * b + n)
                    pe.wait_ge(bank_drained, TQ * b + n + 1 - BANKS if n >= BANKS else TQ * b)
                    pe.matmul(banks[:, n % BANKS, :], after[:], values[:, t, :], start=True, stop=False)
                    pe.matmul(banks[:, n % BANKS, :], ones[:], rest[:, t, :], start=False, stop=True).then_inc(bank_filled, 1)

        @block.scalar
        def _(act):
            with act.Fori(0, BATCH) as b:
                act.wait_ge(stored, 16 * TQ * b)
                for n, t in enumerate(reversed(range(TQ))):
                    act.wait_ge(bank_filled, TQ * b + n + 1)
                    act.activation(sums[:, t, :], banks[:, n % BANKS, :], ACT.Copy).then_inc(bank_drained, 1)


def causal_product_attention(nc, qT, kT, v, later, context, w):
    with ExitStack() as ctx:
        def sbuf(name, shape, dt=fp32):
            return ctx.enter_context(nc.sbuf_tensor(f"{name}_b", shape, dt))

        def sem(name):
            return ctx.enter_context(nc.semaphore(f"{name}_b"))

        ROWS = 3 * B_DIM
        PEAK_ROW = ROWS
        QC = T // CHUNK
        GPAIRS = BATCH * HEAD_PAIRS
        units = [(c, j) for c in range(QC) for j in range(TT * c + TT)]
        UNITS = len(units)
        pieces = [(h, i, k) for h in range(2) for i in range(TQ) for k in range(i // TT + 1)]
        PIECES = len(pieces)
        LAG = 3
        PIECE_TO = 37
        PEAKS_AT = PIECE_TO + 1
        TURN_LAG = 3
        KEPT = 5
        DIAGONALS = TQ
        ends = [sum(TT * d + TT for d in range(c + 1)) - 1 for c in range(QC)]
        NORM_STEPS = 2

        def pieces_at(u):
            def work(u):
                return sum(CHUNK * (c + 1) - query_start(c, j) for c, j in units[:u])

            def before(u):
                return PIECES * min(work(u), work(PIECE_TO)) // work(PIECE_TO)
            return range(before(u), before(u + 1))

        queries = [sbuf(f"queries{e}", [P, 2, T], f32r) for e in range(2)]
        keys = [sbuf(f"keys{e}", [P, 2, T], f32r) for e in range(2)]
        values = [sbuf(f"values{e}", [P, TQ, 2, WITH_SUM]) for e in range(2)]
        later_values = sbuf("later_values", [P, TQ, 2, WITH_SUM])
        counts = sbuf("counts", [P, TQ])
        later_part = [sbuf(f"later_part{e}", [P, TQ, 2, WITH_SUM]) for e in range(2)]
        exps = [sbuf(f"exps{n}", [P, 2, CHUNK]) for n in range(KEPT)]
        identity = sbuf("identity", [P, P])
        upto = sbuf("upto", [P, P])
        since = sbuf("since", [P, P])
        scratch = [sbuf(f"scratch{n}", [P, P]) for n in range(2)]
        piece_peaks = sbuf("piece_peaks", [P, 2, TQ, 6])
        peaks = sbuf("peaks", [P, 2, TQ])
        minus_peaks = sbuf("minus_peaks", [P, 2 * TQ], f32r)
        minus_peaks_T = sbuf("minus_peaks_T", [2 * TQ, P], f32r)
        later_weight = sbuf("later_weight", [P, 2, TQ])
        sumsT = sbuf("sumsT", [P, CHUNK])
        numerator = sbuf("numerator", [P, TT, 2, WITH_SUM])
        over_sum = sbuf("over_sum", [P, TT, 2])
        out = sbuf("out", [P, TQ, 2, B_DIM])
        banks = ctx.enter_context(nc.psum_tensor("banks_b", [P, BANKS, CHUNK], fp32))
        SCORES, PRODUCTS = 2, 6

        constants_loaded, constants_set, counts_loaded = sem("constants_loaded"), sem("constants_set"), sem("counts_loaded")
        counts_set = sem("counts_set")
        queries_loaded = [[sem(f"queries_loaded{e}{c}") for c in range(QC)] for e in range(2)]
        keys_loaded = [[sem(f"keys_loaded{e}{c}") for c in range(QC)] for e in range(2)]
        values_loaded, later_loaded = sem("values_loaded"), sem("later_loaded")
        piece_filled, piece_taken, peaks_taken, peaks_negated = sem("piece_filled"), sem("piece_taken"), sem("peaks_taken"), sem("peaks_negated")
        peaks_turned, peaks_copied, peak_rows_loaded = sem("peaks_turned"), sem("peaks_copied"), sem("peak_rows_loaded")
        later_weight_ready, later_part_ready = sem("later_weight_ready"), sem("later_part_ready")
        scores_filled, exp_done, diagonal_masked = sem("scores_filled"), sem("exp_done"), sem("diagonal_masked")
        products_done, sums_copied, chunk_turned, norm_steps, chunk_out = (
            sem("products_done"), sem("sums_copied"), sem("chunk_turned"), sem("norm_steps"), sem("chunk_out"))
        stored, blocks_masked = sem("stored"), sem("blocks_masked")
        block = ctx.enter_context(nc.Block())

        PARTS = 3
        VALUE_LOADS = 2
        TAIL = LAG + TURN_LAG + 1

        def for_pairs(engine, at, rounds=(GPAIRS - 2) // 2):

            def step(e, g, first=False):
                for u in range(UNITS):
                    if u < TAIL and not first:
                        at(1 - e, g - 1, UNITS + u)
                    at(e, g, u)

            step(0, 0, first=True)
            with engine.Fori(0, rounds) as r:
                step(1, r * 2 + 1)
                step(0, r * 2 + 2)
            for g in range(2 * rounds + 1, GPAIRS):
                step(g % 2, g)
            for u in range(TAIL):
                at(1, GPAIRS - 1, UNITS + u)

        def is_last(g):
            return isinstance(g, int) and g == GPAIRS - 1

        def loads(e, g):
            return 8 * PARTS * (g + 2 - e)

        def query_start(c, j):
            return max(CHUNK * c, P * j)

        def is_diagonal(u):
            c, j = units[u]
            return j >= TT * c

        def diagonals(u):
            return sum(is_diagonal(n) for n in range(u + 1))

        @block.sync
        def _(sp):
            for dst, name in ((identity, "identity"), (upto, "upto"), (since, "since")):
                sp.dma_start(dst[:], w[name]).then_inc(constants_loaded, 16)
            sp.dma_start(counts[:], w["later_counts"]).then_inc(counts_loaded, 16)

            def load_chunk(e, g, c, tiles, view, done, halves):
                for n, half in enumerate(halves):
                    sp.dma_start(
                        tiles[e][n * B_DIM : (n + 1) * B_DIM, :, c * CHUNK : (c + 1) * CHUNK].bitcast(fp32),
                        view[half, bass.ds(g * PAIR_DIM, PAIR_DIM), c * CHUNK : (c + 1) * CHUNK].rearrange(
                            "(h r) t -> r h t", h=2
                        ),
                    ).then_inc(done[e][c], 16)

            def load_queries(e, g, c):
                load_chunk(e, g, c, queries, qT, queries_loaded, (0, 1, 0))

            def load_keys(e, g, c):
                load_chunk(e, g, c, keys, kT, keys_loaded, (0, 0, 1))

            def load_values(e, g):
                for dst, src, done in ((values[e], v, values_loaded), (later_values, later, later_loaded)):
                    for h in range(2):
                        sp.dma_start(
                            dst[:, :, h, 0:B_DIM],
                            src[g, :, h * B_DIM : (h + 1) * B_DIM].rearrange("(t p) c -> p t c", p=P),
                        ).then_inc(done, 16)

            def load_peak_rows(e, g):
                sp.wait_ge(peaks_copied, g + 1)
                for h in range(2):
                    sp.dma_start(
                        queries[e][PEAK_ROW : PEAK_ROW + 1, h, :].bitcast(fp32).rearrange("a (t p) -> a t p", p=P),
                        minus_peaks_T[h * TQ : (h + 1) * TQ, :].bitcast(fp32),
                    ).then_inc(peak_rows_loaded, 16)

            for e in range(2):
                for c in range(QC):
                    load_queries(e, e, c)
                    load_keys(e, e, c)
                if e == 0:
                    load_values(0, 0)
            load_peak_rows(0, 0)

            def at(e, g, u):
                if u == LAG and not is_last(g):
                    wait_for(sp, products_done, UNITS * g)
                    sp.wait_ge(later_part_ready, g + 1)
                    load_values(1 - e, g + 1)
                if u == PEAKS_AT and not is_last(g):
                    load_peak_rows(1 - e, g + 1)
                if not isinstance(g, int) or g < GPAIRS - 2:
                    for c in range(QC):
                        if u == ends[c] + 1:
                            sp.wait_ge(scores_filled, UNITS * g + ends[c] + 1)
                            load_queries(e, g + 2, c)
                        if u == ends[QC - 2] + 1 + TT * (c + 1):
                            sp.wait_ge(scores_filled, UNITS * g + ends[QC - 2] + 1 + TT * (c + 1))
                            load_keys(e, g + 2, c)
                if u == UNITS + LAG + TURN_LAG:
                    sp.wait_ge(chunk_out, QC * (g + 1))
                    sp.dma_start(
                        context[g, :, :].rearrange("(t p) c -> p t c", p=P), out[:].rearrange("p t h c -> p t (h c)")
                    ).then_inc(stored, 16)

            for_pairs(sp, at, (GPAIRS - 2) // 2 - 1)
            sp.wait_ge(stored, 16 * GPAIRS)

        @block.gpsimd
        def _(pool):
            for e in range(2):
                pool.memset(values[e][:, :, :, B_DIM:], 1.0).then_inc(constants_set, 1)
            pool.memset(sumsT[:], 0.0).then_inc(constants_set, 1)
            pool.memset(piece_peaks[:], 0.0).then_inc(constants_set, 1)
            for e in range(2):
                pool.wait_ge(constants_set, 4 + e)
                pool.memset(keys[e][PEAK_ROW : PEAK_ROW + 1, :, :].bitcast(fp32), 1.0).then_inc(constants_set, 1)
            pool.wait_ge(constants_set, 6)
            pool.memset(piece_peaks[:, :, TQ - 1, 5:6], -BIG).then_inc(constants_set, 1)
            pool.wait_ge(constants_loaded, 16 * 3)
            pool.wait_ge(counts_loaded, 16)
            for h in range(2):
                pool.tensor_copy(later_values[:, :, h, B_DIM], counts[:]).then_inc(counts_set, 1)
            pool.wait_ge(counts_set, 2)

            def weigh_later(e, g):
                pool.wait_ge(later_loaded, 16 * VALUE_LOADS * (g + 1))
                pool.wait_ge(later_weight_ready, g + 1)
                pool.tensor_tensor(
                    later_part[e][:], later_values[:],
                    later_weight[:].rearrange("p h (t a) -> p t h a", a=1).broadcast_to([P, TQ, 2, WITH_SUM]), ALU.mult,
                ).then_inc(later_part_ready, 1)

            weigh_later(0, 0)

            def at(e, g, u):
                if u < UNITS and is_diagonal(u):
                    pool.wait_ge(exp_done, UNITS * g + u + 1)
                    corner = exps[u % KEPT][:, :, 0:P]
                    pool.tensor_tensor(
                        corner, corner, since[:].rearrange("p (a q) -> p a q", a=1).broadcast_to([P, 2, P]), ALU.mult
                    ).then_inc(diagonal_masked, 1)
                if u == PEAKS_AT and not is_last(g):
                    wait_for(pool, chunk_out, QC * g)
                    weigh_later(1 - e, g + 1)

            for_pairs(pool, at)

        @block.tensor
        def _(pe):
            pe.wait_ge(constants_loaded, 16 * 3)
            pe.wait_ge(constants_set, 7)

            def piece(e, g, n):
                h, i, k = pieces[n]
                if h == 0 and i % TT == 0 and k == 0:
                    pe.wait_ge(queries_loaded[e][i // TT], loads(e, g))
                    pe.wait_ge(keys_loaded[e][i // TT], loads(e, g))
                if n == 0:
                    wait_for(pe, peaks_copied, g)
                wait_for(pe, piece_taken, PIECES * g + n - 1)
                width = min(CHUNK, P * (i + 1) - CHUNK * k)
                pe.matmul(
                    banks[:, n % 2, 0:width], queries[e][0:ROWS, h, tile(i)],
                    keys[e][0:ROWS, h, CHUNK * k : CHUNK * k + width], start=True, stop=True,
                ).then_inc(piece_filled, 1)

            def turn_peaks(g):
                pe.wait_ge(peaks_negated, g + 1)
                pe.transpose(banks[0 : 2 * TQ, 0, 0:P], minus_peaks[:].bitcast(fp32), identity[:]).then_inc(peaks_turned, 1)

            for n in range(PIECES):
                piece(0, 0, n)
            turn_peaks(0)

            def turn_sums(g, c):
                pe.wait_ge(sums_copied, QC * g + c + 1)
                for t in range(TT):
                    last = pe.transpose(banks[:, PRODUCTS + c % 2, tile(t)], sumsT[:, tile(t)], identity[:])
                last.then_inc(chunk_turned, 1)

            def scores(e, g, u):
                c, j = units[u]
                if u == 0:
                    pe.wait_ge(peak_rows_loaded, 32 * (g + 1))
                wait_for(pe, exp_done, UNITS * g + u - 1)
                q0 = query_start(c, j)
                width = CHUNK * (c + 1) - q0
                for h in range(2):
                    last = pe.matmul(
                        banks[:, SCORES + 2 * (u % 2) + h, 0:width], keys[e][0 : ROWS + 1, h, tile(j)],
                        queries[e][0 : ROWS + 1, h, q0 : q0 + width], start=True, stop=True,
                    )
                last.then_inc(scores_filled, 1)

            def products(e, g, u):
                c, j = units[u]
                pe.wait_ge(exp_done, UNITS * g + u + 1)
                if u == 0:
                    pe.wait_ge(values_loaded, 16 * VALUE_LOADS * (g + 1))
                if is_diagonal(u):
                    pe.wait_ge(diagonal_masked, DIAGONALS * g + diagonals(u))
                if j == 0:
                    wait_for(pe, chunk_out, QC * g + c - 1)
                width = CHUNK * (c + 1) - query_start(c, j)
                for h in range(2):
                    last = pe.matmul(
                        banks[64 * h : 64 * h + WITH_SUM, PRODUCTS + c % 2, CHUNK - width :], values[e][:, j, h, :],
                        exps[u % KEPT][:, h, 0:width], start=j == 0, stop=j == TT * c + TT - 1,
                    )
                last.then_inc(products_done, 1)

            def at(e, g, u):
                for c, end in enumerate(ends):
                    if u == end + LAG + TURN_LAG:
                        turn_sums(g, c)
                next_pieces = [] if u >= UNITS or is_last(g) else list(pieces_at(u))
                for n in next_pieces[:1]:
                    piece(1 - e, g + 1, n)
                if u == PEAKS_AT and not is_last(g):
                    turn_peaks(g + 1)
                if u < UNITS:
                    scores(e, g, u)
                for n in next_pieces[1:2]:
                    piece(1 - e, g + 1, n)
                if LAG <= u < UNITS + LAG:
                    products(e, g, u - LAG)
                for n in next_pieces[2:]:
                    piece(1 - e, g + 1, n)

            for_pairs(pe, at)

        @block.scalar
        def _(act):
            def copy_peaks(g):
                act.wait_ge(peaks_turned, g + 1)
                wait_for(act, peak_rows_loaded, 32 * g)
                act.activation(minus_peaks_T[:], banks[0 : 2 * TQ, 0, 0:P], ACT.Copy).then_inc(peaks_copied, 1)
                wait_for(act, later_part_ready, g)
                act.activation(
                    later_weight[:].rearrange("p h t -> p (h t)"), minus_peaks[:].bitcast(fp32), ACT.Exp, scale=B_SCALE
                ).then_inc(later_weight_ready, 1)

            copy_peaks(0)

            def copy_sums(g, c):
                act.wait_ge(products_done, UNITS * g + ends[c] + 1)
                wait_for(act, chunk_turned, QC * g + c)
                for h in range(2):
                    rows = slice(64 * h, 64 * h + WITH_SUM)
                    last = act.activation(sumsT[rows, :], banks[rows, PRODUCTS + c % 2, :], ACT.Copy)
                last.then_inc(sums_copied, 1)

            def at(e, g, u):
                for c, end in enumerate(ends):
                    if u == end + LAG + 1:
                        copy_sums(g, c)
                if u >= UNITS:
                    return
                c, j = units[u]
                act.wait_ge(scores_filled, UNITS * g + u + 1)
                wait_for(act, products_done, UNITS * g + u + 1 - KEPT)
                width = CHUNK * (c + 1) - query_start(c, j)
                bank = SCORES + 2 * (u % 2)
                act.activation(
                    exps[u % KEPT][:, :, 0:width], banks[:, bank : bank + 2, 0:width], ACT.Exp, scale=B_SCALE
                ).then_inc(exp_done, 1)
                if u == PEAKS_AT and not is_last(g):
                    copy_peaks(g + 1)

            for_pairs(act, at)

        @block.vector
        def _(dve):
            dve.wait_ge(constants_set, 7)
            dve.wait_ge(constants_loaded, 16 * 3)

            def take_piece(g, n):
                h, i, k = pieces[n]
                before = min(CHUNK, P * i - CHUNK * k)
                dve.wait_ge(piece_filled, PIECES * g + n + 1)
                if before:
                    last = dve.tensor_reduce(piece_peaks[:, h, i, k : k + 1], banks[:, n % 2, 0:before], AX.X, ALU.max)
                if k == i // TT and before:
                    last = dve.tensor_tensor_reduce(
                        scratch[n % 2][:], banks[:, n % 2, before : before + P], upto[:], 1.0, -BIG, ALU.mult, ALU.max,
                        piece_peaks[:, h, i, 4:5],
                    )
                elif k == i // TT:
                    dve.tensor_tensor(scratch[n % 2][:], banks[:, n % 2, 0:P], upto[:], ALU.mult).then_inc(blocks_masked, 1)
                    dve.wait_ge(blocks_masked, 2 * QC * g + h * QC + k + 1)
                    last = dve.tensor_reduce(piece_peaks[:, h, i, 4:5], scratch[n % 2][:], AX.X, ALU.max)
                last.then_inc(piece_taken, 1)

            def finish_peaks(g):
                dve.wait_ge(piece_taken, PIECES * (g + 1))
                dve.tensor_reduce(peaks[:], piece_peaks[:], AX.X, ALU.max).then_inc(peaks_taken, 1)
                dve.wait_ge(peaks_taken, g + 1)
                wait_for(dve, later_weight_ready, g)
                dve.tensor_scalar(
                    minus_peaks[:], peaks[:].rearrange("p h t -> p (h t)"), -1.0, None, ALU.mult
                ).then_inc(peaks_negated, 1)

            for n in range(PIECES):
                take_piece(0, n)
            finish_peaks(0)

            def normalise(e, g, c):
                done = QC * g + c
                if c == 0:
                    dve.wait_ge(later_part_ready, g + 1)
                    wait_for(dve, stored, 16 * g)
                wait_for(dve, chunk_out, done)
                dve.wait_ge(chunk_turned, done + 1)
                dve.tensor_tensor(
                    numerator[:],
                    banks[:, PRODUCTS + c % 2, :].rearrange("p (t h c) -> p t h c", h=2, c=64)[:, :, :, 0:WITH_SUM],
                    later_part[e][:, TT * c : TT * c + TT, :, :], ALU.add,
                ).then_inc(norm_steps, 1)
                dve.wait_ge(norm_steps, NORM_STEPS * done + 1)
                dve.reciprocal(over_sum[:], numerator[:, :, :, B_DIM]).then_inc(norm_steps, 1)
                dve.wait_ge(norm_steps, NORM_STEPS * done + 2)
                dve.tensor_tensor(
                    out[:, TT * c : TT * c + TT, :, :], numerator[:, :, :, 0:B_DIM],
                    over_sum[:].rearrange("p t (h a) -> p t h a", a=1).broadcast_to([P, TT, 2, B_DIM]), ALU.mult,
                ).then_inc(chunk_out, 1)

            def at(e, g, u):
                if u < UNITS and not is_last(g):
                    for n in pieces_at(u):
                        take_piece(g + 1, n)
                    if u == PIECE_TO - 1:
                        finish_peaks(g + 1)
                for c, end in enumerate(ends):
                    if u == end + LAG + TURN_LAG:
                        normalise(e, g, c)

            for_pairs(dve, at)


def project_context(nc, context, x_in, x_out, w):
    with ExitStack() as ctx:
        def sbuf(name, shape, dt=fp32):
            return ctx.enter_context(nc.sbuf_tensor(f"{name}_o", shape, dt))

        def sem(name):
            return ctx.enter_context(nc.semaphore(f"{name}_o"))

        wo = Split(sbuf, "Wo", [P, KT, D])
        identity = sbuf("identity", [P, P])
        load_weights(nc, [("Wo", w["Wo"].rearrange("(k p) n -> p k n", p=P), wo)], [(identity[:], w["identity"])])
        mixed = [sbuf(f"mixed{e}", [P, TT, D]) for e in range(2)]
        result = [sbuf(f"result{e}", [P, TT, D]) for e in range(2)]
        mixedT = Split(sbuf, "mixedT", [P, KT, CHUNK])
        banks = ctx.enter_context(nc.psum_tensor("banks_o", [P, BANKS, CHUNK], fp32))
        bank_filled, high_ready, bank_drained = sem("bank_filled"), sem("high_ready"), sem("bank_drained")
        context_loaded = [sem(f"context_loaded{e}") for e in range(2)]
        residual_loaded = [sem(f"residual_loaded{e}") for e in range(2)]
        stored = [sem(f"stored{e}") for e in range(2)]
        X0, OUT0, TILES = 0, 4, 8
        block = ctx.enter_context(nc.Block())
        ROUNDS = CHUNKS // 2
        ROUNDS_PER_SEQUENCE = ROUNDS // BATCH

        @block.sync
        def _(sp):
            with sp.Fori(0, BATCH) as b:
                with sp.Fori(0, ROUNDS_PER_SEQUENCE) as c:
                    r = b * ROUNDS_PER_SEQUENCE + c
                    for e in range(2):
                        sp.wait_ge(bank_filled, TILES * 2 * r)
                        for t in range(TT):
                            sp.dma_start(
                                mixed[e][:, t, :].rearrange("p (g c) -> p g c", c=PAIR_DIM),
                                context[
                                    bass.ds(b * HEAD_PAIRS, HEAD_PAIRS), bass.ds(c * 2 * CHUNK + e * CHUNK + t * P, P), :
                                ].rearrange("g p c -> p g c"),
                            ).then_inc(context_loaded[e], 16)
                        sp.wait_ge(stored[e], 16 * r)
                        sp.dma_start(
                            result[e][:], x_in[bass.ds(r * 2 * CHUNK + e * CHUNK, CHUNK), :].rearrange("(t p) d -> p t d", p=P)
                        ).then_inc(residual_loaded[e], 16)

        @block.gpsimd
        def _(pool):
            with pool.Fori(0, ROUNDS) as r:
                for e in range(2):
                    pool.wait_ge(bank_drained, TILES * 2 * r + TILES * (e + 1))
                    pool.dma_start(
                        x_out[bass.ds(r * 2 * CHUNK + e * CHUNK, CHUNK), :].rearrange("(t p) d -> p t d", p=P), result[e][:]
                    ).then_inc(stored[e], 16)
            for e in range(2):
                pool.wait_ge(stored[e], 16 * ROUNDS)

        @block.tensor
        def _(pe):
            with pe.Fori(0, ROUNDS) as r:
                for e in range(2):
                    at = r * (2 * TILES) + e * TILES
                    pe.wait_ge(context_loaded[e], 16 * TT * (r + 1))
                    for k in range(KT):
                        pe.wait_ge(bank_drained, at)
                        turn(pe, banks[:, X0 + k, :], mixed[e], tile(k), identity).then_inc(bank_filled, 1)
                    for t in range(TT):
                        pe.wait_ge(bank_drained, at + KT)
                        for k in range(KT):
                            last = product(
                                pe, banks[:, OUT0 + t, :], mixedT, wo, (slice(None), k, tile(t)), (slice(None), k),
                                k == 0, k == KT - 1,
                            )
                        last.then_inc(bank_filled, 1)

        @block.scalar
        def _(act):
            with act.Fori(0, ROUNDS) as r:
                for e in range(2):
                    for k in range(KT):
                        act.wait_ge(bank_filled, r * (2 * TILES) + e * TILES + k + 1)
                        act.activation(mixedT.high[:, k, :], banks[:, X0 + k, :], ACT.Copy).then_inc(high_ready, 1)

        @block.vector
        def _(dve):
            with dve.Fori(0, ROUNDS) as r:
                for e in range(2):
                    for k in range(KT):
                        dve.wait_ge(high_ready, r * (2 * KT) + e * KT + k + 1)
                        dve.tensor_tensor(
                            mixedT.low[:, k, :], banks[:, X0 + k, :], mixedT.high[:, k, :].bitcast(fp32), ALU.subtract
                        ).then_inc(bank_drained, 1)
                    dve.wait_ge(residual_loaded[e], 16 * (r + 1))
                    for t in range(TT):
                        dve.wait_ge(bank_filled, r * (2 * TILES) + e * TILES + OUT0 + t + 1)
                        dve.tensor_tensor(
                            result[e][:, t, :], banks[:, OUT0 + t, :], result[e][:, t, :], ALU.add
                        ).then_inc(bank_drained, 1)


def hybrid_block(nc, w, x, out):
    def scratch(name, shape):
        return nc.dram_tensor(name, shape, fp32, kind="Internal").ap()

    x1, x2, x3 = (scratch(n, [TOKENS, D]) for n in ("x1", "x2", "x3"))
    qT, kT = (scratch(n, [2, BATCH * D, T]) for n in ("qT", "kT"))
    v, later, context = (scratch(n, [BATCH * HEAD_PAIRS, T, PAIR_DIM]) for n in ("v", "later", "context"))
    conv_attention(nc, x, x1, w)
    with ExitStack() as ctx:
        experts = Experts(nc, ctx, w)
        routed_experts(nc, x1, x2, experts, "e1", load_experts=True)
        project_qkv(nc, x2, qT, kT, v, w)
        sum_later_values(nc, v, later, w)
        causal_product_attention(nc, qT, kT, v, later, context, w)
        project_context(nc, context, x2, x3, w)
        routed_experts(nc, x3, out, experts, "e2", load_experts=False)


def kernel(**inputs):
    import numpy as np
    import concourse.bacc as bacc
    from concourse.bass_utils import run_bass_kernel_spmd

    a = {n: np.asarray(x) for n, x in inputs.items()}
    one = np.float32(1)
    arrays = {
        "x": a["L0_attn_a_x"].reshape(TOKENS, D),
        "conv_w": a["L0_attn_a_conv_w"],
        "conv_b": a["L0_attn_a_conv_b"].reshape(3, A_WIDTH).T,
        "wq": a["L0_attn_a_wq"].reshape(A_WIDTH, D),
        "wk": a["L0_attn_a_wk"].reshape(A_WIDTH, D),
        "wv": a["L0_attn_a_wv"].reshape(A_WIDTH, D),
        "bq": a["L0_attn_a_bq"].reshape(PAIRS, P).T,
        "bk": a["L0_attn_a_bk"].reshape(PAIRS, P).T,
        "bv": a["L0_attn_a_bv"].reshape(PAIRS, P).T,
        "wo": a["L0_attn_a_wo"].reshape(D, A_WIDTH),
        "bo": a["L0_attn_a_bo"].reshape(A_WIDTH, 1),
        "proj_w": a["L0_attn_a_proj_w"],
        "proj_b": a["L0_attn_a_proj_b"].reshape(1, D),
        "Wq": a["L0_attn_b_Wq"], "Wk": a["L0_attn_b_Wk"], "Wv": a["L0_attn_b_Wv"], "Wo": a["L0_attn_b_Wo"],
        "down": a["L0_ffn_A"].reshape(EXPERTS * RANK, D).T,
        "up": a["L0_ffn_B"].transpose(0, 2, 1).reshape(EXPERTS * RANK, D),
        "router": a["L0_ffn_Wr"].T,
        "router_b": a["L0_ffn_br"].reshape(1, EXPERTS),
        "identity": np.eye(P, dtype=np.float32),
        "causal": np.triu(np.full((P, P), -1e9 / A_SCALE, np.float32), 1),
        "keep": np.tile((np.arange(CHUNKS) % (T // CHUNK) > 0).astype(np.float32), (P, 1)),
        "expert_rank": np.arange(EXPERTS, 0, -1, dtype=np.float32).reshape(1, EXPERTS),
        "upto": np.tril(np.full((P, P), one)),
        "since": np.triu(np.full((P, P), one)),
        "after": np.tril(np.full((P, P), one), -1),
        "later_counts": (T - 1 - np.arange(T, dtype=np.float32)).reshape(TQ, P).T,
    }
    arrays = {n: np.ascontiguousarray(x) for n, x in arrays.items()}
    nc = bacc.Bacc("TRN2", target_bir_lowering=False, num_devices=1)
    dram = {n: nc.dram_tensor(n, x.shape, mybir.dt.from_np(x.dtype), kind="ExternalInput").ap() for n, x in arrays.items()}
    out = nc.dram_tensor("out", [TOKENS, D], fp32, kind="ExternalOutput").ap()
    hybrid_block(nc, dram, dram["x"], out)
    got = run_bass_kernel_spmd(nc, [arrays], core_ids=[0])
    return got.results[0]["out"].reshape(BATCH, T, D)
```

```python
import concourse.bass as bass
from concourse import mybir
from contextlib import ExitStack

fp32 = mybir.dt.float32
f32r = mybir.dt.float32r
ALU = mybir.AluOpType
ACT = mybir.ActivationFunctionType
AX = mybir.AxisListType

P = 128
D = 512
KT = D // P
TOKENS = 4096
BATCH = 2
T = TOKENS // BATCH
CHUNK = 512
TT = CHUNK // P
CHUNKS = TOKENS // CHUNK
EPS = 1e-5
TAPS = 3
HALO = TAPS - 1
A_HEADS, A_DIM, A_WIDTH = 8, 64, 128
PAIRS = A_HEADS // 2
A_SCALE = A_DIM ** -0.5
EXPERTS, RANK = 8, 64
B_HEADS, B_DIM = 16, 32
TQ = T // P
B_SCALE = T ** -0.5
BANKS = 8
BIG = 3.0e38


class Split:

    def __init__(self, new, name, shape):
        self.high = new(name + "_high", shape, f32r)
        self.low = new(name + "_low", shape, f32r)


def product(pe, out, stationary, moving, at, mv, first, last):
    pe.matmul(out, stationary.high[at], moving.high[mv], start=first, stop=False)
    pe.matmul(out, stationary.low[at], moving.high[mv], start=False, stop=False)
    return pe.matmul(out, stationary.high[at], moving.low[mv], start=False, stop=last)


class Weights:

    def __init__(self, sem, parts, tag):
        self.parts = parts
        self.arrived = [sem(f"weight{n}_arrived_{tag}") for n in range(len(parts))]
        self.high_ready = sem(f"weight_high_ready_{tag}")
        self.ready = sem(f"weight_ready_{tag}")

    def load(self, engine, n):
        _, view, staged = self.parts[n]
        engine.dma_start(staged, view).then_inc(self.arrived[n], 16)

    def write_high(self, act, n):
        split, _, staged = self.parts[n]
        act.wait_ge(self.arrived[n], 16)
        act.activation(split.high[:], staged, ACT.Copy).then_inc(self.high_ready, 1)

    def write_low(self, dve, n):
        split, _, staged = self.parts[n]
        dve.wait_ge(self.high_ready, n + 1)
        dve.tensor_tensor(split.low[:], staged, split.high[:].bitcast(fp32), ALU.subtract).then_inc(self.ready, 1)

    def wait(self, engine, n):
        engine.wait_ge(self.ready, n + 1)


def wait_for(engine, semaphore, value):
    if not isinstance(value, int) or value > 0:
        engine.wait_ge(semaphore, value)


class Norm:

    def __init__(self, nc, ctx, tag):
        def sbuf(name, shape):
            return ctx.enter_context(nc.sbuf_tensor(f"{name}_{tag}", shape, fp32))

        def sem(name):
            return ctx.enter_context(nc.semaphore(f"{name}_{tag}"))

        self.x = sbuf("x", [P, TT, D])
        self.xn = sbuf("xn", [P, TT, D])
        self.stats = sbuf("stats", [P, TT, 6])
        self.moments = sbuf("moments", [P, TT, 2])
        self.var_eps = sbuf("var_eps", [P, TT])
        self.rstd = sbuf("rstd", [P, TT])
        self.eps = sbuf("eps", [P, TT])
        self.minus_half = sbuf("minus_half", [P, TT])
        self.x_loaded = sem("x_loaded")
        self.stats_taken = sem("stats_taken")
        self.moments_ready = sem("moments_ready")
        self.norm_steps = sem("norm_steps")
        self.xn_ready = sem("xn_ready")
        self.constants_set = sem("constants_set")

    def load(self, sp, view, i, row=None):
        wait_for(sp, self.xn_ready, i)
        row = i * CHUNK if row is None else row
        sp.dma_start(self.x[:], view[bass.ds(row, CHUNK), :].rearrange("(t p) d -> p t d", p=P)).then_inc(
            self.x_loaded, 16
        )

    def take_moments(self, dve, i):
        dve.wait_ge(self.x_loaded, 16 * (i + 1))
        wait_for(dve, self.xn_ready, i)
        for t in range(TT):
            last = dve.bn_stats(self.stats[:, t, :], self.x[:, t, :])
        last.then_inc(self.stats_taken, 1)
        dve.wait_ge(self.constants_set, 2)
        dve.wait_ge(self.stats_taken, i + 1)
        for t in range(TT):
            last = dve.bn_aggr(self.moments[:, t, :], self.stats[:, t, :])
        last.then_inc(self.moments_ready, 1)

    def set_constants(self, pool):
        pool.memset(self.minus_half[:], -0.5).then_inc(self.constants_set, 1)
        pool.memset(self.eps[:], EPS).then_inc(self.constants_set, 1)
        pool.wait_ge(self.constants_set, 2)

    def start_first(self, pool):
        pool.wait_ge(self.moments_ready, 1)
        pool.tensor_tensor(self.var_eps[:], self.moments[:, :, 1], self.eps[:], ALU.add).then_inc(self.norm_steps, 1)
        pool.wait_ge(self.norm_steps, 1)
        pool.tensor_tensor(self.rstd[:], self.var_eps[:], self.minus_half[:], ALU.pow).then_inc(self.norm_steps, 2)

    def finish_first(self, dve):
        dve.wait_ge(self.norm_steps, 3)
        for t in range(TT):
            last = dve.tensor_scalar(
                self.xn[:, t, :], self.x[:, t, :], self.moments[:, t, 0:1], self.rstd[:, t : t + 1], ALU.subtract, ALU.mult
            )
        last.then_inc(self.xn_ready, 1)

    def apply(self, pool, i):
        pool.wait_ge(self.moments_ready, i + 1)
        pool.tensor_tensor(self.var_eps[:], self.moments[:, :, 1], self.eps[:], ALU.add).then_inc(self.norm_steps, 1)
        pool.tensor_tensor(
            self.xn[:], self.x[:], self.moments[:, :, 0:1].broadcast_to([P, TT, D]), ALU.subtract
        ).then_inc(self.norm_steps, 1)
        pool.wait_ge(self.norm_steps, 3 * i + 1)
        pool.tensor_tensor(self.rstd[:], self.var_eps[:], self.minus_half[:], ALU.pow).then_inc(self.norm_steps, 1)
        pool.wait_ge(self.norm_steps, 3 * i + 3)
        pool.tensor_tensor(
            self.xn[:], self.xn[:], self.rstd[:].rearrange("p (t a) -> p t a", a=1).broadcast_to([P, TT, D]), ALU.mult
        ).then_inc(self.xn_ready, 1)


def all_steps(engine, step, peeled=1):
    step(0, False)
    with engine.Fori(1, CHUNKS - peeled) as i:
        step(i, False)
    for i in range(CHUNKS - peeled, CHUNKS):
        step(i, i == CHUNKS - 1)


def norms_more(i):
    return not isinstance(i, int) or i + 2 < CHUNKS


def turn(pe, bank, source, columns, identity):
    for t in range(TT):
        last = pe.transpose(bank[:, t * P : (t + 1) * P], source[:, t, columns], identity[:])
    return last


def tile(n):
    return slice(n * P, (n + 1) * P)


def conv_attention(nc, x_in, x_out, w):
    with ExitStack() as ctx:
        def sbuf(name, shape, dt=fp32):
            return ctx.enter_context(nc.sbuf_tensor(f"{name}_a", shape, dt))

        def sem(name):
            return ctx.enter_context(nc.semaphore(f"{name}_a"))

        conv = [Split(sbuf, f"conv_{n}", [P, TAPS * KT, A_WIDTH]) for n in "qkv"]
        wq, wk, wv = (Split(sbuf, n, [P, D]) for n in ("wq", "wk", "wv"))
        wo = Split(sbuf, "wo", [P, PAIRS, A_WIDTH])
        proj = Split(sbuf, "proj", [P, D])
        identity = sbuf("identity", [P, P])
        causal = sbuf("causal", [P, P])
        conv_b = sbuf("conv_b", [P, 3])
        bq, bk, bv = (sbuf(n, [P, PAIRS]) for n in ("bq", "bk", "bv"))
        bo = sbuf("bo", [P, 1])
        proj_b = sbuf("proj_b", [P, D])
        keep = sbuf("keep", [P, CHUNKS])

        CONVS = ("v", "q", "k")
        of_conv = {"q": 0, "k": 1, "v": 2}
        W_Q, W_K, W_LAST = 3, 4, 7
        CONSTANTS = [
            (keep[:], w["keep"]), (conv_b[:], w["conv_b"]), (bq[:], w["bq"]), (bk[:], w["bk"]),
            (causal[:], w["causal"]), (bv[:], w["bv"]), (bo[:], w["bo"]), (proj_b[:], w["proj_b"].broadcast_to([P, D])),
        ]

        norm = Norm(nc, ctx, "a")
        xT = Split(sbuf, "xT", [P, KT, HALO + CHUNK])
        qkv = [Split(sbuf, n, [P, CHUNK]) for n in ("q", "k", "v")]
        qh = [sbuf(f"qh{e}", [P, CHUNK]) for e in range(2)]
        kh = [sbuf(f"kh{e}", [P, CHUNK]) for e in range(2)]
        vh = sbuf("vh", [P, TT, D])
        masked = [sbuf(f"masked{h}", [P, TT, P]) for h in range(2)]
        peak = [sbuf(f"peak{h}", [P, TT]) for h in range(2)]
        minus_peak = [[sbuf(f"minus_peak{e}{h}", [P, TT]) for h in range(2)] for e in range(2)]
        probs = [[sbuf(f"probs{e}{h}", [P, TT, P]) for h in range(2)] for e in range(2)]
        sums = [[sbuf(f"sums{e}{h}", [P, TT]) for h in range(2)] for e in range(2)]
        over_sums = [[sbuf(f"over_sums{e}{h}", [P, TT]) for h in range(2)] for e in range(2)]
        probsT = [sbuf(f"probsT{h}", [P, CHUNK]) for h in range(2)]
        ctxT = Split(sbuf, "ctxT", [P, PAIRS, CHUNK])
        mixT = Split(sbuf, "mixT", [P, CHUNK])
        result = sbuf("result", [P, TT, D])
        conv_v_staged = sbuf("conv_v_staged", [P, TAPS * KT, A_WIDTH])

        def over_taps(a):
            return a[:, 0:TAPS, :].rearrange("p s (k n) -> p (s k) n", n=A_WIDTH)

        def flat(a):
            return a[:].rearrange("p t s -> p (t s)")

        by_output = w["conv_w"].rearrange("s (k p) n -> p (s k) n", p=P)
        staged = (conv_v_staged[:], over_taps(vh), over_taps(result))
        weights = Weights(sem, [
            *((conv[of_conv[c]], by_output[:, :, tile(of_conv[c])], to) for c, to in zip(CONVS, staged)),
            (wq, w["wq"], flat(probs[0][0])), (wk, w["wk"], flat(probs[0][1])), (wv, w["wv"], flat(probs[1][0])),
            (wo, w["wo"].rearrange("(j p) n -> p j n", p=P), probs[1][1][:]), (proj, w["proj_w"], flat(masked[0])),
        ], "a")
        banks = ctx.enter_context(nc.psum_tensor("banks_a", [P, BANKS, CHUNK], fp32))
        conv_bank = {"v": 6, "q": 7, "k": 6}

        constants_loaded, identity_loaded = sem("constants_loaded"), sem("identity_loaded")
        bank_filled, high_ready = sem("bank_filled"), sem("high_ready")
        drained_by_act, drained_by_dve = sem("drained_by_act"), sem("drained_by_dve")
        conv_filled, conv_high, conv_drained = sem("conv_filled"), sem("conv_high"), sem("conv_drained")
        halo_cleared, halo_high, halo_low = sem("halo_cleared"), sem("halo_high"), sem("halo_low")
        peak_taken, peak_ready = sem("peak_taken"), sem("peak_ready")
        exp_done, sums_inverted, probs_ready = sem("exp_done"), sem("sums_inverted"), sem("probs_ready")
        residual_loaded, residual_ready, stored = sem("residual_loaded"), sem("residual_ready"), sem("stored")

        RING = 6
        before_steps = [("x", k) for k in range(KT)] + [("q", 0), ("k", 0)]

        def tiles_of(last):
            def heads(name, j):
                return [(name, j, 0), (name, j, 1)]

            return (
                heads("s", 0) + ([] if last else [("x", k) for k in range(KT)]) + [("v", t) for t in range(TT)]
                + [("q", 1), ("k", 1)] + heads("s", 1) + heads("t", 0) + [("c", 0)]
                + [("q", 2), ("k", 2)] + heads("s", 2) + heads("t", 1) + [("q", 3), ("k", 3), ("c", 1)]
                + heads("s", 3) + heads("t", 2) + [("c", 2)] + heads("t", 3) + [("c", 3), ("mix", 0), ("mix", 1)]
                + ([] if last else [("q", 0), ("k", 0)]) + [("o", t) for t in range(TT)]
            )

        every_step = tiles_of(False)

        def by_act(name):
            return name[0] in "qkv"

        def by_dve(name):
            return not by_act(name)

        def is_split(name):
            return name[0] in ("x", "c") or name == ("mix", 0)

        class Counts:

            def __init__(self, i, last):
                self.i, self.last = i, last
                self.names = tiles_of(last)
                self.earlier = before_steps if isinstance(i, int) and i == 0 else every_step

            def start(self, kind):
                return sum(map(kind, before_steps)) + sum(map(kind, every_step)) * self.i

            def up_to(self, kind, name):
                return self.start(kind) + sum(map(kind, self.names[: self.names.index(name) + 1]))

            def filled(self, name):
                return self.up_to(bool, name)

            def bank(self, name):
                return banks[:, self.names.index(name) % RING, :]

            def freed(self, kind, n):
                n -= RING
                if n >= 0:
                    return sum(map(kind, self.names[: n + 1]))
                return -sum(map(kind, self.earlier[len(self.earlier) + n + 1 :]))

        block = ctx.enter_context(nc.Block())

        @block.sync
        def _(sp):
            norm.load(sp, x_in, 0)
            sp.dma_start(identity[:], w["identity"]).then_inc(identity_loaded, 16)
            for n in range(len(CONVS)):
                weights.load(sp, n)
            for dst, src in CONSTANTS:
                sp.dma_start(dst, src).then_inc(constants_loaded, 16)
            for n in range(W_Q, W_LAST + 1):
                weights.load(sp, n)
            norm.load(sp, x_in, 1)
            weights.wait(sp, len(CONVS) - 1)

            def step(i, last):
                wait_for(sp, stored, 16 * i)
                sp.dma_start(
                    result[:], x_in[bass.ds(i * CHUNK, CHUNK), :].rearrange("(t p) d -> p t d", p=P)
                ).then_inc(residual_loaded, 16)
                if norms_more(i):
                    norm.load(sp, x_in, i + 2)
                sp.wait_ge(drained_by_dve, Counts(i, last).up_to(by_dve, ("o", TT - 1)))
                sp.dma_start(
                    x_out[bass.ds(i * CHUNK, CHUNK), :].rearrange("(t p) d -> p t d", p=P), result[:]
                ).then_inc(stored, 16)

            all_steps(sp, step, peeled=2)
            sp.wait_ge(stored, 16 * CHUNKS)

        @block.gpsimd
        def _(pool):
            for part in (xT.high, xT.low):
                pool.memset(part[:, :, CHUNK:].bitcast(fp32), 0.0).then_inc(halo_cleared, 1)
            norm.set_constants(pool)
            norm.start_first(pool)
            pool.wait_ge(bank_filled, KT)
            norm.apply(pool, 1)
            pool.wait_ge(constants_loaded, 16 * len(CONSTANTS))

            def step(i, last):
                for j in range(PAIRS):
                    for h in range(2):
                        e = j % 2
                        pool.wait_ge(sums_inverted, 2 * PAIRS * i + 2 * j + h + 1)
                        pool.tensor_tensor(
                            probs[e][h][:], probs[e][h][:],
                            over_sums[e][h][:].rearrange("p (t a) -> p t a", a=1).broadcast_to([P, TT, P]), ALU.mult,
                        ).then_inc(probs_ready, 1)
                    if j == 1:
                        pool.wait_ge(residual_loaded, 16 * (i + 1))
                        pool.tensor_tensor(
                            result[:], result[:], proj_b[:].rearrange("p (a d) -> p a d", a=1).broadcast_to([P, TT, D]),
                            ALU.add,
                        ).then_inc(residual_ready, 1)
                if norms_more(i):
                    pool.wait_ge(bank_filled, Counts(i, last).filled(("x", KT - 1)))
                    norm.apply(pool, i + 2)

            all_steps(pool, step, peeled=2)

        @block.tensor
        def _(pe):
            def convolve(c, taps):
                out = banks[:, conv_bank[c], :]
                for s in taps:
                    for k in range(KT):
                        last = product(
                            pe, out, conv[of_conv[c]], xT, (slice(None), s * KT + k),
                            (slice(None), k, slice(s, s + CHUNK)), s == 0 and k == 0, s == TAPS - 1 and k == KT - 1,
                        )
                if s == TAPS - 1:
                    last.then_inc(conv_filled, 1)

            def heads(out, weight, j, of):
                product(pe, out, weight, qkv[of], (slice(None), tile(j)), slice(None), True, True).then_inc(bank_filled, 1)

            pe.wait_ge(identity_loaded, 16)
            pe.wait_ge(norm.xn_ready, 1)
            for k in range(KT):
                turn(pe, banks[:, k, :], norm.xn, tile(k), identity).then_inc(bank_filled, 1)
            pe.wait_ge(drained_by_dve, KT)
            for n, c in enumerate(CONVS):
                weights.wait(pe, n)
                if n == 2:
                    pe.wait_ge(conv_drained, 1)
                convolve(c, range(TAPS))
            weights.wait(pe, W_K)
            pe.wait_ge(conv_drained, len(CONVS))
            heads(banks[:, KT, :], wq, 0, 0)
            heads(banks[:, KT + 1, :], wk, 0, 1)
            weights.wait(pe, W_LAST)

            def step(i, last):
                counts = Counts(i, last)
                awaited = {}

                def await_drained(kind, count):
                    if count > awaited.get(kind, -RING - 1):
                        awaited[kind] = count
                        pe.wait_ge(drained_by_act if kind is by_act else drained_by_dve, counts.start(kind) + count)

                def fill(*names):
                    n = counts.names.index(names[-1])
                    await_drained(by_act, counts.freed(by_act, n))
                    await_drained(by_dve, counts.freed(by_dve, n))
                    return [counts.bank(name) for name in names]

                def needs(kind, name):
                    await_drained(kind, sum(map(kind, counts.names[: counts.names.index(name) + 1])))

                def scores(j):
                    if j == 0:
                        await_drained(by_act, 0)
                    else:
                        needs(by_act, ("k", j))
                    for h, out in enumerate(fill(("s", j, 0), ("s", j, 1))):
                        rows = slice(64 * h, 64 * h + 64)
                        for t in range(TT):
                            done = pe.matmul(
                                out[:, tile(t)], qh[j % 2][rows, tile(t)], kh[j % 2][rows, tile(t)], start=True, stop=True
                            )
                        done.then_inc(bank_filled, 1)

                def queries_and_keys(j):
                    outs = fill(("q", j), ("k", j))
                    heads(outs[0], wq, j, 0)
                    heads(outs[1], wk, j, 1)

                def turn_probs(j):
                    outs = fill(("t", j, 0), ("t", j, 1))
                    for h in range(2):
                        pe.wait_ge(probs_ready, 2 * PAIRS * i + 2 * j + h + 1)
                        turn(pe, outs[h], probs[j % 2][h], slice(0, P), identity).then_inc(bank_filled, 1)

                def contexts(j):
                    (out,) = fill(("c", j))
                    needs(by_dve, ("t", j, 1))
                    if j == 0:
                        needs(by_act, ("v", TT - 1))
                    for t in range(TT):
                        for h in range(2):
                            rows = slice(64 * h, 64 * h + 64)
                            done = pe.matmul(
                                out[rows, tile(t)], vh[:, t, j * P + 64 * h : j * P + 64 * h + 64], probsT[h][:, tile(t)],
                                start=True, stop=True,
                            )
                    done.then_inc(bank_filled, 1)

                def convolve_next(c, tap):
                    if last:
                        return
                    if c == "v" and tap == 0:
                        needs(by_dve, ("x", KT - 1))
                    if c == "k" and tap == 0:
                        pe.wait_ge(conv_drained, len(CONVS) * (i + 1) + 1)
                    convolve(c, [tap])

                scores(0)
                if not last:
                    pe.wait_ge(norm.xn_ready, i + 2)
                    for k in range(KT):
                        turn(pe, fill(("x", k))[0], norm.xn, tile(k), identity).then_inc(bank_filled, 1)
                for t in range(TT):
                    (out,) = fill(("v", t))
                    product(pe, out, qkv[2], wv, (slice(None), tile(t)), slice(None), True, True).then_inc(bank_filled, 1)
                queries_and_keys(1)
                convolve_next("v", 0)
                scores(1)
                convolve_next("v", 1)
                turn_probs(0)
                convolve_next("v", 2)
                contexts(0)
                queries_and_keys(2)
                convolve_next("q", 0)
                scores(2)
                turn_probs(1)
                queries_and_keys(3)
                convolve_next("q", 1)
                contexts(1)
                scores(3)
                convolve_next("q", 2)
                turn_probs(2)
                convolve_next("k", 0)
                contexts(2)
                convolve_next("k", 1)
                turn_probs(3)
                convolve_next("k", 2)
                contexts(3)
                out, _ = fill(("mix", 0), ("mix", 1))
                for j in range(PAIRS):
                    if j == PAIRS - 1:
                        needs(by_dve, ("c", j))
                    elif j == 0:
                        needs(by_dve, ("c", PAIRS - 2))
                    done = product(pe, out, wo, ctxT, (slice(None), j), (slice(None), j), j == 0, j == PAIRS - 1)
                done.then_inc(bank_filled, 2)
                if not last:
                    pe.wait_ge(conv_drained, len(CONVS) * (i + 2))
                    queries_and_keys(0)
                needs(by_dve, ("mix", 1))
                for t in range(TT):
                    (out,) = fill(("o", t))
                    product(pe, out, mixT, proj, (slice(None), tile(t)), slice(None), True, True).then_inc(bank_filled, 1)

            all_steps(pe, step)

        @block.scalar
        def _(act):
            act.wait_ge(halo_cleared, 2)
            act.wait_ge(constants_loaded, 16 * len(CONSTANTS))

            def turned_high(chunk, filled, bank):
                act.activation(
                    xT.high[:, :, 0:HALO], xT.high[:, :, CHUNK:].bitcast(fp32), ACT.Copy, scale=keep[:, bass.ds(chunk, 1)]
                ).then_inc(halo_high, 1)
                act.wait_ge(halo_high, chunk + 1)
                for k in range(KT):
                    act.wait_ge(bank_filled, filled(k))
                    act.activation(xT.high[:, k, HALO:], bank(k), ACT.Copy).then_inc(high_ready, 1)

            def conv_to_high(c, chunk):
                of = of_conv[c]
                act.wait_ge(conv_filled, len(CONVS) * chunk + CONVS.index(c) + 1)
                act.activation(
                    qkv[of].high[:], banks[:, conv_bank[c], :], ACT.Identity, bias=conv_b[:, of : of + 1]
                ).then_inc(conv_high, 1)

            def drain(filled, out, bank, bias=None):
                act.wait_ge(bank_filled, filled)
                if bias is None:
                    act.activation(out, bank, ACT.Copy).then_inc(drained_by_act, 1)
                else:
                    act.activation(out, bank, ACT.Identity, bias=bias).then_inc(drained_by_act, 1)

            turned_high(0, lambda k: k + 1, lambda k: banks[:, k, :])
            for n, c in enumerate(CONVS):
                weights.write_high(act, n)
            conv_to_high("v", 0)
            for n in range(W_Q, W_LAST + 1):
                weights.write_high(act, n)
            conv_to_high("q", 0)
            conv_to_high("k", 0)
            drain(KT + 1, qh[0][:], banks[:, KT, :], bq[:, 0:1])
            drain(KT + 2, kh[0][:], banks[:, KT + 1, :], bk[:, 0:1])

            def step(i, last):
                counts = Counts(i, last)

                def queries_and_keys(j):
                    drain(counts.filled(("q", j)), qh[j % 2][:], counts.bank(("q", j)), bq[:, j : j + 1])
                    drain(counts.filled(("k", j)), kh[j % 2][:], counts.bank(("k", j)), bk[:, j : j + 1])

                def exponentials(j):
                    e = j % 2
                    for h in range(2):
                        act.wait_ge(peak_ready, 2 * PAIRS * i + 2 * j + h + 1)
                        for t in range(TT):
                            done = act.activation(
                                probs[e][h][:, t, :], masked[h][:, t, :], ACT.Exp, bias=minus_peak[e][h][:, t : t + 1],
                                scale=A_SCALE, accum_out=sums[e][h][:, t : t + 1],
                            )
                        done.then_inc(exp_done, 1)

                def contexts_high(j):
                    act.wait_ge(bank_filled, counts.filled(("c", j)))
                    act.activation(
                        ctxT.high[:, j, :], counts.bank(("c", j)), ACT.Identity, bias=bv[:, j : j + 1]
                    ).then_inc(high_ready, 1)

                def conv_next(c):
                    if not last:
                        conv_to_high(c, i + 1)

                if not last:
                    turned_high(i + 1, lambda k: counts.filled(("x", k)), lambda k: counts.bank(("x", k)))
                exponentials(0)
                for t in range(TT):
                    drain(counts.filled(("v", t)), vh[:, t, :], counts.bank(("v", t)))
                queries_and_keys(1)
                exponentials(1)
                conv_next("v")
                contexts_high(0)
                queries_and_keys(2)
                queries_and_keys(3)
                exponentials(2)
                contexts_high(1)
                conv_next("q")
                exponentials(3)
                contexts_high(2)
                conv_next("k")
                contexts_high(3)
                act.wait_ge(bank_filled, counts.filled(("mix", 1)))
                act.activation(mixT.high[:], counts.bank(("mix", 0)), ACT.Identity, bias=bo[:, 0:1]).then_inc(high_ready, 1)
                if not last:
                    queries_and_keys(0)

            all_steps(act, step)

        @block.vector
        def _(dve):
            dve.wait_ge(halo_cleared, 2)
            norm.take_moments(dve, 0)
            norm.finish_first(dve)
            dve.wait_ge(constants_loaded, 16 * len(CONSTANTS))

            def turned_low(chunk, high, bank):
                dve.tensor_scalar(
                    xT.low[:, :, 0:HALO], xT.low[:, :, CHUNK:].bitcast(fp32), keep[:, bass.ds(chunk, 1)], None, ALU.mult
                ).then_inc(halo_low, 1)
                dve.wait_ge(halo_low, chunk + 1)
                for k in range(KT):
                    dve.wait_ge(high_ready, high(k))
                    dve.tensor_tensor(
                        xT.low[:, k, HALO:], bank(k), xT.high[:, k, HALO:].bitcast(fp32), ALU.subtract
                    ).then_inc(drained_by_dve, 1)

            def less_high(out, bank, bias, high, done, by=1):
                dve.scalar_tensor_tensor(
                    out=out, in0=bank, scalar=bias, in1=high.bitcast(fp32), op0=ALU.add, op1=ALU.subtract
                ).then_inc(done, by)

            def conv_to_low(c, chunk):
                of = of_conv[c]
                dve.wait_ge(conv_high, len(CONVS) * chunk + CONVS.index(c) + 1)
                less_high(qkv[of].low[:], banks[:, conv_bank[c], :], conv_b[:, of : of + 1], qkv[of].high[:], conv_drained)

            turned_low(0, lambda k: k + 1, lambda k: banks[:, k, :])
            for n, c in enumerate(CONVS):
                weights.write_low(dve, n)
            conv_to_low("v", 0)
            norm.take_moments(dve, 1)
            for n in range(W_Q, W_LAST + 1):
                weights.write_low(dve, n)
            conv_to_low("q", 0)
            conv_to_low("k", 0)

            def step(i, last):
                counts = Counts(i, last)

                def mask_scores(j):
                    for h in range(2):
                        n = 2 * PAIRS * i + 2 * j + h + 1
                        dve.wait_ge(bank_filled, counts.filled(("s", j, h)))
                        dve.tensor_tensor(
                            masked[h][:], counts.bank(("s", j, h)).rearrange("p (t s) -> p t s", s=P),
                            causal[:].rearrange("p (a s) -> p a s", a=1).broadcast_to([P, TT, P]), ALU.add,
                        ).then_inc(drained_by_dve, 1)
                        dve.wait_ge(drained_by_dve, counts.up_to(by_dve, ("s", j, h)))
                        dve.tensor_reduce(peak[h][:], masked[h][:], AX.X, ALU.max).then_inc(peak_taken, 1)
                        dve.wait_ge(peak_taken, n)
                        dve.tensor_scalar(minus_peak[j % 2][h][:], peak[h][:], -A_SCALE, None, ALU.mult).then_inc(peak_ready, 1)

                def invert_sums(j):
                    for h in range(2):
                        dve.wait_ge(exp_done, 2 * PAIRS * i + 2 * j + h + 1)
                        dve.reciprocal(over_sums[j % 2][h][:], sums[j % 2][h][:]).then_inc(sums_inverted, 1)

                def copy_probs(j):
                    for h in range(2):
                        dve.wait_ge(bank_filled, counts.filled(("t", j, h)))
                        dve.tensor_copy(probsT[h][:], counts.bank(("t", j, h))).then_inc(drained_by_dve, 1)

                def contexts_low(j):
                    dve.wait_ge(high_ready, counts.up_to(is_split, ("c", j)))
                    less_high(ctxT.low[:, j, :], counts.bank(("c", j)), bv[:, j : j + 1], ctxT.high[:, j, :], drained_by_dve)

                def conv_next(c):
                    if not last:
                        conv_to_low(c, i + 1)

                mask_scores(0)
                if not last:
                    turned_low(i + 1, lambda k: counts.up_to(is_split, ("x", k)), lambda k: counts.bank(("x", k)))
                invert_sums(0)
                mask_scores(1)
                copy_probs(0)
                invert_sums(1)
                conv_next("v")
                contexts_low(0)
                if norms_more(i):
                    norm.take_moments(dve, i + 2)
                mask_scores(2)
                copy_probs(1)
                invert_sums(2)
                contexts_low(1)
                mask_scores(3)
                conv_next("q")
                copy_probs(2)
                invert_sums(3)
                contexts_low(2)
                copy_probs(3)
                conv_next("k")
                contexts_low(3)
                dve.wait_ge(high_ready, counts.up_to(is_split, ("mix", 0)))
                less_high(mixT.low[:], counts.bank(("mix", 0)), bo[:, 0:1], mixT.high[:], drained_by_dve, by=2)
                dve.wait_ge(residual_ready, i + 1)
                for t in range(TT):
                    dve.wait_ge(bank_filled, counts.filled(("o", t)))
                    dve.tensor_tensor(result[:, t, :], counts.bank(("o", t)), result[:, t, :], ALU.add).then_inc(drained_by_dve, 1)

            all_steps(dve, step, peeled=2)


class Experts:

    def __init__(self, nc, ctx, w):
        def sbuf(name, shape, dt=fp32):
            return ctx.enter_context(nc.sbuf_tensor(f"{name}_e", shape, dt))

        def sem(name):
            return ctx.enter_context(nc.semaphore(f"{name}_e"))

        self.down = Split(sbuf, "down", [P, KT, EXPERTS * RANK])
        self.up = Split(sbuf, "up", [P, EXPERTS * RANK // P, D])
        self.router = sbuf("router", [P, KT, 2, EXPERTS], f32r)
        router = Split(lambda name, shape, dt: self.router[:, :, int(name.endswith("low")), :], "router", None)
        self.identity = sbuf("identity", [P, P])
        self.router_b = sbuf("router_b", [P, EXPERTS])
        self.rank = sbuf("rank", [P, EXPERTS])
        self.constants = [
            (self.identity[:], w["identity"]), (self.router_b[:], w["router_b"].broadcast_to([P, EXPERTS])),
            (self.rank[:], w["expert_rank"].broadcast_to([P, EXPERTS])),
        ]
        self.constants_loaded = sem("constants_loaded")
        self.weights = Weights(sem, [
            (router, w["router"].rearrange("(k p) n -> p k n", p=P), sbuf("router_staged", [P, KT, EXPERTS])[:]),
            (self.down, w["down"].rearrange("(k p) n -> p k n", p=P), sbuf("down_staged", [P, KT, EXPERTS * RANK])[:]),
            (self.up, w["up"].rearrange("(k p) n -> p k n", p=P), sbuf("up_staged", [P, KT, D])[:]),
        ], "e")


def routed_experts(nc, x_in, x_out, experts, tag, load_experts):
    with ExitStack() as ctx:
        def sbuf(name, shape, dt=fp32):
            return ctx.enter_context(nc.sbuf_tensor(f"{name}_{tag}", shape, dt))

        def sem(name):
            return ctx.enter_context(nc.semaphore(f"{name}_{tag}"))

        norm = Norm(nc, ctx, tag)
        xT = Split(sbuf, "xT", [P, KT, CHUNK])
        logitsT = sbuf("logitsT", [2 * EXPERTS, CHUNK])
        logits = [sbuf(f"logits{n}", [P, TT, EXPERTS]) for n in range(2)]
        peak = sbuf("peak", [P, TT])
        shifted = sbuf("shifted", [P, TT, EXPERTS])
        exps = sbuf("exps", [P, TT, EXPERTS])
        total = sbuf("total", [P, TT])
        weight = sbuf("weight", [P, TT])
        ranked = sbuf("ranked", [P, TT, EXPERTS])
        first = sbuf("first", [P, TT])
        chosen = sbuf("chosen", [P, TT, EXPERTS])
        gate = sbuf("gate", [P, TT, EXPERTS])
        hidden = sbuf("hidden", [P, TT, EXPERTS * RANK])
        hiddenT = Split(sbuf, "hiddenT", [P, KT, CHUNK])
        result = sbuf("result", [P, TT, D])
        banks = ctx.enter_context(nc.psum_tensor(f"banks_{tag}", [P, BANKS, CHUNK], fp32))
        bank_filled, high_ready, bank_drained = sem("bank_filled"), sem("high_ready"), sem("bank_drained")
        router_filled, logits_copied, logits_turned = sem("router_filled"), sem("logits_copied"), sem("logits_turned")
        gate_steps, exp_done = sem("gate_steps"), sem("exp_done")
        residual_loaded, stored = sem("residual_loaded"), sem("stored")
        X_BANKS, HT_BANKS, OUT_BANKS, H_BANKS, LOGITS = (0, 1, 2, 3), (4, 5, 6, 0), (1, 2, 3, 1), (4, 5, 6, 4), 7
        BEFORE, TILES = 2 * KT, 4 * KT
        GATE_STEPS = 10

        def over_experts(a):
            return a.rearrange("p (t a) -> p t a", a=1).broadcast_to([P, TT, EXPERTS])

        def over_tiles(a):
            return a.rearrange("p (a e) -> p a e", a=1).broadcast_to([P, TT, EXPERTS])

        def firsts(i, last):
            start = BEFORE + TILES * i
            turned = 0 if last else KT
            return start, start + turned, start + turned + KT, start + turned + KT + TT

        def highs(i, last):
            return KT + 2 * KT * i, KT + 2 * KT * i + (0 if last else KT)

        block = ctx.enter_context(nc.Block())

        @block.sync
        def _(sp):
            norm.load(sp, x_in, 0)
            if load_experts:
                for dst, src in experts.constants:
                    sp.dma_start(dst, src).then_inc(experts.constants_loaded, 16)
                for n in range(3):
                    experts.weights.load(sp, n)
            for i in range(1, 3):
                norm.load(sp, x_in, i)

            def step(i, last):
                wait_for(sp, stored, 16 * i)
                sp.dma_start(
                    result[:], x_in[bass.ds(i * CHUNK, CHUNK), :].rearrange("(t p) d -> p t d", p=P)
                ).then_inc(residual_loaded, 16)
                if not isinstance(i, int) or i + 3 < CHUNKS:
                    norm.load(sp, x_in, i + 3)
                sp.wait_ge(bank_drained, firsts(i, last)[2] + TT)
                sp.dma_start(
                    x_out[bass.ds(i * CHUNK, CHUNK), :].rearrange("(t p) d -> p t d", p=P), result[:]
                ).then_inc(stored, 16)

            all_steps(sp, step, peeled=3)
            sp.wait_ge(stored, 16 * CHUNKS)

        @block.gpsimd
        def _(pool):
            norm.set_constants(pool)
            norm.start_first(pool)
            pool.wait_ge(bank_filled, KT)
            norm.apply(pool, 1)

            def step(i, last):
                if norms_more(i):
                    pool.wait_ge(bank_filled, firsts(i, last)[0] + KT)
                    norm.apply(pool, i + 2)

            all_steps(pool, step, peeled=2)

        @block.tensor
        def _(pe):
            def turn_x():
                for k in range(KT):
                    turn(pe, banks[:, X_BANKS[k], :], norm.xn, tile(k), experts.identity).then_inc(bank_filled, 1)

            def route():
                for k in range(KT):
                    for part in (xT.high, xT.low):
                        last = pe.matmul(
                            banks[0 : 2 * EXPERTS, LOGITS, :], experts.router[:, k, :, :].rearrange("p s e -> p (s e)"),
                            part[:, k, :], start=k == 0 and part is xT.high, stop=k == KT - 1 and part is xT.low,
                        )
                last.then_inc(router_filled, 1)

            def turn_logits(chunk):
                pe.wait_ge(experts.constants_loaded, 16)
                pe.wait_ge(logits_copied, chunk + 1)
                for t in range(TT):
                    last = pe.transpose(
                        banks[:, LOGITS, t * 2 * EXPERTS : (t + 1) * 2 * EXPERTS], logitsT[:, tile(t)],
                        experts.identity[0 : 2 * EXPERTS, 0 : 2 * EXPERTS],
                    )
                last.then_inc(logits_turned, 1)

            def four_tiles(bank_of, left, right, reused, routed=None):
                for t in range(TT):
                    if t == 1 and routed is not None:
                        turn_logits(routed)
                    if t == TT - 1:
                        pe.wait_ge(bank_drained, reused)
                    for k in range(KT):
                        last = product(
                            pe, banks[:, bank_of[t], :], left, right, (slice(None), k, tile(t)), (slice(None), k),
                            k == 0, k == KT - 1,
                        )
                    last.then_inc(bank_filled, 1)

            pe.wait_ge(experts.constants_loaded, 16 * len(experts.constants))
            pe.wait_ge(norm.xn_ready, 1)
            turn_x()
            if load_experts:
                experts.weights.wait(pe, 0)
            pe.wait_ge(bank_drained, KT)
            route()
            if load_experts:
                experts.weights.wait(pe, 1)
            four_tiles(H_BANKS, xT, experts.down, KT + 1, routed=0)
            if load_experts:
                experts.weights.wait(pe, 2)

            def step(i, last):
                start, back, out, ahead = firsts(i, last)
                if not last:
                    pe.wait_ge(norm.xn_ready, i + 2)
                    pe.wait_ge(bank_drained, start - KT)
                    turn_x()
                pe.wait_ge(bank_drained, start)
                for k in range(KT):
                    if k == KT - 1 and not last:
                        pe.wait_ge(bank_drained, start + 1)
                    turn(pe, banks[:, HT_BANKS[k], :], hidden, tile(k), experts.identity).then_inc(bank_filled, 1)
                if not last:
                    pe.wait_ge(bank_drained, start + KT)
                    route()
                pe.wait_ge(bank_drained, out)
                four_tiles(OUT_BANKS, hiddenT, experts.up, out + 1, routed=None if last else i + 1)
                if not last:
                    four_tiles(H_BANKS, xT, experts.down, ahead + 1)

            all_steps(pe, step)

        @block.scalar
        def _(act):
            def high(n, bank, out):
                act.wait_ge(bank_filled, n + 1)
                act.activation(out, banks[:, bank, :], ACT.Copy).then_inc(high_ready, 1)

            def copy_logits(chunk):
                act.wait_ge(router_filled, chunk + 1)
                act.activation(logitsT[:], banks[0 : 2 * EXPERTS, LOGITS, :], ACT.Copy).then_inc(logits_copied, 1)

            def exponentials(chunk):
                act.wait_ge(gate_steps, GATE_STEPS * chunk + 4)
                act.activation(exps[:], shifted[:], ACT.Exp).then_inc(exp_done, 1)

            for k in range(KT):
                high(k, X_BANKS[k], xT.high[:, k, :])
            if load_experts:
                for n in range(3):
                    experts.weights.write_high(act, n)
            copy_logits(0)
            exponentials(0)

            def step(i, last):
                start, back, _, _ = firsts(i, last)
                if not last:
                    for k in range(KT):
                        high(start + k, X_BANKS[k], xT.high[:, k, :])
                for k in range(KT):
                    high(back + k, HT_BANKS[k], hiddenT.high[:, k, :])
                if not last:
                    copy_logits(i + 1)
                    exponentials(i + 1)

            all_steps(act, step)

        @block.vector
        def _(dve):
            def low(n, bank, split, k):
                dve.wait_ge(high_ready, n + 1)
                dve.tensor_tensor(
                    split.low[:, k, :], banks[:, bank, :], split.high[:, k, :].bitcast(fp32), ALU.subtract
                ).then_inc(bank_drained, 1)

            def take_gate(chunk):
                at = GATE_STEPS * chunk
                both = banks[:, LOGITS, 0 : TT * 2 * EXPERTS].rearrange("p (t s e) -> p t s e", s=2, e=EXPERTS)
                dve.wait_ge(logits_turned, chunk + 1)
                dve.tensor_tensor(logits[0][:], both[:, :, 1, :], over_tiles(experts.router_b[:]), ALU.add).then_inc(gate_steps, 1)
                dve.wait_ge(gate_steps, at + 1)
                dve.tensor_tensor(logits[1][:], both[:, :, 0, :], logits[0][:], ALU.add).then_inc(gate_steps, 1)
                dve.wait_ge(gate_steps, at + 2)
                dve.tensor_reduce(peak[:], logits[1][:], AX.X, ALU.max).then_inc(gate_steps, 1)
                dve.wait_ge(gate_steps, at + 3)
                dve.tensor_tensor(shifted[:], logits[1][:], over_experts(peak[:]), ALU.subtract).then_inc(gate_steps, 1)
                dve.wait_ge(gate_steps, at + 4)
                dve.scalar_tensor_tensor(
                    out=ranked[:], in0=shifted[:], scalar=0.0, in1=over_tiles(experts.rank[:]), op0=ALU.is_ge, op1=ALU.mult
                ).then_inc(gate_steps, 1)
                dve.wait_ge(gate_steps, at + 5)
                dve.tensor_reduce(first[:], ranked[:], AX.X, ALU.max).then_inc(gate_steps, 1)
                dve.wait_ge(gate_steps, at + 6)
                dve.tensor_tensor(chosen[:], ranked[:], over_experts(first[:]), ALU.is_equal).then_inc(gate_steps, 1)
                dve.wait_ge(exp_done, chunk + 1)
                dve.tensor_reduce(total[:], exps[:], AX.X, ALU.add).then_inc(gate_steps, 1)
                dve.wait_ge(gate_steps, at + 8)
                dve.reciprocal(weight[:], total[:]).then_inc(gate_steps, 1)
                dve.wait_ge(gate_steps, at + 9)
                dve.scalar_tensor_tensor(
                    out=gate[:], in0=chosen[:], scalar=1.0 / RANK, in1=over_experts(weight[:]), op0=ALU.mult, op1=ALU.mult
                ).then_inc(gate_steps, 1)

            def gate_hidden(chunk, ahead):
                dve.wait_ge(gate_steps, GATE_STEPS * (chunk + 1))
                for t in range(TT):
                    dve.wait_ge(bank_filled, ahead + t + 1)
                    dve.tensor_tensor(
                        hidden[:, t, :].rearrange("p (e r) -> p e r", r=RANK),
                        banks[:, H_BANKS[t], :].rearrange("p (e r) -> p e r", r=RANK),
                        gate[:, t, :].rearrange("p (e a) -> p e a", a=1).broadcast_to([P, EXPERTS, RANK]), ALU.mult,
                    ).then_inc(bank_drained, 1)

            norm.take_moments(dve, 0)
            norm.finish_first(dve)
            for k in range(KT):
                low(k, X_BANKS[k], xT, k)
            if load_experts:
                for n in range(3):
                    experts.weights.write_low(dve, n)
            take_gate(0)
            norm.take_moments(dve, 1)
            gate_hidden(0, KT)

            def step(i, last):
                start, back, out, ahead = firsts(i, last)
                high_x, high_back = highs(i, last)
                if not last:
                    for k in range(KT):
                        low(high_x + k, X_BANKS[k], xT, k)
                for k in range(KT):
                    low(high_back + k, HT_BANKS[k], hiddenT, k)
                if norms_more(i):
                    norm.take_moments(dve, i + 2)
                if not last:
                    take_gate(i + 1)
                dve.wait_ge(residual_loaded, 16 * (i + 1))
                for t in range(TT):
                    dve.wait_ge(bank_filled, out + t + 1)
                    dve.tensor_tensor(result[:, t, :], banks[:, OUT_BANKS[t], :], result[:, t, :], ALU.add).then_inc(bank_drained, 1)
                if not last:
                    gate_hidden(i + 1, ahead)

            all_steps(dve, step, peeled=2)


HEAD_PAIRS = B_HEADS // 2
PAIR_DIM = 2 * B_DIM
WITH_SUM = B_DIM + 1


def project_qkv(nc, x_in, qT, kT, v, later, w):
    with ExitStack() as ctx:
        def sbuf(name, shape, dt=fp32):
            return ctx.enter_context(nc.sbuf_tensor(f"{name}_p", shape, dt))

        def sem(name):
            return ctx.enter_context(nc.semaphore(f"{name}_p"))

        wq, wk, wv = (Split(sbuf, n, [P, KT, D]) for n in ("Wq", "Wk", "Wv"))
        identity = sbuf("identity", [P, P])
        after = sbuf("after", [P, P])
        ones = sbuf("ones", [P, P])
        follows = sbuf("follows", [P, CHUNKS])
        norm = Norm(nc, ctx, "p")
        xT = Split(sbuf, "xT", [P, KT, CHUNK])
        queries, keys = (Split(sbuf, n, [P, KT, CHUNK]) for n in ("queries", "keys"))
        values = sbuf("values", [P, TT, D])
        rest = sbuf("rest", [P, TT + 1, D])
        sums = sbuf("sums", [P, TT, D])
        weights = Weights(sem, [
            (split, w[n].rearrange("(k p) n -> p k n", p=P), to[:])
            for split, n, to in ((wq, "Wq", values), (wv, "Wv", sums), (wk, "Wk", sbuf("Wk_staged", [P, KT, D])))
        ], "p")
        banks = ctx.enter_context(nc.psum_tensor("banks_p", [P, BANKS, CHUNK], fp32))
        constants_loaded, ones_set = sem("constants_loaded"), sem("ones_set")
        bank_filled, high_ready, bank_drained = sem("bank_filled"), sem("high_ready"), sem("bank_drained")
        sums_filled, sums_drained, rest_ready = sem("sums_filled"), sem("sums_drained"), sem("rest_ready")
        queries_stored, keys_stored = sem("queries_stored"), sem("keys_stored")
        values_stored, sums_stored = sem("values_stored"), sem("sums_stored")
        Q0, V0, K0, X0, TILES, BEFORE = 0, 4, 8, 12, 16, 4
        Q_BANK, V_BANK, K_BANK, X_BANK, SUM_BANK = 0, 4, 0, 4, 0
        HIGHS = 3 * KT
        STORES = 2
        RESTS = TT + 1
        CHUNKS_PER_SEQUENCE = T // CHUNK
        from_last = list(reversed(range(TT)))
        block = ctx.enter_context(nc.Block())

        def tiles_before(i):
            return BEFORE + TILES * i

        @block.sync
        def _(sp):
            for dst, src in ((identity, "identity"), (after, "after"), (follows, "follows")):
                sp.dma_start(dst[:], w[src]).then_inc(constants_loaded, 16)
            for n in range(3):
                weights.load(sp, n)
            with sp.Fori(0, BATCH) as b:
                with sp.Fori(0, CHUNKS_PER_SEQUENCE) as c:
                    start = tiles_before(b * CHUNKS_PER_SEQUENCE + c)
                    row, token = b * -D + (BATCH - 1) * D, c * -CHUNK + (CHUNKS_PER_SEQUENCE - 1) * CHUNK
                    pair = b * -HEAD_PAIRS + (BATCH - 1) * HEAD_PAIRS

                    def store_split(dst, src, done):
                        for half, part in ((0, src.high), (1, src.low)):
                            sp.dma_start(
                                dst[half, bass.ds(row, D), bass.ds(token, CHUNK)].rearrange("(k p) t -> p k t", p=P),
                                part[:].bitcast(fp32),
                            ).then_inc(done, 16)

                    def store_by_pair(dst, src, t, done):
                        sp.dma_start(
                            dst[bass.ds(pair, HEAD_PAIRS), bass.ds(token + t * P, P), :].rearrange("g p c -> p g c"),
                            src[:, t, :].rearrange("p (g c) -> p g c", c=PAIR_DIM),
                        ).then_inc(done, 16)

                    sp.wait_ge(bank_drained, start + Q0 + KT)
                    store_split(qT, queries, queries_stored)
                    sp.wait_ge(bank_drained, start + V0 + TT)
                    for t in from_last:
                        store_by_pair(v, values, t, values_stored)
                    sp.wait_ge(bank_drained, start + K0 + KT)
                    store_split(kT, keys, keys_stored)
                    sp.wait_ge(sums_drained, (b * CHUNKS_PER_SEQUENCE + c) * TT + TT)
                    for t in from_last:
                        store_by_pair(later, sums, t, sums_stored)
            for done, stores in ((queries_stored, STORES), (keys_stored, STORES), (values_stored, TT), (sums_stored, TT)):
                sp.wait_ge(done, 16 * stores * CHUNKS)

        @block.gpsimd
        def _(pool):
            def load(i):
                norm.load(pool, x_in, i, i * -CHUNK + (CHUNKS - 1) * CHUNK)

            load(0)
            norm.set_constants(pool)
            pool.memset(ones[:], 1.0).then_inc(ones_set, 1)
            pool.memset(rest[:, TT, :], 0.0).then_inc(ones_set, 1)
            pool.wait_ge(ones_set, 2)
            norm.start_first(pool)
            load(1)
            pool.wait_ge(bank_filled, BEFORE)
            norm.apply(pool, 1)
            load(2)
            pool.wait_ge(constants_loaded, 16 * 3)

            def step(i, last):
                wait_for(pool, sums_filled, TT * i)
                wait_for(pool, rest_ready, RESTS * i)
                pool.tensor_tensor(
                    rest[:, 0, :], rest[:, TT, :], follows[:, bass.ds(i, 1)].broadcast_to([P, D]), ALU.mult
                ).then_inc(rest_ready, 1)
                pool.wait_ge(bank_drained, tiles_before(i) + V0 + TT)
                for n, t in enumerate(from_last):
                    pool.wait_ge(rest_ready, RESTS * i + n + 1)
                    pool.tensor_tensor(rest[:, n + 1, :], rest[:, n, :], values[:, t, :], ALU.add).then_inc(rest_ready, 1)
                if norms_more(i):
                    pool.wait_ge(bank_filled, tiles_before(i) + X0 + KT)
                    norm.apply(pool, i + 2)
                if not isinstance(i, int) or i + 3 < CHUNKS:
                    load(i + 3)

            all_steps(pool, step, peeled=3)

        @block.tensor
        def _(pe):
            def turn_x():
                for k in range(KT):
                    turn(pe, banks[:, X_BANK + k, :], norm.xn, tile(k), identity).then_inc(bank_filled, 1)

            pe.wait_ge(constants_loaded, 16 * 3)
            pe.wait_ge(norm.xn_ready, 1)
            turn_x()
            pe.wait_ge(ones_set, 2)

            def step(i, last):
                start = tiles_before(i)

                def project(weight, bank):
                    for m in range(KT):
                        if m == KT - 1 and bank == Q_BANK and weight is wq:
                            wait_for(pe, sums_drained, TT * i)
                        for k in range(KT):
                            done = product(
                                pe, banks[:, bank + m, :], weight, xT, (slice(None), k, tile(m)), (slice(None), k),
                                k == 0, k == KT - 1,
                            )
                        done.then_inc(bank_filled, 1)

                def first_use(n):
                    if isinstance(i, int) and i == 0:
                        weights.wait(pe, n)

                pe.wait_ge(bank_drained, start)
                wait_for(pe, sums_drained, TT * i - 1)
                first_use(0)
                project(wq, Q_BANK)
                first_use(1)
                for n, t in enumerate(from_last):
                    for k in range(KT):
                        done = product(
                            pe, banks[:, V_BANK + n, :], xT, wv, (slice(None), k, tile(t)), (slice(None), k), k == 0, k == KT - 1
                        )
                    done.then_inc(bank_filled, 1)
                first_use(2)
                pe.wait_ge(bank_drained, start + Q0 + KT)
                project(wk, K_BANK)
                if not last:
                    pe.wait_ge(norm.xn_ready, i + 2)
                    pe.wait_ge(bank_drained, start + V0 + TT)
                    turn_x()
                pe.wait_ge(bank_drained, start + K0 + KT)
                for n, t in enumerate(from_last):
                    pe.wait_ge(rest_ready, RESTS * i + n + 1)
                    out = banks[:, SUM_BANK + n, :]
                    pe.matmul(out, after[:], values[:, t, :], start=True, stop=False)
                    pe.matmul(out, ones[:], rest[:, n, :], start=False, stop=True).then_inc(sums_filled, 1)

            all_steps(pe, step)

        @block.scalar
        def _(act):
            def highs(first, split, bank):
                for k in range(KT):
                    act.wait_ge(bank_filled, first + k + 1)
                    act.activation(split.high[:, k, :], banks[:, bank + k, :], ACT.Copy).then_inc(high_ready, 1)

            highs(0, xT, X_BANK)
            for n in range(3):
                weights.write_high(act, n)

            def step(i, last):
                start = tiles_before(i)
                wait_for(act, queries_stored, 16 * STORES * i)
                highs(start + Q0, queries, Q_BANK)
                wait_for(act, keys_stored, 16 * STORES * i)
                highs(start + K0, keys, K_BANK)
                if not last:
                    highs(start + X0, xT, X_BANK)
                wait_for(act, sums_stored, 16 * TT * i)
                for n, t in enumerate(from_last):
                    act.wait_ge(sums_filled, TT * i + n + 1)
                    act.activation(sums[:, t, :], banks[:, SUM_BANK + n, :], ACT.Copy).then_inc(sums_drained, 1)

            all_steps(act, step)

        @block.vector
        def _(dve):
            def lows(first, split, bank):
                for k in range(KT):
                    dve.wait_ge(high_ready, first + k + 1)
                    dve.tensor_tensor(
                        split.low[:, k, :], banks[:, bank + k, :], split.high[:, k, :].bitcast(fp32), ALU.subtract
                    ).then_inc(bank_drained, 1)

            norm.take_moments(dve, 0)
            norm.finish_first(dve)
            lows(0, xT, X_BANK)
            for n in range(3):
                weights.write_low(dve, n)
            norm.take_moments(dve, 1)

            def step(i, last):
                start, high = tiles_before(i), KT + HIGHS * i
                lows(high, queries, Q_BANK)
                wait_for(dve, values_stored, 16 * TT * i)
                wait_for(dve, sums_filled, TT * i)
                wait_for(dve, rest_ready, RESTS * i)
                for n, t in enumerate(from_last):
                    dve.wait_ge(bank_filled, start + V0 + n + 1)
                    dve.tensor_copy(values[:, t, :], banks[:, V_BANK + n, :]).then_inc(bank_drained, 1)
                if norms_more(i):
                    norm.take_moments(dve, i + 2)
                lows(high + KT, keys, K_BANK)
                if not last:
                    lows(high + 2 * KT, xT, X_BANK)

            all_steps(dve, step, peeled=2)


def causal_product_attention(nc, qT, kT, v, later, context, w):
    with ExitStack() as ctx:
        def sbuf(name, shape, dt=fp32):
            return ctx.enter_context(nc.sbuf_tensor(f"{name}_b", shape, dt))

        def sem(name):
            return ctx.enter_context(nc.semaphore(f"{name}_b"))

        ROWS = 3 * B_DIM
        PEAK_ROW = ROWS
        QC = T // CHUNK
        GPAIRS = BATCH * HEAD_PAIRS
        units = [(c, j) for c in range(QC) for j in range(TT * c + TT)]
        UNITS = len(units)
        pieces = [(h, i, k) for h in range(2) for i in range(TQ) for k in range(i // TT + 1)]
        PIECES = len(pieces)
        LAG = 3
        PIECE_TO = 37
        PEAKS_AT = PIECE_TO + 1
        TURN_LAG = 3
        KEPT = 5
        RING = 3
        DIAGONALS = TQ
        ends = [sum(TT * d + TT for d in range(c + 1)) - 1 for c in range(QC)]
        NORM_STEPS = 2

        def pieces_at(u):
            def work(u):
                return sum(CHUNK * (c + 1) - query_start(c, j) for c, j in units[:u])

            def before(u):
                return PIECES * min(work(u), work(PIECE_TO)) // work(PIECE_TO)
            return range(before(u), before(u + 1))

        queries = [sbuf(f"queries{e}", [P, 2, T], f32r) for e in range(2)]
        keys = [sbuf(f"keys{e}", [P, 2, T], f32r) for e in range(2)]
        values = [sbuf(f"values{e}", [P, TQ, 2, WITH_SUM]) for e in range(2)]
        later_values = sbuf("later_values", [P, TQ, 2, WITH_SUM])
        counts = sbuf("counts", [P, TQ])
        later_part = [sbuf(f"later_part{e}", [P, TQ, 2, WITH_SUM]) for e in range(2)]
        exps = [sbuf(f"exps{n}", [P, 2, CHUNK]) for n in range(KEPT)]
        identity = sbuf("identity", [P, P])
        upto = sbuf("upto", [P, P])
        since = sbuf("since", [P, P])
        scratch = [sbuf(f"scratch{n}", [P, P]) for n in range(RING + 1)]
        piece_peaks = sbuf("piece_peaks", [P, 2, TQ, 6])
        peaks = sbuf("peaks", [P, 2, TQ])
        minus_peaks = sbuf("minus_peaks", [P, 2 * TQ], f32r)
        minus_peaks_T = sbuf("minus_peaks_T", [2 * TQ, P], f32r)
        later_weight = sbuf("later_weight", [P, 2, TQ])
        sumsT = sbuf("sumsT", [P, CHUNK])
        numerator = sbuf("numerator", [P, TT, 2, WITH_SUM])
        over_sum = sbuf("over_sum", [P, TT, 2])
        out = sbuf("out", [P, TQ, 2, B_DIM])
        banks = ctx.enter_context(nc.psum_tensor("banks_b", [P, BANKS, CHUNK], fp32))
        PIECE_BANKS, SCORE_BANKS, PRODUCTS = (0, 1, 2), (3, 4, 5), 6

        def piece_bank(n):
            return PIECE_BANKS[n % RING]

        def score_bank(u, h):
            return SCORE_BANKS[(2 * u + h) % RING]


        constants_loaded, constants_set, counts_loaded = sem("constants_loaded"), sem("constants_set"), sem("counts_loaded")
        counts_set = sem("counts_set")
        queries_loaded = [[sem(f"queries_loaded{e}{c}") for c in range(QC)] for e in range(2)]
        keys_loaded = [[sem(f"keys_loaded{e}{c}") for c in range(QC)] for e in range(2)]
        values_loaded, later_loaded = sem("values_loaded"), sem("later_loaded")
        piece_filled, piece_taken, peaks_taken, peaks_negated = sem("piece_filled"), sem("piece_taken"), sem("peaks_taken"), sem("peaks_negated")
        peaks_turned, peaks_copied, peak_rows_loaded = sem("peaks_turned"), sem("peaks_copied"), sem("peak_rows_loaded")
        later_weight_ready, later_part_ready = sem("later_weight_ready"), sem("later_part_ready")
        scores_filled, exp_done = sem("scores_filled"), [sem(f"exp_done{h}") for h in range(2)]
        diagonal_masked = sem("diagonal_masked")
        products_done, sums_copied, chunk_turned, norm_steps, chunk_out = (
            sem("products_done"), sem("sums_copied"), sem("chunk_turned"), sem("norm_steps"), sem("chunk_out"))
        stored, blocks_masked = sem("stored"), sem("blocks_masked")
        block = ctx.enter_context(nc.Block())

        PARTS = 3
        VALUE_LOADS = 2
        TAIL = LAG + TURN_LAG + 1

        def for_pairs(engine, at, rounds=(GPAIRS - 2) // 2):

            def step(e, g, first=False):
                for u in range(UNITS):
                    if u < TAIL and not first:
                        at(1 - e, g - 1, UNITS + u)
                    at(e, g, u)

            step(0, 0, first=True)
            with engine.Fori(0, rounds) as r:
                step(1, r * 2 + 1)
                step(0, r * 2 + 2)
            for g in range(2 * rounds + 1, GPAIRS):
                step(g % 2, g)
            for u in range(TAIL):
                at(1, GPAIRS - 1, UNITS + u)

        def is_last(g):
            return isinstance(g, int) and g == GPAIRS - 1

        def loads(e, g):
            return 8 * PARTS * (g + 2 - e)

        def query_start(c, j):
            return max(CHUNK * c, P * j)

        def is_diagonal(u):
            c, j = units[u]
            return j >= TT * c

        def diagonals(u):
            return sum(is_diagonal(n) for n in range(u + 1))

        @block.sync
        def _(sp):
            for dst, name in ((identity, "identity"), (upto, "upto"), (since, "since")):
                sp.dma_start(dst[:], w[name]).then_inc(constants_loaded, 16)
            sp.dma_start(counts[:], w["later_counts"]).then_inc(counts_loaded, 16)

            def load_chunk(e, g, c, tiles, view, done, halves):
                for n, half in enumerate(halves):
                    sp.dma_start(
                        tiles[e][n * B_DIM : (n + 1) * B_DIM, :, c * CHUNK : (c + 1) * CHUNK].bitcast(fp32),
                        view[half, bass.ds(g * PAIR_DIM, PAIR_DIM), c * CHUNK : (c + 1) * CHUNK].rearrange(
                            "(h r) t -> r h t", h=2
                        ),
                    ).then_inc(done[e][c], 16)

            def load_queries(e, g, c):
                load_chunk(e, g, c, queries, qT, queries_loaded, (0, 1, 0))

            def load_keys(e, g, c):
                load_chunk(e, g, c, keys, kT, keys_loaded, (0, 0, 1))

            def load_values(e, g):
                for dst, src, done in ((values[e], v, values_loaded), (later_values, later, later_loaded)):
                    for h in range(2):
                        sp.dma_start(
                            dst[:, :, h, 0:B_DIM],
                            src[g, :, h * B_DIM : (h + 1) * B_DIM].rearrange("(t p) c -> p t c", p=P),
                        ).then_inc(done, 16)

            def load_peak_rows(e, g):
                sp.wait_ge(peaks_copied, g + 1)
                for h in range(2):
                    sp.dma_start(
                        queries[e][PEAK_ROW : PEAK_ROW + 1, h, :].bitcast(fp32).rearrange("a (t p) -> a t p", p=P),
                        minus_peaks_T[h * TQ : (h + 1) * TQ, :].bitcast(fp32),
                    ).then_inc(peak_rows_loaded, 16)

            for e in range(2):
                for c in range(QC):
                    load_queries(e, e, c)
                    load_keys(e, e, c)
                if e == 0:
                    load_values(0, 0)
            load_peak_rows(0, 0)

            def at(e, g, u):
                if u == LAG and not is_last(g):
                    wait_for(sp, products_done, UNITS * g)
                    sp.wait_ge(later_part_ready, g + 1)
                    load_values(1 - e, g + 1)
                if u == PEAKS_AT and not is_last(g):
                    load_peak_rows(1 - e, g + 1)
                if not isinstance(g, int) or g < GPAIRS - 2:
                    for c in range(QC):
                        if u == ends[c] + 1:
                            sp.wait_ge(scores_filled, 2 * UNITS * g + 2 * (ends[c] + 1))
                            load_queries(e, g + 2, c)
                        if u == ends[QC - 2] + 1 + TT * (c + 1):
                            sp.wait_ge(scores_filled, 2 * UNITS * g + 2 * (ends[QC - 2] + 1 + TT * (c + 1)))
                            load_keys(e, g + 2, c)
                if u == UNITS + LAG + TURN_LAG:
                    sp.wait_ge(chunk_out, QC * (g + 1))
                    sp.dma_start(
                        context[g, :, :].rearrange("(t p) c -> p t c", p=P), out[:].rearrange("p t h c -> p t (h c)")
                    ).then_inc(stored, 16)

            for_pairs(sp, at, (GPAIRS - 2) // 2 - 1)
            sp.wait_ge(stored, 16 * GPAIRS)

        @block.gpsimd
        def _(pool):
            for e in range(2):
                pool.memset(values[e][:, :, :, B_DIM:], 1.0).then_inc(constants_set, 1)
            pool.memset(sumsT[:], 0.0).then_inc(constants_set, 1)
            pool.memset(piece_peaks[:], 0.0).then_inc(constants_set, 1)
            for e in range(2):
                pool.wait_ge(constants_set, 4 + e)
                pool.memset(keys[e][PEAK_ROW : PEAK_ROW + 1, :, :].bitcast(fp32), 1.0).then_inc(constants_set, 1)
            pool.wait_ge(constants_set, 6)
            pool.memset(piece_peaks[:, :, TQ - 1, 5:6], -BIG).then_inc(constants_set, 1)
            pool.wait_ge(constants_loaded, 16 * 3)
            pool.wait_ge(counts_loaded, 16)
            for h in range(2):
                pool.tensor_copy(later_values[:, :, h, B_DIM], counts[:]).then_inc(counts_set, 1)
            pool.wait_ge(counts_set, 2)

            def weigh_later(e, g):
                pool.wait_ge(later_loaded, 16 * VALUE_LOADS * (g + 1))
                pool.wait_ge(later_weight_ready, g + 1)
                pool.tensor_tensor(
                    later_part[e][:], later_values[:],
                    later_weight[:].rearrange("p h (t a) -> p t h a", a=1).broadcast_to([P, TQ, 2, WITH_SUM]), ALU.mult,
                ).then_inc(later_part_ready, 1)

            weigh_later(0, 0)

            def at(e, g, u):
                if u < UNITS and is_diagonal(u):
                    pool.wait_ge(exp_done[1], UNITS * g + u + 1)
                    corner = exps[u % KEPT][:, :, 0:P]
                    pool.tensor_tensor(
                        corner, corner, since[:].rearrange("p (a q) -> p a q", a=1).broadcast_to([P, 2, P]), ALU.mult
                    ).then_inc(diagonal_masked, 1)
                if u == PEAKS_AT and not is_last(g):
                    wait_for(pool, chunk_out, QC * g)
                    weigh_later(1 - e, g + 1)

            for_pairs(pool, at)

        @block.tensor
        def _(pe):
            pe.wait_ge(constants_loaded, 16 * 3)
            pe.wait_ge(constants_set, 7)

            def piece(e, g, n):
                h, i, k = pieces[n]
                if h == 0 and i % TT == 0 and k == 0:
                    pe.wait_ge(queries_loaded[e][i // TT], loads(e, g))
                    pe.wait_ge(keys_loaded[e][i // TT], loads(e, g))
                if n == 0:
                    wait_for(pe, peaks_copied, g)
                if n == 0:
                    wait_for(pe, piece_taken, PIECES * g)
                elif n >= RING:
                    pe.wait_ge(piece_taken, PIECES * g + n + 1 - RING)
                width = min(CHUNK, P * (i + 1) - CHUNK * k)
                pe.matmul(
                    banks[:, piece_bank(n), 0:width], queries[e][0:ROWS, h, tile(i)],
                    keys[e][0:ROWS, h, CHUNK * k : CHUNK * k + width], start=True, stop=True,
                ).then_inc(piece_filled, 1)

            def turn_peaks(g):
                pe.wait_ge(peaks_negated, g + 1)
                pe.transpose(banks[0 : 2 * TQ, 0, 0:P], minus_peaks[:].bitcast(fp32), identity[:]).then_inc(peaks_turned, 1)

            for n in range(PIECES):
                piece(0, 0, n)
            turn_peaks(0)

            def turn_sums(g, c):
                pe.wait_ge(sums_copied, QC * g + c + 1)
                for t in range(TT):
                    last = pe.transpose(banks[:, PRODUCTS + c % 2, tile(t)], sumsT[:, tile(t)], identity[:])
                last.then_inc(chunk_turned, 1)

            def scores(e, g, u):
                c, j = units[u]
                if u == 0:
                    pe.wait_ge(peak_rows_loaded, 32 * (g + 1))
                q0 = query_start(c, j)
                width = CHUNK * (c + 1) - q0
                for h in range(2):
                    if u == 0 and h == 0:
                        wait_for(pe, exp_done[1], UNITS * g)
                    elif 2 * u + h >= RING:
                        before, _ = divmod(2 * u + h - RING, 2)
                        pe.wait_ge(exp_done[1 - h], UNITS * g + before + 1)
                    pe.matmul(
                        banks[:, score_bank(u, h), 0:width], keys[e][0 : ROWS + 1, h, tile(j)],
                        queries[e][0 : ROWS + 1, h, q0 : q0 + width], start=True, stop=True,
                    ).then_inc(scores_filled, 1)

            def products(e, g, u):
                c, j = units[u]
                pe.wait_ge(exp_done[1], UNITS * g + u + 1)
                if u == 0:
                    pe.wait_ge(values_loaded, 16 * VALUE_LOADS * (g + 1))
                if is_diagonal(u):
                    pe.wait_ge(diagonal_masked, DIAGONALS * g + diagonals(u))
                if j == 0:
                    wait_for(pe, chunk_out, QC * g + c - 1)
                width = CHUNK * (c + 1) - query_start(c, j)
                for h in range(2):
                    last = pe.matmul(
                        banks[64 * h : 64 * h + WITH_SUM, PRODUCTS + c % 2, CHUNK - width :], values[e][:, j, h, :],
                        exps[u % KEPT][:, h, 0:width], start=j == 0, stop=j == TT * c + TT - 1,
                    )
                last.then_inc(products_done, 1)

            def at(e, g, u):
                for c, end in enumerate(ends):
                    if u == end + LAG + TURN_LAG:
                        turn_sums(g, c)
                next_pieces = [] if u >= UNITS or is_last(g) else list(pieces_at(u))
                for n in next_pieces[:1]:
                    piece(1 - e, g + 1, n)
                if u == PEAKS_AT and not is_last(g):
                    turn_peaks(g + 1)
                if u < UNITS:
                    scores(e, g, u)
                for n in next_pieces[1:2]:
                    piece(1 - e, g + 1, n)
                if LAG <= u < UNITS + LAG:
                    products(e, g, u - LAG)
                for n in next_pieces[2:]:
                    piece(1 - e, g + 1, n)

            for_pairs(pe, at)

        @block.scalar
        def _(act):
            def copy_peaks(g):
                act.wait_ge(peaks_turned, g + 1)
                wait_for(act, peak_rows_loaded, 32 * g)
                act.activation(minus_peaks_T[:], banks[0 : 2 * TQ, 0, 0:P], ACT.Copy).then_inc(peaks_copied, 1)
                wait_for(act, later_part_ready, g)
                act.activation(
                    later_weight[:].rearrange("p h t -> p (h t)"), minus_peaks[:].bitcast(fp32), ACT.Exp, scale=B_SCALE
                ).then_inc(later_weight_ready, 1)

            copy_peaks(0)

            def copy_sums(g, c):
                act.wait_ge(products_done, UNITS * g + ends[c] + 1)
                wait_for(act, chunk_turned, QC * g + c)
                for h in range(2):
                    rows = slice(64 * h, 64 * h + WITH_SUM)
                    last = act.activation(sumsT[rows, :], banks[rows, PRODUCTS + c % 2, :], ACT.Copy)
                last.then_inc(sums_copied, 1)

            def at(e, g, u):
                for c, end in enumerate(ends):
                    if u == end + LAG + 1:
                        copy_sums(g, c)
                if u >= UNITS:
                    return
                c, j = units[u]
                wait_for(act, products_done, UNITS * g + u + 1 - KEPT)
                width = CHUNK * (c + 1) - query_start(c, j)
                for h in range(2):
                    act.wait_ge(scores_filled, 2 * UNITS * g + 2 * u + h + 1)
                    act.activation(
                        exps[u % KEPT][:, h, 0:width], banks[:, score_bank(u, h), 0:width], ACT.Exp, scale=B_SCALE
                    ).then_inc(exp_done[h], 1)
                if u == PEAKS_AT and not is_last(g):
                    copy_peaks(g + 1)

            for_pairs(act, at)

        @block.vector
        def _(dve):
            dve.wait_ge(constants_set, 7)
            dve.wait_ge(constants_loaded, 16 * 3)

            def take_piece(g, n):
                h, i, k = pieces[n]
                before = min(CHUNK, P * i - CHUNK * k)
                dve.wait_ge(piece_filled, PIECES * g + n + 1)
                if before:
                    last = dve.tensor_reduce(piece_peaks[:, h, i, k : k + 1], banks[:, piece_bank(n), 0:before], AX.X, ALU.max)
                if k == i // TT and before:
                    last = dve.tensor_tensor_reduce(
                        scratch[n % (RING + 1)][:], banks[:, piece_bank(n), before : before + P], upto[:], 1.0, -BIG, ALU.mult, ALU.max,
                        piece_peaks[:, h, i, 4:5],
                    )
                elif k == i // TT:
                    dve.tensor_tensor(scratch[n % (RING + 1)][:], banks[:, piece_bank(n), 0:P], upto[:], ALU.mult).then_inc(blocks_masked, 1)
                    dve.wait_ge(blocks_masked, 2 * QC * g + h * QC + k + 1)
                    last = dve.tensor_reduce(piece_peaks[:, h, i, 4:5], scratch[n % (RING + 1)][:], AX.X, ALU.max)
                last.then_inc(piece_taken, 1)

            def finish_peaks(g):
                dve.wait_ge(piece_taken, PIECES * (g + 1))
                dve.tensor_reduce(peaks[:], piece_peaks[:], AX.X, ALU.max).then_inc(peaks_taken, 1)
                dve.wait_ge(peaks_taken, g + 1)
                wait_for(dve, later_weight_ready, g)
                dve.tensor_scalar(
                    minus_peaks[:], peaks[:].rearrange("p h t -> p (h t)"), -1.0, None, ALU.mult
                ).then_inc(peaks_negated, 1)

            for n in range(PIECES):
                take_piece(0, n)
            finish_peaks(0)

            def normalise(e, g, c):
                done = QC * g + c
                if c == 0:
                    dve.wait_ge(later_part_ready, g + 1)
                    wait_for(dve, stored, 16 * g)
                wait_for(dve, chunk_out, done)
                dve.wait_ge(chunk_turned, done + 1)
                dve.tensor_tensor(
                    numerator[:],
                    banks[:, PRODUCTS + c % 2, :].rearrange("p (t h c) -> p t h c", h=2, c=64)[:, :, :, 0:WITH_SUM],
                    later_part[e][:, TT * c : TT * c + TT, :, :], ALU.add,
                ).then_inc(norm_steps, 1)
                dve.wait_ge(norm_steps, NORM_STEPS * done + 1)
                dve.reciprocal(over_sum[:], numerator[:, :, :, B_DIM]).then_inc(norm_steps, 1)
                dve.wait_ge(norm_steps, NORM_STEPS * done + 2)
                dve.tensor_tensor(
                    out[:, TT * c : TT * c + TT, :, :], numerator[:, :, :, 0:B_DIM],
                    over_sum[:].rearrange("p t (h a) -> p t h a", a=1).broadcast_to([P, TT, 2, B_DIM]), ALU.mult,
                ).then_inc(chunk_out, 1)

            def at(e, g, u):
                if u < UNITS and not is_last(g):
                    for n in pieces_at(u):
                        take_piece(g + 1, n)
                    if u == PIECE_TO - 1:
                        finish_peaks(g + 1)
                for c, end in enumerate(ends):
                    if u == end + LAG + TURN_LAG:
                        normalise(e, g, c)

            for_pairs(dve, at)


def project_context(nc, context, x_in, x_out, w):
    with ExitStack() as ctx:
        def sbuf(name, shape, dt=fp32):
            return ctx.enter_context(nc.sbuf_tensor(f"{name}_o", shape, dt))

        def sem(name):
            return ctx.enter_context(nc.semaphore(f"{name}_o"))

        wo = Split(sbuf, "Wo", [P, KT, D])
        identity = sbuf("identity", [P, P])
        weights = Weights(sem, [(wo, w["Wo"].rearrange("(k p) n -> p k n", p=P), sbuf("Wo_staged", [P, KT, D])[:])], "o")
        mixed = [sbuf(f"mixed{e}", [P, TT, D]) for e in range(2)]
        result = [sbuf(f"result{e}", [P, TT, D]) for e in range(2)]
        mixedT = [Split(sbuf, f"mixedT{e}", [P, KT, CHUNK]) for e in range(2)]
        banks = ctx.enter_context(nc.psum_tensor("banks_o", [P, BANKS, CHUNK], fp32))
        identity_loaded = sem("identity_loaded")
        bank_filled, high_ready, bank_drained = sem("bank_filled"), sem("high_ready"), sem("bank_drained")
        context_loaded = [sem(f"context_loaded{e}") for e in range(2)]
        residual_loaded = [sem(f"residual_loaded{e}") for e in range(2)]
        stored = [sem(f"stored{e}") for e in range(2)]
        X_BANK, OUT_BANK, TILES = 0, KT, KT + TT
        ROUNDS = CHUNKS // 2
        block = ctx.enter_context(nc.Block())

        def all_rounds(engine, step):
            def both(r, last):
                for e in range(2):
                    step(e, r, r * 2 + e, last and e == 1)

            both(0, False)
            with engine.Fori(1, ROUNDS - 1) as r:
                both(r, False)
            both(ROUNDS - 1, True)

        @block.sync
        def _(sp):
            def load_context(i):
                b, c = divmod(i, T // CHUNK)
                for t in range(TT):
                    sp.dma_start(
                        mixed[i % 2][:, t, :].rearrange("p (g c) -> p g c", c=PAIR_DIM),
                        context[
                            b * HEAD_PAIRS : (b + 1) * HEAD_PAIRS, c * CHUNK + t * P : c * CHUNK + (t + 1) * P, :
                        ].rearrange("g p c -> p g c"),
                    ).then_inc(context_loaded[i % 2], 16)

            def load_residual(i):
                sp.dma_start(
                    result[i % 2][:], x_in[i * CHUNK : (i + 1) * CHUNK, :].rearrange("(t p) d -> p t d", p=P)
                ).then_inc(residual_loaded[i % 2], 16)

            sp.dma_start(identity[:], w["identity"]).then_inc(identity_loaded, 16)
            load_context(0)
            weights.load(sp, 0)
            load_context(1)
            load_residual(0)
            load_residual(1)
            for i in range(CHUNKS):
                if i + 2 < CHUNKS:
                    sp.wait_ge(bank_filled, KT + TILES * (i - 1) + KT if i else KT)
                    load_context(i + 2)
                sp.wait_ge(bank_drained, KT + TILES * (i + 1) - (KT if i == CHUNKS - 1 else 0))
                sp.dma_start(
                    x_out[i * CHUNK : (i + 1) * CHUNK, :].rearrange("(t p) d -> p t d", p=P), result[i % 2][:]
                ).then_inc(stored[i % 2], 16)
                if i + 2 < CHUNKS:
                    sp.wait_ge(stored[i % 2], 16 * (i // 2 + 1))
                    load_residual(i + 2)
            for e in range(2):
                sp.wait_ge(stored[e], 16 * ROUNDS)

        @block.tensor
        def _(pe):
            def turn_context(e):
                for k in range(KT):
                    turn(pe, banks[:, X_BANK + k, :], mixed[e], tile(k), identity).then_inc(bank_filled, 1)

            pe.wait_ge(identity_loaded, 16)
            pe.wait_ge(context_loaded[0], 16 * TT)
            turn_context(0)
            weights.wait(pe, 0)

            def step(e, r, i, last):
                start = KT + TILES * i
                pe.wait_ge(bank_drained, start)
                if not last:
                    pe.wait_ge(context_loaded[1 - e], 16 * TT * (r + 1 + e))
                    turn_context(1 - e)
                for t in range(TT):
                    for k in range(KT):
                        done = product(
                            pe, banks[:, OUT_BANK + t, :], mixedT[e], wo, (slice(None), k, tile(t)), (slice(None), k),
                            k == 0, k == KT - 1,
                        )
                    done.then_inc(bank_filled, 1)

            all_rounds(pe, step)

        @block.scalar
        def _(act):
            def highs(e, first):
                for k in range(KT):
                    act.wait_ge(bank_filled, first + k + 1)
                    act.activation(mixedT[e].high[:, k, :], banks[:, X_BANK + k, :], ACT.Copy).then_inc(high_ready, 1)

            highs(0, 0)
            weights.write_high(act, 0)

            def step(e, r, i, last):
                if not last:
                    highs(1 - e, KT + TILES * i)

            all_rounds(act, step)

        @block.vector
        def _(dve):
            def lows(e, first):
                for k in range(KT):
                    dve.wait_ge(high_ready, first + k + 1)
                    dve.tensor_tensor(
                        mixedT[e].low[:, k, :], banks[:, X_BANK + k, :], mixedT[e].high[:, k, :].bitcast(fp32), ALU.subtract
                    ).then_inc(bank_drained, 1)

            lows(0, 0)
            weights.write_low(dve, 0)

            def step(e, r, i, last):
                first_result = KT + TILES * i + KT
                if last:
                    first_result -= KT
                else:
                    lows(1 - e, KT + KT * i)
                dve.wait_ge(residual_loaded[e], 16 * (r + 1))
                for t in range(TT):
                    dve.wait_ge(bank_filled, first_result + t + 1)
                    dve.tensor_tensor(
                        result[e][:, t, :], banks[:, OUT_BANK + t, :], result[e][:, t, :], ALU.add
                    ).then_inc(bank_drained, 1)

            all_rounds(dve, step)


def hybrid_block(nc, w, x, out):
    def scratch(name, shape):
        return nc.dram_tensor(name, shape, fp32, kind="Internal").ap()

    x1, x2, x3 = (scratch(n, [TOKENS, D]) for n in ("x1", "x2", "x3"))
    qT, kT = (scratch(n, [2, BATCH * D, T]) for n in ("qT", "kT"))
    v, later, context = (scratch(n, [BATCH * HEAD_PAIRS, T, PAIR_DIM]) for n in ("v", "later", "context"))
    conv_attention(nc, x, x1, w)
    with ExitStack() as ctx:
        experts = Experts(nc, ctx, w)
        routed_experts(nc, x1, x2, experts, "e1", load_experts=True)
        project_qkv(nc, x2, qT, kT, v, later, w)
        causal_product_attention(nc, qT, kT, v, later, context, w)
        project_context(nc, context, x2, x3, w)
        routed_experts(nc, x3, out, experts, "e2", load_experts=False)


def kernel(**inputs):
    import numpy as np
    import concourse.bacc as bacc
    from concourse.bass_utils import run_bass_kernel_spmd

    a = {n: np.asarray(x) for n, x in inputs.items()}
    one = np.float32(1)
    arrays = {
        "x": a["L0_attn_a_x"].reshape(TOKENS, D),
        "conv_w": a["L0_attn_a_conv_w"],
        "conv_b": a["L0_attn_a_conv_b"].reshape(3, A_WIDTH).T,
        "wq": a["L0_attn_a_wq"].reshape(A_WIDTH, D),
        "wk": a["L0_attn_a_wk"].reshape(A_WIDTH, D),
        "wv": a["L0_attn_a_wv"].reshape(A_WIDTH, D),
        "bq": a["L0_attn_a_bq"].reshape(PAIRS, P).T,
        "bk": a["L0_attn_a_bk"].reshape(PAIRS, P).T,
        "bv": a["L0_attn_a_bv"].reshape(PAIRS, P).T,
        "wo": a["L0_attn_a_wo"].reshape(D, A_WIDTH),
        "bo": a["L0_attn_a_bo"].reshape(A_WIDTH, 1),
        "proj_w": a["L0_attn_a_proj_w"],
        "proj_b": a["L0_attn_a_proj_b"].reshape(1, D),
        "Wq": a["L0_attn_b_Wq"], "Wk": a["L0_attn_b_Wk"], "Wv": a["L0_attn_b_Wv"], "Wo": a["L0_attn_b_Wo"],
        "down": a["L0_ffn_A"].reshape(EXPERTS * RANK, D).T,
        "up": a["L0_ffn_B"].transpose(0, 2, 1).reshape(EXPERTS * RANK, D),
        "router": a["L0_ffn_Wr"].T,
        "router_b": a["L0_ffn_br"].reshape(1, EXPERTS),
        "identity": np.eye(P, dtype=np.float32),
        "causal": np.triu(np.full((P, P), -1e9 / A_SCALE, np.float32), 1),
        "keep": np.tile((np.arange(CHUNKS) % (T // CHUNK) > 0).astype(np.float32), (P, 1)),
        "expert_rank": np.arange(EXPERTS, 0, -1, dtype=np.float32).reshape(1, EXPERTS),
        "upto": np.tril(np.full((P, P), one)),
        "since": np.triu(np.full((P, P), one)),
        "follows": np.tile((np.arange(CHUNKS) % (T // CHUNK) > 0).astype(np.float32), (P, 1)),
        "after": np.tril(np.full((P, P), one), -1),
        "later_counts": (T - 1 - np.arange(T, dtype=np.float32)).reshape(TQ, P).T,
    }
    arrays = {n: np.ascontiguousarray(x) for n, x in arrays.items()}
    nc = bacc.Bacc("TRN2", target_bir_lowering=False, num_devices=1)
    dram = {n: nc.dram_tensor(n, x.shape, mybir.dt.from_np(x.dtype), kind="ExternalInput").ap() for n, x in arrays.items()}
    out = nc.dram_tensor("out", [TOKENS, D], fp32, kind="ExternalOutput").ap()
    hybrid_block(nc, dram, dram["x"], out)
    got = run_bass_kernel_spmd(nc, [arrays], core_ids=[0])
    return got.results[0]["out"].reshape(BATCH, T, D)
```
